# Optimizing a Trainium2 kernel written in Bass

```python
import numpy as np
import jax
import jax.numpy as jnp

def _softmax(x, axis=-1):
    return jax.nn.softmax(x, axis=axis)

def _gelu(x):
    return jax.nn.gelu(x, approximate=True)

def _silu(x):
    return jax.nn.silu(x)

def _sigmoid(x):
    return jax.nn.sigmoid(x)

def _layernorm(x, axis=-1, eps=1e-05):
    m = jnp.mean(x, axis=axis, keepdims=True)
    v = jnp.var(x, axis=axis, keepdims=True)
    return (x - m) / jnp.sqrt(v + eps)

def _scatter_add(tgt, idx, src, axis=0):
    return tgt.at[idx].add(src)

def _segment_sum(src, seg, n):
    return jax.ops.segment_sum(src, seg, n)
kernel_name = 'mk_adaln_d2_jaxref_r8_e32f8c'

def setup_inputs(seed: int=0):
    np.random.seed(seed)
    _w = jnp.asarray

    def _L0_attn_setup():
        import jax, jax.numpy as jnp
        import numpy as np
        H = 16
        EPS_LN = 1e-05

        def _ln(x, g, b):
            m = jnp.mean(x, axis=-1, keepdims=True)
            v = jnp.mean((x - m) ** 2, axis=-1, keepdims=True)
            return (x - m) / jnp.sqrt(v + EPS_LN) * g + b

        def _fwd(x, Wq, bq, gq, betaq, Wk, bk, gk, betak, Wv, bv, gv, betav, Wfq, bfq, Wfk, bfk, ga, ba, W1, b1, W2, b2):
            B, L, d = x.shape
            D = d // H
            Q = _ln(x @ Wq + bq, gq, betaq)
            Kc = _ln(x @ Wk + bk, gk, betak)
            Vc = _ln(x @ Wv + bv, gv, betav)
            z = jnp.zeros((B, 1, d), x.dtype)
            K = jnp.concatenate([z, Kc], axis=1)
            V = jnp.concatenate([z, Vc], axis=1)
            phi_Q = jnp.tanh(Q @ Wfq + bfq) + 1.0
            phi_K = jnp.tanh(K @ Wfk + bfk) + 1.0
            split = lambda t: t.reshape(B, t.shape[1], H, D).transpose(0, 2, 1, 3)
            Qh, Kh, Vh = (split(Q), split(K), split(V))
            pQ, pK = (split(phi_Q), split(phi_K))
            q_probe = jnp.mean(Qh, axis=2) / jnp.sqrt(jnp.asarray(D, x.dtype))
            score = jax.nn.softmax(jnp.einsum('bhd,bhkd->bhk', q_probe, Kh), axis=-1)
            pKw = pK * score[..., None]
            KV = jnp.einsum('bhkd,bhke->bhde', pKw, Vh)
            Ksum = jnp.sum(pKw, axis=2)
            num = jnp.einsum('bhqd,bhde->bhqe', pQ, KV)
            den = jnp.einsum('bhqd,bhd->bhq', pQ, Ksum)[..., None] + 1e-06
            out = num / den
            out = out.transpose(0, 2, 1, 3).reshape(B, L, d)
            a = _ln(out, ga, ba)
            h = a + (jax.nn.gelu(a @ W1 + b1, approximate=False) @ W2 + b2)
            return h + x
        key = jax.random.key(seed)
        B, L, d, mlp = (4, 512, 128, 512)
        ks = jax.random.split(key, 12)
        s = 0.02
        inp = {'x': jax.random.normal(ks[0], (B, L, d), jnp.float32), 'Wq': jax.random.normal(ks[1], (d, d), jnp.float32) * s, 'bq': jnp.zeros((d,), jnp.float32), 'gq': jnp.ones((d,), jnp.float32), 'betaq': jnp.zeros((d,), jnp.float32), 'Wk': jax.random.normal(ks[2], (d, d), jnp.float32) * s, 'bk': jnp.zeros((d,), jnp.float32), 'gk': jnp.ones((d,), jnp.float32), 'betak': jnp.zeros((d,), jnp.float32), 'Wv': jax.random.normal(ks[3], (d, d), jnp.float32) * s, 'bv': jnp.zeros((d,), jnp.float32), 'gv': jnp.ones((d,), jnp.float32), 'betav': jnp.zeros((d,), jnp.float32), 'Wfq': jax.random.normal(ks[4], (d, d), jnp.float32) * s, 'bfq': jnp.zeros((d,), jnp.float32), 'Wfk': jax.random.normal(ks[5], (d, d), jnp.float32) * s, 'bfk': jnp.zeros((d,), jnp.float32), 'ga': jnp.ones((d,), jnp.float32), 'ba': jnp.zeros((d,), jnp.float32), 'W1': jax.random.normal(ks[6], (d, mlp), jnp.float32) * s, 'b1': jnp.zeros((mlp,), jnp.float32), 'W2': jax.random.normal(ks[7], (mlp, d), jnp.float32) * s, 'b2': jnp.zeros((d,), jnp.float32)}
        return inp
    _L0_attn_in = _L0_attn_setup()

    def _L0_ffn_setup():
        import jax, jax.numpy as jnp
        import numpy as np
        DIM = 128
        DEPTH = 6
        HEADS = 16
        DIM_HEAD = 64
        WINDOW = 32
        INNER = HEADS * DIM_HEAD
        DIM_INNER = int(DIM * 4 * 2 / 3)
        QK_SCALE = 8.0

        def shift_tokens(t):
            a, s = jnp.split(t, 2, -1)
            s = jnp.pad(s, ((0, 0), (1, 0), (0, 0)))[:, :-1]
            return jnp.concatenate([a, s], -1)

        def l2norm(t):
            return t / jnp.maximum(jnp.linalg.norm(t, axis=-1, keepdims=True), 1e-12)

        def rotate_half(x):
            x1, x2 = jnp.split(x, 2, -1)
            return jnp.concatenate([-x2, x1], -1)

        def rotary_tables(n):
            half = jnp.arange(0, DIM_HEAD, 2, dtype=jnp.float32)
            inv_freq = 1.0 / 10000.0 ** (half / DIM_HEAD)
            t = jnp.arange(n, dtype=jnp.float32)
            freqs = t[:, None] * inv_freq[None, :]
            freqs = jnp.concatenate([freqs, freqs], -1)
            base_scale = (half + 0.4 * DIM_HEAD) / (1.4 * DIM_HEAD)
            power = (t - n // 2) / (WINDOW // 2)
            scale = base_scale[None, :] ** power[:, None]
            scale = jnp.concatenate([scale, scale], -1)
            return (freqs, scale)

        def local_attention(q, k, v):
            b, h, n, d = q.shape
            w = WINDOW
            nw = n // w
            bq = q.reshape(b, h, nw, w, d)
            bk = k.reshape(b, h, nw, w, d)
            bv = v.reshape(b, h, nw, w, d)

            def look(t):
                p = jnp.pad(t, ((0, 0), (0, 0), (1, 0), (0, 0), (0, 0)))
                return jnp.concatenate([p[:, :, :nw], p[:, :, 1:]], axis=3)
            bk2, bv2 = (look(bk), look(bv))
            seq = jnp.arange(n).reshape(nw, w)
            seq_p = jnp.pad(seq, ((1, 0), (0, 0)), constant_values=-1)
            jt = jnp.concatenate([seq_p[:nw], seq_p[1:]], axis=1)
            it = seq[:, :, None]
            jb = jt[:, None, :]
            mask = (it < jb) | (it > jb + w) | (jb == -1)
            sim = jnp.einsum('bhwie,bhwje->bhwij', bq, bk2) * QK_SCALE
            sim = jnp.where(mask, -jnp.finfo(sim.dtype).max, sim)
            attn = jax.nn.softmax(sim, -1)
            out = jnp.einsum('bhwij,bhwje->bhwie', attn, bv2)
            return out.reshape(b, h, n, d)

        def attn_layer(x, Wqkv, qs, ksc, Wo):
            b, n, _ = x.shape
            qkv = x @ Wqkv
            q, k, v = jnp.split(qkv, 3, -1)
            sh = lambda t: t.reshape(b, n, HEADS, DIM_HEAD).transpose(0, 2, 1, 3)
            q, k, v = (sh(q), sh(k), sh(v))
            q = l2norm(q) * qs
            k = l2norm(k) * ksc
            freqs, scale = rotary_tables(n)
            cos, sin = (jnp.cos(freqs), jnp.sin(freqs))
            q = q * cos * scale + rotate_half(q) * sin * scale
            inv = 1.0 / scale
            k = k * cos * inv + rotate_half(k) * sin * inv
            out = local_attention(q, k, v)
            out = out.transpose(0, 2, 1, 3).reshape(b, n, INNER)
            return out @ Wo

        def ffn_layer(x, g, bln, W1, b1, W2, b2):
            mu = x.mean(-1, keepdims=True)
            var = ((x - mu) ** 2).mean(-1, keepdims=True)
            xn = (x - mu) / jnp.sqrt(var + 1e-05) * g + bln
            hg = xn @ W1 + b1
            a, gate = jnp.split(hg, 2, -1)
            return a * jax.nn.gelu(gate, approximate=False) @ W2 + b2
        key = jax.random.key(seed)
        ks = jax.random.split(key, 8)
        B, N = (2, 256)
        init = lambda k, shape: jax.random.normal(k, shape, jnp.float32) * 0.02
        return {'x': jax.random.normal(ks[0], (B, N, DIM), jnp.float32), 'Wqkv': init(ks[1], (DEPTH, DIM, 3 * INNER)), 'q_scale': jnp.ones((DEPTH, DIM_HEAD), jnp.float32), 'k_scale': jnp.ones((DEPTH, DIM_HEAD), jnp.float32), 'Wo': init(ks[2], (DEPTH, INNER, DIM)), 'ln_g': jnp.ones((DEPTH, DIM), jnp.float32), 'ln_b': jnp.zeros((DEPTH, DIM), jnp.float32), 'W1': init(ks[3], (DEPTH, DIM, 2 * DIM_INNER)), 'b1': jnp.zeros((DEPTH, 2 * DIM_INNER), jnp.float32), 'W2': init(ks[4], (DEPTH, DIM_INNER, DIM)), 'b2': jnp.zeros((DEPTH, DIM), jnp.float32)}
    _L0_ffn_in = _L0_ffn_setup()
    _L0_c = _w((lambda *s: np.random.randn(*s).astype(np.float32) * 0.05)(16, 128))
    _L0_wmod = _w((lambda *s: np.random.randn(*s).astype(np.float32) * 0.05)(128, 6 * 128) * 128 ** (-0.5))

    def _L1_attn_setup():
        import jax, jax.numpy as jnp
        import numpy as np
        import math
        DIM = 128
        HEADS = 16
        DIM_HEAD = 64
        INNER = HEADS * DIM_HEAD
        NUM_BUCKETS = 32
        MAX_DISTANCE = 128

        def _relative_position_bucket(rel_pos, num_buckets=NUM_BUCKETS, max_distance=MAX_DISTANCE):
            n = jnp.maximum(-rel_pos, 0)
            max_exact = num_buckets // 2
            is_small = n < max_exact
            n_safe = jnp.maximum(n, 1)
            val_if_large = max_exact + (jnp.log(n_safe.astype(jnp.float32) / max_exact) / math.log(max_distance / max_exact) * (num_buckets - max_exact)).astype(jnp.int32)
            val_if_large = jnp.minimum(val_if_large, num_buckets - 1)
            return jnp.where(is_small, n, val_if_large)
        key = jax.random.key(seed)
        ks = jax.random.split(key, 6)
        x = jax.random.normal(ks[0], (2, 256, DIM), dtype=jnp.float32)
        Wq = jax.random.normal(ks[1], (DIM, INNER), dtype=jnp.float32) * DIM ** (-0.5)
        Wkv = jax.random.normal(ks[2], (DIM, 2 * DIM_HEAD), dtype=jnp.float32) * DIM ** (-0.5)
        Wout = jax.random.normal(ks[3], (INNER, DIM), dtype=jnp.float32) * INNER ** (-0.5)
        bout = jnp.zeros((DIM,), dtype=jnp.float32)
        rel_emb = jax.random.normal(ks[4], (NUM_BUCKETS, HEADS), dtype=jnp.float32) * 0.02
        return {'x': x, 'Wq': Wq, 'Wkv': Wkv, 'Wout': Wout, 'bout': bout, 'rel_emb': rel_emb}
    _L1_attn_in = _L1_attn_setup()

    def _L1_ffn_setup():
        import jax, jax.numpy as jnp
        import numpy as np
        N_EMBD = 128
        N_STATE = 512
        key = jax.random.key(seed)
        k_x, k_w1, k_b1, k_w2, k_b2 = jax.random.split(key, 5)
        x = jax.random.normal(k_x, (4, 256, N_EMBD), dtype=jnp.float32)
        w1 = jax.random.normal(k_w1, (N_EMBD, N_STATE), dtype=jnp.float32) * (1.0 / np.sqrt(N_EMBD))
        b1 = jax.random.normal(k_b1, (N_STATE,), dtype=jnp.float32) * 0.02
        w2 = jax.random.normal(k_w2, (N_STATE, N_EMBD), dtype=jnp.float32) * (1.0 / np.sqrt(N_STATE))
        b2 = jax.random.normal(k_b2, (N_EMBD,), dtype=jnp.float32) * 0.02
        return {'x': x, 'w1': w1, 'b1': b1, 'w2': w2, 'b2': b2}
    _L1_ffn_in = _L1_ffn_setup()
    _L1_c = _w((lambda *s: np.random.randn(*s).astype(np.float32) * 0.05)(16, 128))
    _L1_wmod = _w((lambda *s: np.random.randn(*s).astype(np.float32) * 0.05)(128, 6 * 128) * 128 ** (-0.5))
    _d = {'L0_attn_x': _L0_attn_in['x'], 'L0_attn_Wq': _L0_attn_in['Wq'], 'L0_attn_bq': _L0_attn_in['bq'], 'L0_attn_gq': _L0_attn_in['gq'], 'L0_attn_betaq': _L0_attn_in['betaq'], 'L0_attn_Wk': _L0_attn_in['Wk'], 'L0_attn_bk': _L0_attn_in['bk'], 'L0_attn_gk': _L0_attn_in['gk'], 'L0_attn_betak': _L0_attn_in['betak'], 'L0_attn_Wv': _L0_attn_in['Wv'], 'L0_attn_bv': _L0_attn_in['bv'], 'L0_attn_gv': _L0_attn_in['gv'], 'L0_attn_betav': _L0_attn_in['betav'], 'L0_attn_Wfq': _L0_attn_in['Wfq'], 'L0_attn_bfq': _L0_attn_in['bfq'], 'L0_attn_Wfk': _L0_attn_in['Wfk'], 'L0_attn_bfk': _L0_attn_in['bfk'], 'L0_attn_ga': _L0_attn_in['ga'], 'L0_attn_ba': _L0_attn_in['ba'], 'L0_attn_W1': _L0_attn_in['W1'], 'L0_attn_b1': _L0_attn_in['b1'], 'L0_attn_W2': _L0_attn_in['W2'], 'L0_attn_b2': _L0_attn_in['b2'], 'L0_ffn_Wqkv': _L0_ffn_in['Wqkv'], 'L0_ffn_q_scale': _L0_ffn_in['q_scale'], 'L0_ffn_k_scale': _L0_ffn_in['k_scale'], 'L0_ffn_Wo': _L0_ffn_in['Wo'], 'L0_ffn_ln_g': _L0_ffn_in['ln_g'], 'L0_ffn_ln_b': _L0_ffn_in['ln_b'], 'L0_ffn_W1': _L0_ffn_in['W1'], 'L0_ffn_b1': _L0_ffn_in['b1'], 'L0_ffn_W2': _L0_ffn_in['W2'], 'L0_ffn_b2': _L0_ffn_in['b2'], 'L0_c': _L0_c, 'L0_wmod': _L0_wmod, 'L1_attn_Wq': _L1_attn_in['Wq'], 'L1_attn_Wkv': _L1_attn_in['Wkv'], 'L1_attn_Wout': _L1_attn_in['Wout'], 'L1_attn_bout': _L1_attn_in['bout'], 'L1_attn_rel_emb': _L1_attn_in['rel_emb'], 'L1_ffn_w1': _L1_ffn_in['w1'], 'L1_ffn_b1': _L1_ffn_in['b1'], 'L1_ffn_w2': _L1_ffn_in['w2'], 'L1_ffn_b2': _L1_ffn_in['b2'], 'L1_c': _L1_c, 'L1_wmod': _L1_wmod}
    _x0 = _d['L0_attn_x']
    _d['L0_attn_x'] = jax.random.normal(jax.random.fold_in(jax.random.key(seed), 1), (16, 256, 128), dtype=_x0.dtype)
    del _x0
    return _d

def reference(L0_attn_x, L0_attn_Wq, L0_attn_bq, L0_attn_gq, L0_attn_betaq, L0_attn_Wk, L0_attn_bk, L0_attn_gk, L0_attn_betak, L0_attn_Wv, L0_attn_bv, L0_attn_gv, L0_attn_betav, L0_attn_Wfq, L0_attn_bfq, L0_attn_Wfk, L0_attn_bfk, L0_attn_ga, L0_attn_ba, L0_attn_W1, L0_attn_b1, L0_attn_W2, L0_attn_b2, L0_ffn_Wqkv, L0_ffn_q_scale, L0_ffn_k_scale, L0_ffn_Wo, L0_ffn_ln_g, L0_ffn_ln_b, L0_ffn_W1, L0_ffn_b1, L0_ffn_W2, L0_ffn_b2, L0_c, L0_wmod, L1_attn_Wq, L1_attn_Wkv, L1_attn_Wout, L1_attn_bout, L1_attn_rel_emb, L1_ffn_w1, L1_ffn_b1, L1_ffn_w2, L1_ffn_b2, L1_c, L1_wmod):

    def _L0_attn_ref(x, Wq, bq, gq, betaq, Wk, bk, gk, betak, Wv, bv, gv, betav, Wfq, bfq, Wfk, bfk, ga, ba, W1, b1, W2, b2):
        import jax, jax.numpy as jnp
        import numpy as np
        H = 16
        EPS_LN = 1e-05

        def _ln(x, g, b):
            m = jnp.mean(x, axis=-1, keepdims=True)
            v = jnp.mean((x - m) ** 2, axis=-1, keepdims=True)
            return (x - m) / jnp.sqrt(v + EPS_LN) * g + b

        def _fwd(x, Wq, bq, gq, betaq, Wk, bk, gk, betak, Wv, bv, gv, betav, Wfq, bfq, Wfk, bfk, ga, ba, W1, b1, W2, b2):
            B, L, d = x.shape
            D = d // H
            Q = _ln(x @ Wq + bq, gq, betaq)
            Kc = _ln(x @ Wk + bk, gk, betak)
            Vc = _ln(x @ Wv + bv, gv, betav)
            z = jnp.zeros((B, 1, d), x.dtype)
            K = jnp.concatenate([z, Kc], axis=1)
            V = jnp.concatenate([z, Vc], axis=1)
            phi_Q = jnp.tanh(Q @ Wfq + bfq) + 1.0
            phi_K = jnp.tanh(K @ Wfk + bfk) + 1.0
            split = lambda t: t.reshape(B, t.shape[1], H, D).transpose(0, 2, 1, 3)
            Qh, Kh, Vh = (split(Q), split(K), split(V))
            pQ, pK = (split(phi_Q), split(phi_K))
            q_probe = jnp.mean(Qh, axis=2) / jnp.sqrt(jnp.asarray(D, x.dtype))
            score = jax.nn.softmax(jnp.einsum('bhd,bhkd->bhk', q_probe, Kh), axis=-1)
            pKw = pK * score[..., None]
            KV = jnp.einsum('bhkd,bhke->bhde', pKw, Vh)
            Ksum = jnp.sum(pKw, axis=2)
            num = jnp.einsum('bhqd,bhde->bhqe', pQ, KV)
            den = jnp.einsum('bhqd,bhd->bhq', pQ, Ksum)[..., None] + 1e-06
            out = num / den
            out = out.transpose(0, 2, 1, 3).reshape(B, L, d)
            a = _ln(out, ga, ba)
            h = a + (jax.nn.gelu(a @ W1 + b1, approximate=False) @ W2 + b2)
            return h + x
        return _fwd(x, Wq, bq, gq, betaq, Wk, bk, gk, betak, Wv, bv, gv, betav, Wfq, bfq, Wfk, bfk, ga, ba, W1, b1, W2, b2)

    def _L0_ffn_ref(x, Wqkv, q_scale, k_scale, Wo, ln_g, ln_b, W1, b1, W2, b2):
        import jax, jax.numpy as jnp
        import numpy as np
        DIM = 128
        DEPTH = 6
        HEADS = 16
        DIM_HEAD = 64
        WINDOW = 32
        INNER = HEADS * DIM_HEAD
        DIM_INNER = int(DIM * 4 * 2 / 3)
        QK_SCALE = 8.0

        def shift_tokens(t):
            a, s = jnp.split(t, 2, -1)
            s = jnp.pad(s, ((0, 0), (1, 0), (0, 0)))[:, :-1]
            return jnp.concatenate([a, s], -1)

        def l2norm(t):
            return t / jnp.maximum(jnp.linalg.norm(t, axis=-1, keepdims=True), 1e-12)

        def rotate_half(x):
            x1, x2 = jnp.split(x, 2, -1)
            return jnp.concatenate([-x2, x1], -1)

        def rotary_tables(n):
            half = jnp.arange(0, DIM_HEAD, 2, dtype=jnp.float32)
            inv_freq = 1.0 / 10000.0 ** (half / DIM_HEAD)
            t = jnp.arange(n, dtype=jnp.float32)
            freqs = t[:, None] * inv_freq[None, :]
            freqs = jnp.concatenate([freqs, freqs], -1)
            base_scale = (half + 0.4 * DIM_HEAD) / (1.4 * DIM_HEAD)
            power = (t - n // 2) / (WINDOW // 2)
            scale = base_scale[None, :] ** power[:, None]
            scale = jnp.concatenate([scale, scale], -1)
            return (freqs, scale)

        def local_attention(q, k, v):
            b, h, n, d = q.shape
            w = WINDOW
            nw = n // w
            bq = q.reshape(b, h, nw, w, d)
            bk = k.reshape(b, h, nw, w, d)
            bv = v.reshape(b, h, nw, w, d)

            def look(t):
                p = jnp.pad(t, ((0, 0), (0, 0), (1, 0), (0, 0), (0, 0)))
                return jnp.concatenate([p[:, :, :nw], p[:, :, 1:]], axis=3)
            bk2, bv2 = (look(bk), look(bv))
            seq = jnp.arange(n).reshape(nw, w)
            seq_p = jnp.pad(seq, ((1, 0), (0, 0)), constant_values=-1)
            jt = jnp.concatenate([seq_p[:nw], seq_p[1:]], axis=1)
            it = seq[:, :, None]
            jb = jt[:, None, :]
            mask = (it < jb) | (it > jb + w) | (jb == -1)
            sim = jnp.einsum('bhwie,bhwje->bhwij', bq, bk2) * QK_SCALE
            sim = jnp.where(mask, -jnp.finfo(sim.dtype).max, sim)
            attn = jax.nn.softmax(sim, -1)
            out = jnp.einsum('bhwij,bhwje->bhwie', attn, bv2)
            return out.reshape(b, h, n, d)

        def attn_layer(x, Wqkv, qs, ksc, Wo):
            b, n, _ = x.shape
            qkv = x @ Wqkv
            q, k, v = jnp.split(qkv, 3, -1)
            sh = lambda t: t.reshape(b, n, HEADS, DIM_HEAD).transpose(0, 2, 1, 3)
            q, k, v = (sh(q), sh(k), sh(v))
            q = l2norm(q) * qs
            k = l2norm(k) * ksc
            freqs, scale = rotary_tables(n)
            cos, sin = (jnp.cos(freqs), jnp.sin(freqs))
            q = q * cos * scale + rotate_half(q) * sin * scale
            inv = 1.0 / scale
            k = k * cos * inv + rotate_half(k) * sin * inv
            out = local_attention(q, k, v)
            out = out.transpose(0, 2, 1, 3).reshape(b, n, INNER)
            return out @ Wo

        def ffn_layer(x, g, bln, W1, b1, W2, b2):
            mu = x.mean(-1, keepdims=True)
            var = ((x - mu) ** 2).mean(-1, keepdims=True)
            xn = (x - mu) / jnp.sqrt(var + 1e-05) * g + bln
            hg = xn @ W1 + b1
            a, gate = jnp.split(hg, 2, -1)
            return a * jax.nn.gelu(gate, approximate=False) @ W2 + b2
        for i in range(DEPTH):
            x = attn_layer(shift_tokens(x), Wqkv[i], q_scale[i], k_scale[i], Wo[i]) + x
            x = ffn_layer(shift_tokens(x), ln_g[i], ln_b[i], W1[i], b1[i], W2[i], b2[i]) + x
        return x

    def _L1_attn_ref(x, Wq, Wkv, Wout, bout, rel_emb):
        import jax, jax.numpy as jnp
        import numpy as np
        import math
        DIM = 128
        HEADS = 16
        DIM_HEAD = 64
        INNER = HEADS * DIM_HEAD
        NUM_BUCKETS = 32
        MAX_DISTANCE = 128

        def _relative_position_bucket(rel_pos, num_buckets=NUM_BUCKETS, max_distance=MAX_DISTANCE):
            n = jnp.maximum(-rel_pos, 0)
            max_exact = num_buckets // 2
            is_small = n < max_exact
            n_safe = jnp.maximum(n, 1)
            val_if_large = max_exact + (jnp.log(n_safe.astype(jnp.float32) / max_exact) / math.log(max_distance / max_exact) * (num_buckets - max_exact)).astype(jnp.int32)
            val_if_large = jnp.minimum(val_if_large, num_buckets - 1)
            return jnp.where(is_small, n, val_if_large)
        b, n, _ = x.shape
        scale = DIM_HEAD ** (-0.5)
        bias_scale = DIM_HEAD ** 0.5
        q = (x @ Wq).reshape(b, n, HEADS, DIM_HEAD).transpose(0, 2, 1, 3) * scale
        kv = x @ Wkv
        k, v = (kv[..., :DIM_HEAD], kv[..., DIM_HEAD:])
        sim = jnp.einsum('bhid,bjd->bhij', q, k)
        pos = jnp.arange(n, dtype=jnp.int32)
        rel_pos = pos[None, :] - pos[:, None]
        rp_bucket = _relative_position_bucket(rel_pos)
        bias = rel_emb[rp_bucket]
        sim = sim + jnp.transpose(bias, (2, 0, 1))[None] * bias_scale
        causal_mask = jnp.triu(jnp.ones((n, n), dtype=bool), k=1)
        neg = jnp.finfo(sim.dtype).max
        sim = jnp.where(causal_mask[None, None], -neg, sim)
        attn = jax.nn.softmax(sim, axis=-1)
        out = jnp.einsum('bhij,bjd->bhid', attn, v)
        out = out.transpose(0, 2, 1, 3).reshape(b, n, INNER)
        return out @ Wout + bout

    def _L1_ffn_ref(x, w1, b1, w2, b2):
        import jax, jax.numpy as jnp
        import numpy as np
        N_EMBD = 128
        N_STATE = 512
        h = jax.nn.gelu(jnp.einsum('bse,eh->bsh', x, w1) + b1, approximate=False)
        return jnp.einsum('bsh,he->bse', h, w2) + b2
    x = L0_attn_x
    mod = (_silu(L0_c) @ L0_wmod).reshape(L0_c.shape[0], 6, 1, -1)
    sa, ca, ga, sb, cb, gb = (mod[:, 0], mod[:, 1], mod[:, 2], mod[:, 3], mod[:, 4], mod[:, 5])
    ga = (2 * (ga >= 0) - 1) * jnp.maximum(jnp.abs(ga), 0.25)
    gb = (2 * (gb >= 0) - 1) * jnp.maximum(jnp.abs(gb), 0.25)
    h = _layernorm(x, axis=-1) * (1 + ca) + sa
    x = x + ga * _L0_attn_ref(h, L0_attn_Wq, L0_attn_bq, L0_attn_gq, L0_attn_betaq, L0_attn_Wk, L0_attn_bk, L0_attn_gk, L0_attn_betak, L0_attn_Wv, L0_attn_bv, L0_attn_gv, L0_attn_betav, L0_attn_Wfq, L0_attn_bfq, L0_attn_Wfk, L0_attn_bfk, L0_attn_ga, L0_attn_ba, L0_attn_W1, L0_attn_b1, L0_attn_W2, L0_attn_b2)
    h = _layernorm(x, axis=-1) * (1 + cb) + sb
    x = x + gb * _L0_ffn_ref(h, L0_ffn_Wqkv, L0_ffn_q_scale, L0_ffn_k_scale, L0_ffn_Wo, L0_ffn_ln_g, L0_ffn_ln_b, L0_ffn_W1, L0_ffn_b1, L0_ffn_W2, L0_ffn_b2)
    mod = (_silu(L1_c) @ L1_wmod).reshape(L1_c.shape[0], 6, 1, -1)
    sa, ca, ga, sb, cb, gb = (mod[:, 0], mod[:, 1], mod[:, 2], mod[:, 3], mod[:, 4], mod[:, 5])
    ga = (2 * (ga >= 0) - 1) * jnp.maximum(jnp.abs(ga), 0.25)
    gb = (2 * (gb >= 0) - 1) * jnp.maximum(jnp.abs(gb), 0.25)
    h = _layernorm(x, axis=-1) * (1 + ca) + sa
    x = x + ga * _L1_attn_ref(h, L1_attn_Wq, L1_attn_Wkv, L1_attn_Wout, L1_attn_bout, L1_attn_rel_emb)
    h = _layernorm(x, axis=-1) * (1 + cb) + sb
    x = x + gb * _L1_ffn_ref(h, L1_ffn_w1, L1_ffn_b1, L1_ffn_w2, L1_ffn_b2)
    return x

_drawn_inputs = setup_inputs


def setup_inputs(seed=0):
    import zlib

    import numpy as np

    out = dict(_drawn_inputs(seed))
    spreads = {'L0_attn_bq': (0.0, 2.0),
     'L0_attn_gq': (1.0, 0.6),
     'L0_attn_betaq': (0.0, 0.8),
     'L0_attn_bk': (0.0, 0.8),
     'L0_attn_gk': (1.0, 0.6),
     'L0_attn_betak': (0.0, 2.0),
     'L0_attn_bv': (0.0, 0.1),
     'L0_attn_gv': (1.0, 0.2),
     'L0_attn_betav': (0.0, 0.1),
     'L0_attn_bfq': (0.0, 2.0),
     'L0_attn_bfk': (0.0, 2.0),
     'L0_attn_ga': (1.0, 0.2),
     'L0_attn_ba': (0.0, 0.33),
     'L0_attn_b1': (0.0, 0.8),
     'L0_attn_b2': (0.0, 0.317),
     'L0_ffn_q_scale': (1.0, 0.6),
     'L0_ffn_k_scale': (1.0, 0.6),
     'L0_ffn_ln_g': (1.0, 0.6),
     'L0_ffn_ln_b': (0.0, 0.8),
     'L0_ffn_b1': (0.0, 0.8),
     'L0_ffn_b2': (0.0, 0.745),
     'L1_attn_bout': (0.0, 2.0)}
    factors = {'L0_attn_Wq': 28.288,
     'L0_attn_Wfq': 27.029,
     'L0_attn_Wfk': 8.0,
     'L0_attn_W1': 3.977,
     'L0_attn_W2': 4.442,
     'L0_ffn_W1': 7.803,
     'L0_ffn_W2': 7.66,
     'L1_attn_rel_emb': 64.0,
     'L1_ffn_b1': 64.0,
     'L1_ffn_b2': 64.0,
     'L1_attn_Wq': 8.0,
     'L1_attn_Wkv': 4.281,
     'L1_attn_Wout': 4.259,
     'L1_ffn_w1': 4.344,
     'L1_ffn_w2': 3.845}
    for name, (base, spread) in spreads.items():
        noise = np.random.default_rng([zlib.crc32(name.encode()), seed]).standard_normal(out[name].shape)
        drawn = base * np.exp(spread * noise) if base else spread * noise
        out[name] = jnp.asarray(drawn.astype(out[name].dtype))
    for name, factor in factors.items():
        out[name] = (out[name] * factor).astype(out[name].dtype)
    return out
```

```python
import concourse.bass as bass
from concourse import mybir
from contextlib import ExitStack

F32 = mybir.dt.float32
BF16 = mybir.dt.bfloat16
F32R = mybir.dt.float32r
ALU = mybir.AluOpType
ACT = mybir.ActivationFunctionType
AX = mybir.AxisListType

D = 128
NB = 16
SEQ = 256
TOK = NB * SEQ
GRP = 512
NGRP = TOK // GRP
SPG = GRP // SEQ
TPG = GRP // D
HEADS = 16
HD = 64
INNER = HEADS * HD
DEPTH = 6
LIN_HD = D // HEADS
MLP = 512
MCH = MLP // D
GLU = int(D * 4 * 2 / 3)
GCH = 3
GW = -(-GLU // GCH)
WIN = 32
BLK = 2 * WIN
KEYS = BLK + WIN
EPS = 1e-5
NEG = -1e30
BUCKETS = 32


def glu_rows(j):
    return min(GW, GLU - j * GW)


def three_passes(nc, out, lhs, rhs, start=True, stop=True):
    nc.tensor.matmul(out, lhs[0], rhs[0], start=start, stop=False)
    nc.tensor.matmul(out, lhs[0], rhs[1], start=False, stop=False)
    return nc.tensor.matmul(out, lhs[1], rhs[0], start=False, stop=stop)


def phase_semaphores(nc, ctx, tag):
    made = []

    def sem(name):
        made.append(nc.alloc_semaphore(tag + name))
        return made[-1]

    def finish():
        nc.clear_and_free_semaphores(made)
        nc.all_engine_barrier()

    ctx.callback(finish)
    return sem


def window_attention(nc, layer, g, w):
    yT, ident, identb, maskb = g.yT, g.ident, g.identb, g.maskb
    HG = HEADS // 2
    PR = HG // 2
    UPS = 4
    UPL = UPS * NB
    with ExitStack() as ctx:
        sb = lambda n, s, d=F32: ctx.enter_context(nc.sbuf_tensor("wa_" + n, s, d))
        ps = lambda n: ctx.enter_context(nc.psum_tensor("wa_" + n, [128, 512], F32))
        s = g.wa_sems
        wqkv = g.lw.wqkv
        scb = g.lw.scb
        wo = sb("wo", [128, HEADS // 2, D])
        ctab = sb("ctab", [128, 2, 2, HD])
        stab = sb("stab", [128, 2, 2, HD])
        xs = sb("xs", [128, WIN + SEQ])
        xp = [sb(f"x{n}", [128, WIN + SEQ], F32R) for n in ("high", "low")]
        raw = sb("raw", [128, 2, 2, HG, HD])
        sq = sb("sq", [128, 2 * HG, HD])
        t1 = sb("t1", [128, 2, 2, HG, HD])
        t2 = sb("t2", [128, 2, 2, HG, HD])
        ss = sb("ss", [128, 2, 2 * HG])
        rn = sb("rn", [128, 2, 2 * HG])
        qT = sb("qT", [128, 2, PR, 128])
        kT = sb("kT", [128, 2, PR, WIN + SEQ])
        vv = sb("vv", [128, UPS, 2, HG, HD + 1])
        pb = sb("pb", [128, 2, 2, PR, KEYS])
        pT = sb("pT", [128, 2, 2, PR, 128])
        mx = sb("mx", [128, 2, PR])
        rs = sb("rs", [128, 2, PR])
        on = sb("on", [128, 2, HG, HD])
        oT = sb("oT", [128, 2, HEADS // 2, 128])
        PJ = [ps("pj0"), ps("pj1")]
        TR = [ps("tr0"), ps("tr1")]
        SC = [ps("sc0"), ps("sc1")]
        PV = [ps("pv0"), ps("pv1")]

        class Slot:

            def __init__(self, k, lead, loop=None):
                self.k, self.lead, self.loop, self.tail = k, lead, loop, lead == NB

            def has(self, lag):
                u = self.k - lag
                return u >= 0 if self.lead == 0 else u < 0 if self.tail else True

            def was(self, lag):
                return self.lead > 0 or self.k >= lag

            def count(self, per, lag, r):
                here = layer * (UPL * per) + (per * (UPS * self.lead + self.k - lag) + r)
                return here if self.loop is None else here + self.loop * (UPS * per)

            def tiles(self, lag, r):
                here = layer * (UPL // 2) + (2 * self.lead + (self.k - lag) // 2 + r)
                return here if self.loop is None else here + self.loop * 2

            def splits(self, seq, r):
                here = layer * (2 * NB) + (2 * seq + r)
                return here if self.loop is None else here + self.loop * 2

            def par(self, lag):
                return (self.k - lag) % 2

            def tile(self, lag):
                return (self.k - lag) % UPS // 2

            def half(self, lag):
                return (self.k - lag) % 2

        def run(eng, slot):
            for k in range(UPS):
                slot(Slot(k, 0))
            with eng.Fori(0, NB - 2) as loop:
                for k in range(UPS):
                    slot(Slot(k, 1, loop))
            for k in range(UPS):
                slot(Slot(k, NB - 1))
            for k in range(3):
                slot(Slot(k, NB))

        with nc.Block() as block:

            @block.sync
            def _(sp):
                sp.wait_ge(s.pads, layer * 3 + 1)

                def shift(seq, col):
                    sp.dma_start(xs[0:64, WIN:WIN + SEQ], yT[0:64, col]).then_inc(s.xs_ready, 16)
                    sp.dma_start(xs[64:128, WIN + 1:WIN + SEQ], seq).then_inc(s.xs_ready, 16)

                shift(yT[64:128, 0:SEQ - 1], slice(0, SEQ))
                sp.dma_start(wo[:, :, :], w.Wo[bass.ds(layer, 1)].rearrange(
                    "l (j p) n -> (l p) j n", p=128)).then_inc(s.w_o, 16)
                gated_weights_load(sp, layer, g, w)
                with sp.Fori(0, NB - 1) as loop:
                    sp.wait_ge(s.split_done, layer * (2 * NB) + loop * 2 + 2)
                    shift(yT[64:128, bass.ds(loop * SEQ + SEQ, SEQ - 1)], bass.ds(loop * SEQ + SEQ, SEQ))

            @block.tensor
            def _(pe):
                def transposes(out, src, n, rows=128):
                    for p in range(n):
                        last = nc.tensor.transpose(out[0:rows, p * 128:(p + 1) * 128], src(p), ident[:, :])
                    return last

                def slot(u):
                    T, hg = u.tile(0), u.half(0)
                    if u.has(0):
                        if u.k == 0:
                            pe.wait_ge(s.split_done, u.splits(u.lead, 2))
                        for j in range(2):
                            if u.was(1):
                                pe.wait_ge(s.proj_out, u.count(4, 1, 3 + j))
                            three_passes(nc, PJ[j][:, :], [x[:, WIN + T * 128:WIN + (T + 1) * 128] for x in xp],
                                         [x[:, j, hg * 512:(hg + 1) * 512] for x in wqkv]).then_inc(s.proj_done, 1)
                    def project_values(c):
                        pe.wait_ge(s.proj_out, u.count(4, 0, 1 + c))
                        k0 = (2 * T + c) * BLK
                        three_passes(nc, PJ[c][0:KEYS, :], [x[:, k0:k0 + KEYS] for x in xp],
                                     [x[:, 2, hg * 512:(hg + 1) * 512] for x in wqkv]).then_inc(s.proj_done, 1)

                    for e in range(2):
                        if u.has(2):
                            pe.wait_ge(s.exp_done, u.count(2, 2, e + 1))
                            if e == 0:
                                pe.wait_ge(s.qk_out, u.count(2, 2, 2))
                            elif u.k % 2 and u.was(4):
                                pe.wait_ge(s.wo_out, u.tiles(4, 1))
                            transposes(TR[e], lambda p: pb[:, u.par(2), e, p, :], PR, KEYS).then_inc(s.pT_done, 1)
                        if u.has(0):
                            project_values(e)
                    if u.has(3):
                        pe.wait_ge(s.norm_done, u.count(2, 3, 2))
                        if u.has(2):
                            pe.wait_ge(s.pT_out, u.count(2, 2, 1))
                        else:
                            pe.wait_ge(s.oT_out, u.count(1, 4, 1))
                        transposes(TR[0], lambda p: on[:, u.par(3), 2 * p:2 * p + 2, :].rearrange(
                            "p a b -> p (a b)"), PR).then_inc(s.oT_done, 1)

                    def turn_rotated(j):
                        transposes(TR[1 - j], lambda p: t1[:, u.par(1), j, 2 * p:2 * p + 2, :].rearrange(
                            "p a b -> p (a b)"), PR).then_inc(s.qk_done, 1)

                    def weigh_values(e):
                        pe.wait_ge(s.pT_out, u.count(2, 2, e + 1))
                        if u.was(3):
                            pe.wait_ge(s.norm_done, u.count(2, 3, e + 1))
                        for p in range(PR):
                            for c in range(2):
                                last = nc.tensor.matmul(
                                    PV[e][64 * c:64 * c + 64, p * (HD + 1):(p + 1) * (HD + 1)],
                                    pT[0:KEYS, u.par(2), e, p, 64 * c:64 * c + 64],
                                    vv[0:KEYS, (u.k - 2) % UPS, c, 2 * p + e, :], start=True, stop=True)
                        last.then_inc(s.pv_done, 1)

                    if u.has(1):
                        pe.wait_ge(s.qk_ready, u.count(1, 1, 1))
                        if u.was(2):
                            pe.wait_ge(s.pT_out, u.count(2, 2, 2))
                        turn_rotated(0)
                    if u.has(2):
                        pe.wait_ge(s.proj_out, u.count(4, 2, 4))
                        weigh_values(0)
                    if u.has(1):
                        if u.was(3):
                            pe.wait_ge(s.oT_out, u.count(1, 3, 1))
                        elif u.was(2):
                            pe.wait_ge(s.pT_out, u.count(2, 2, 1))
                        turn_rotated(1)
                    if u.has(2):
                        weigh_values(1)
                    if u.has(3) and u.k % 2 == 0:
                        pe.wait_ge(s.oT_out, u.count(1, 3, 1))
                        if u.has(1):
                            pe.wait_ge(s.qk_out, u.count(2, 1, 1))
                        else:
                            pe.wait_ge(s.pT_out, u.count(2, 2 if u.has(2) else 3, 2))
                        if u.lead == 1 and u.k == 0:
                            pe.wait_ge(s.w_o, layer * 16 + 16)
                        for j in range(HEADS // 2):
                            last = nc.tensor.matmul(TR[1][:, 0:128], wo[:, j, :], oT[:, u.tile(3), j, :],
                                                    start=(j == 0), stop=(j == HEADS // 2 - 1))
                        last.then_inc(s.wo_done, 1)
                    if u.has(1):
                        pe.wait_ge(s.qk_out, u.count(2, 1, 2))
                        t, h1 = u.tile(1), u.half(1)
                        for e in range(2):
                            if u.was(2):
                                pe.wait_ge(s.sub_done, u.count(2, 2, e + 1))
                            nc.tensor.matmul(SC[e][:, 0:PR * KEYS], identb[:, :], maskb[:, t, :, :],
                                             start=True, stop=False, skip_group_check=True)
                            for p in range(PR):
                                for c in range(2):
                                    k0 = (2 * t + c) * BLK
                                    last = nc.tensor.matmul(
                                        SC[e][64 * c:64 * c + 64, p * KEYS:(p + 1) * KEYS],
                                        qT[64 * e:64 * e + 64, u.par(1), p, 64 * c:64 * c + 64],
                                        kT[64 * e:64 * e + 64, h1, p, k0:k0 + KEYS],
                                        start=False, stop=True, skip_group_check=True)
                            last.then_inc(s.score_done, 1)

                run(pe, slot)

            @block.scalar
            def _(act):
                def slot(u):
                    def weights(lag, e):
                        if u.has(lag):
                            act.wait_ge(s.sub_done, u.count(2, lag, e + 1))
                            nc.scalar.activation(pb[:, u.par(lag), e, :, :], pb[:, u.par(lag), e, :, :],
                                                 ACT.Exp).then_inc(s.exp_done, 1)

                    for j in range(2):
                        if u.has(0):
                            act.wait_ge(s.proj_done, u.count(4, 0, j + 1))
                            if u.was(2):
                                act.wait_ge(s.rot_done, u.count(1, 2, 1))
                            nc.scalar.activation(raw[:, u.par(0), j, :, :], PJ[j][:, :].rearrange(
                                "p (h d) -> p h d", h=HG), ACT.Copy).then_inc(s.proj_out, 1)
                        if j == 0:
                            weights(2, 1)
                    if u.has(2):
                        for e in range(2):
                            act.wait_ge(s.pT_done, u.count(2, 2, e + 1))
                            if u.was(4):
                                act.wait_ge(s.pv_done, u.count(2, 4, 2))
                            nc.scalar.activation(pT[0:KEYS, u.par(2), e, :, :], TR[e][0:KEYS, :].rearrange(
                                "p (a b) -> p a b", a=PR), ACT.Copy).then_inc(s.pT_out, 1)
                    if u.has(0):
                        act.wait_ge(s.proj_out, u.count(4, 0, 2))
                        if u.was(1):
                            act.wait_ge(s.ss_done, u.count(1, 1, 1))
                        nc.scalar.activation(sq[:, :, :], raw[:, u.par(0), :, :, :].rearrange(
                            "p j h d -> p (j h) d"), ACT.Square).then_inc(s.sq_done, 1)
                    if u.has(3):
                        act.wait_ge(s.oT_done, u.count(1, 3, 1))
                        nc.scalar.activation(oT[:, u.tile(3), PR * u.half(3):PR * (u.half(3) + 1), :],
                                             TR[0][:, :].rearrange("p (a b) -> p a b", a=PR),
                                             ACT.Copy).then_inc(s.oT_out, 1)
                    if u.has(1):
                        act.wait_ge(s.qk_done, u.count(2, 1, 1))
                        if u.was(3):
                            act.wait_ge(s.score_done, u.count(2, 3, 2))
                        nc.scalar.activation(qT[:, u.par(1), :, :], TR[1][:, :].rearrange(
                            "p (a b) -> p a b", a=PR), ACT.Copy).then_inc(s.qk_out, 1)
                    def values_out(c):
                        act.wait_ge(s.proj_done, u.count(4, 0, 3 + c))
                        if u.was(4):
                            act.wait_ge(s.pv_done, u.count(2, 4, 2))
                        nc.scalar.activation(vv[0:KEYS, u.k, c, :, 0:HD], PJ[c][0:KEYS, :].rearrange(
                            "p (h d) -> p h d", h=HG), ACT.Copy).then_inc(s.proj_out, 1)

                    if u.has(0):
                        values_out(0)
                    if u.has(1):
                        act.wait_ge(s.qk_done, u.count(2, 1, 2))
                        k0 = WIN + u.tile(1) * 128
                        nc.scalar.activation(kT[:, u.half(1), :, k0:k0 + 128], TR[0][:, :].rearrange(
                            "p (a b) -> p a b", a=PR), ACT.Copy).then_inc(s.qk_out, 1)
                    if u.has(0):
                        values_out(1)
                    weights(1, 0)

                run(act, slot)

            @block.vector
            def _(dve):
                nc.vector.memset(xs[:, 0:WIN + 1], 0.0).then_inc(s.pads, 1)
                nc.vector.memset(kT[:, :, :, 0:WIN], 0.0)
                nc.vector.memset(vv[:, :, :, :, HD:HD + 1], 1.0).then_inc(s.pads, 2)

                def split(loaded, first):
                    dve.wait_ge(s.xs_ready, loaded)
                    nc.vector.tensor_copy(xp[0][:, :], xs[:, :]).then_inc(s.split_done, 1)
                    dve.wait_ge(s.split_done, first)
                    nc.vector.tensor_tensor(xp[1][:, :], xs[:, :], xp[0][:, :].bitcast(F32),
                                            ALU.subtract).then_inc(s.split_done, 1)

                split(layer * (32 * NB) + 32, layer * (2 * NB) + 1)
                for t in range(2):
                    nc.vector.tensor_tensor(ctab[:, t, :, :], g.cbase[:, t, :, :], scb[:, :, :], ALU.mult)
                    nc.vector.tensor_tensor(stab[:, t, :, 0:32], g.sbase[:, t, :, 0:32], scb[:, :, 32:64], ALU.mult)
                    last = nc.vector.tensor_tensor(stab[:, t, :, 32:64], g.sbase[:, t, :, 32:64],
                                                   scb[:, :, 0:32], ALU.mult)
                last.then_inc(s.tables, 1)
                dve.wait_ge(s.tables, layer + 1)

                def bc(x, n):
                    return x.unsqueeze(2).broadcast_to((128, 2, HG, n))

                def slot(u):
                    if u.has(0):
                        b, T = u.par(0), u.tile(0)
                        dve.wait_ge(s.proj_out, u.count(4, 0, 2))
                        if u.was(2):
                            dve.wait_ge(s.qk_done, u.count(2, 2, 2))
                        nc.vector.tensor_tensor(t1[:, b], raw[:, b], bc(ctab[:, T], HD), ALU.mult)
                        nc.vector.tensor_tensor(t2[:, b, :, :, 0:32], raw[:, b, :, :, 32:64],
                                                bc(stab[:, T, :, 0:32], 32), ALU.mult)
                        nc.vector.tensor_tensor(t2[:, b, :, :, 32:64], raw[:, b, :, :, 0:32],
                                                bc(stab[:, T, :, 32:64], 32), ALU.mult).then_inc(s.rot_done, 1)
                        dve.wait_ge(s.sq_done, u.count(1, 0, 1))
                        if u.was(2):
                            dve.wait_ge(s.rn_done, u.count(1, 2, 1))
                        nc.vector.tensor_reduce(ss[:, b, :], sq[:, :, :], AX.X, ALU.add).then_inc(s.sum_done, 1)
                        dve.wait_ge(s.sum_done, u.count(1, 0, 1))
                        nc.vector.tensor_scalar(ss[:, b, :], ss[:, b, :], 1e-24, None,
                                                ALU.max).then_inc(s.ss_done, 1)
                    if u.has(2):
                        b = u.par(2)
                        pv = [PV[e][:, 0:PR * (HD + 1)].rearrange("p (a b) -> p a b", a=PR) for e in range(2)]
                        for e in range(2):
                            dve.wait_ge(s.pv_done, u.count(2, 2, e + 1))
                            nc.vector.reciprocal(rs[:, e, :], pv[e][:, :, HD]).then_inc(s.rs_done, 1)
                        if u.was(4):
                            dve.wait_ge(s.oT_done, u.count(1, 4, 1))
                        for e in range(2):
                            dve.wait_ge(s.rs_done, u.count(2, 2, e + 1))
                            nc.vector.tensor_tensor(
                                on[:, b, :, :].rearrange("p (a e) d -> p a e d", e=2)[:, :, e, :],
                                pv[e][:, :, 0:HD], rs[:, e, :].unsqueeze(2).broadcast_to((128, PR, HD)),
                                ALU.mult).then_inc(s.norm_done, 1)
                    if u.k == UPS - 1 and u.lead < NB - 1:
                        dve.wait_ge(s.proj_done, u.count(4, 0, 4))
                        loaded = layer * (32 * NB) + 32 * (u.lead + 2)
                        split(loaded if u.loop is None else loaded + u.loop * 32, u.splits(u.lead + 1, 1))
                    if u.has(3) and u.k % 2 == 0:
                        dve.wait_ge(s.wo_done, u.tiles(3, 1))
                        c0 = u.tile(3) * 128
                        col = slice((u.lead - 1) * SEQ + c0, (u.lead - 1) * SEQ + c0 + 128)
                        if u.loop is not None:
                            col = bass.ds(u.loop * SEQ + c0, 128)
                        nc.vector.tensor_tensor(yT[:, col], TR[1][:, 0:128], yT[:, col],
                                                ALU.add).then_inc(s.wo_out, 1)
                    if u.has(1):
                        b = u.par(1)
                        for e in range(2):
                            sc = SC[e][:, 0:PR * KEYS].rearrange("p (a b) -> p a b", a=PR)
                            dve.wait_ge(s.score_done, u.count(2, 1, e + 1))
                            nc.vector.tensor_reduce(mx[:, e, :], sc, AX.X, ALU.max).then_inc(s.mx_done, 1)
                            dve.wait_ge(s.mx_done, u.count(2, 1, e + 1))
                            if u.was(3):
                                dve.wait_ge(s.pT_done, u.count(2, 3, 2))
                            nc.vector.tensor_tensor(pb[:, b, e], sc, mx[:, e, :].unsqueeze(2).broadcast_to(
                                (128, PR, KEYS)), ALU.subtract).then_inc(s.sub_done, 1)

                run(dve, slot)

            @block.gpsimd
            def _(pool):
                def slot(u):
                    if not u.has(0):
                        return
                    b = u.par(0)
                    pool.wait_ge(s.rot_done, u.count(1, 0, 1))
                    nc.gpsimd.tensor_tensor(t1[:, b], t1[:, b], t2[:, b], ALU.add).then_inc(s.radd_done, 1)
                    pool.wait_ge(s.ss_done, u.count(1, 0, 1))
                    if u.was(1):
                        pool.wait_ge(s.qk_ready, u.count(1, 1, 1))
                    nc.gpsimd.tensor_tensor(rn[:, b, :], ss[:, b, :], g.mhalf[:, 0:2 * HG], ALU.pow).then_inc(s.rn_done, 1)
                    pool.wait_ge(s.radd_done, u.count(1, 0, 1))
                    pool.wait_ge(s.rn_done, u.count(1, 0, 1))
                    q = t1[:, b].rearrange("p j h d -> p (j h) d")
                    nc.gpsimd.tensor_tensor(q, q, rn[:, b, :].unsqueeze(2).broadcast_to((128, 2 * HG, HD)),
                                            ALU.mult).then_inc(s.qk_ready, 1)

                run(pool, slot)
                pool.wait_ge(s.gated_loaded, layer * (16 * GATED_LOADS) + 16 * GATED_LOADS)
                nc.gpsimd.tensor_tensor(g.lw.w1[0][:, :], g.lw.w1_full[:, :], g.zero.broadcast_to((128, 2 * GLU)),
                                        ALU.add).then_inc(s.w1_high, 1)
                pool.wait_ge(s.w1_high, layer + 1)
                nc.gpsimd.tensor_tensor(g.lw.w1[1][:, :], g.lw.w1_full[:, :], g.lw.w1[0][:, :].bitcast(F32),
                                        ALU.subtract)


WA_SEMS = ("w_o", "gated_loaded", "w1_high", "split_done", "pads", "tables", "xs_ready", "proj_done", "proj_out", "sq_done", "ss_done",
           "sum_done", "rn_done", "rot_done", "radd_done", "qk_ready", "qk_done", "qk_out", "score_done", "mx_done",
           "sub_done", "exp_done", "pT_done", "pT_out", "pv_done", "rs_done", "norm_done", "oT_done", "oT_out",
           "wo_done", "wo_out")


class Group:

    def __init__(self, at, loop=None, step=1, base=0):
        self.at, self.loop, self.step, self.base = at, loop, step, base
        self.par = at % 2

    def count(self, per, r, lag=0):
        n = self.base + (per * (self.at - lag) + r)
        return n if self.loop is None else n + self.loop * (per * self.step)

    def has(self, lag):
        return self.loop is not None and self.at >= 1 or self.at >= lag

    def turns(self, per):
        n = per * (self.at // 2 + 1)
        return n if self.loop is None else n + self.loop * per

    def cols(self, start=0, size=GRP):
        if self.loop is None:
            return slice(self.at * GRP + start, self.at * GRP + start + size)
        return bass.ds(self.loop * (GRP * self.step) + (self.at * GRP + start), size)

    def seq(self, q):
        if self.loop is None:
            return slice(self.at * SPG + q, self.at * SPG + q + 1)
        return bass.ds(self.loop * (SPG * self.step) + (self.at * SPG + q), 1)


def skewed(eng, order, steps, n=NGRP):
    deepest = max(lag for _, lag in order)
    head = deepest + 2
    pairs = (n - head) // 2

    def turn(t, loop=None):
        for name, lag in order:
            if name in steps and (loop is not None or 0 <= t - lag < n):
                steps[name](Group(t - lag, loop, 2))

    for t in range(head):
        turn(t)
    with eng.Fori(0, pairs) as loop:
        turn(head, loop)
        turn(head + 1, loop)
    for t in range(head + 2 * pairs, n + deepest):
        turn(t)


def ring_wait(eng, sem, grp, per, lag=2):
    if grp.at >= lag or grp.loop is not None:
        eng.wait_ge(sem, grp.count(per, per, lag))


LN_ORDER = [("front", 0), ("back", 1)]


def layernorm_modulate(nc, tag, g, dst, scale, bias, from_dram=None):
    with ExitStack() as ctx:
        sb = lambda n, s, d=F32: ctx.enter_context(nc.sbuf_tensor(tag + n, s, d))
        ps = lambda n: ctx.enter_context(nc.psum_tensor(tag + n, [128, GRP], F32))
        sem = phase_semaphores(nc, ctx, tag)
        src = sb("src", [128, 2, TPG, D])
        xn = sb("xn", [128, 2, TPG, D])
        st = sb("st", [128, 2, TPG, 6])
        mv = sb("mv", [128, 2, TPG, 2])
        rstd = sb("rstd", [128, 2, TPG])
        tick = sb("tick", [128, 1])
        TA = [ps("ta0"), ps("ta1")]
        TB = [ps("tb0"), ps("tb1")]
        src_ready = [sem("src_ready0"), sem("src_ready1")]
        turned, stats, aggr, varp, rstd_done, normed, back_done, out_done, x_done = map(sem, (
            "turned", "stats", "aggr", "varp", "rstd_done", "normed", "back_done", "out_done", "x_done"))
        per_src = 16 if from_dram is not None else 1
        with nc.Block() as block:
            if from_dram is not None:
                @block.sync
                def _(sp):
                    tokens = from_dram.rearrange("b (t p) f -> p (b t) f", p=128)

                    def front(u):
                        ring_wait(sp, normed, u, 1)
                        ring_wait(sp, turned, u, 1)
                        t = slice(u.at * TPG, (u.at + 1) * TPG) if u.loop is None else bass.ds(
                            u.loop * (2 * TPG) + u.at * TPG, TPG)
                        sp.dma_start(src[:, u.par], tokens[:, t, :]).then_inc(src_ready[u.par], 16)

                    skewed(sp, LN_ORDER, {"front": front})

            @block.tensor
            def _(pe):
                def front(u):
                    pe.wait_ge(src_ready[u.par], u.turns(per_src))
                    if from_dram is None:
                        ring_wait(pe, normed, u, 1)
                    else:
                        ring_wait(pe, x_done, u, 1)
                    for t in range(TPG):
                        last = nc.tensor.transpose(TA[u.par][:, t * D:(t + 1) * D], src[:, u.par, t, :], g.ident[:, :])
                    last.then_inc(turned, 1)

                def back(u):
                    pe.wait_ge(normed, u.count(1, 1))
                    ring_wait(pe, out_done, u, SPG)
                    for t in range(TPG):
                        last = nc.tensor.transpose(TB[u.par][:, t * D:(t + 1) * D], xn[:, u.par, t, :], g.ident[:, :])
                    last.then_inc(back_done, 1)

                skewed(pe, LN_ORDER, {"front": front, "back": back})

            @block.vector
            def _(dve):
                def front(u):
                    if from_dram is None:
                        ring_wait(dve, turned, u, 1)
                        nc.vector.tensor_copy(src[:, u.par].rearrange("p t f -> p (t f)"),
                                              g.xT[:, u.cols()]).then_inc(src_ready[u.par], 1)
                        dve.wait_ge(turned, u.count(1, 1))
                        rows = TA[u.par][:, :].rearrange("p (t f) -> p t f", t=TPG)
                    else:
                        dve.wait_ge(src_ready[u.par], u.turns(16))
                        rows = src[:, u.par]
                    for t in range(TPG):
                        last = nc.vector.bn_stats(st[:, u.par, t, :], rows[:, t, :])
                    last.then_inc(stats, 1)
                    dve.wait_ge(stats, u.count(1, 1))
                    nc.vector.memset(tick[:, :], 0.0)
                    for t in range(TPG):
                        last = nc.vector.bn_aggr(mv[:, u.par, t, :], st[:, u.par, t, :])
                    last.then_inc(aggr, 1)
                    dve.wait_ge(rstd_done, u.count(1, 1))
                    ring_wait(dve, back_done, u, 1)
                    for t in range(TPG):
                        last = nc.vector.tensor_scalar(xn[:, u.par, t, :], rows[:, t, :], mv[:, u.par, t, 0:1],
                                                       rstd[:, u.par, t:t + 1], ALU.subtract, ALU.mult)
                    last.then_inc(normed, 1)

                skewed(dve, LN_ORDER, {"front": front})

            @block.gpsimd
            def _(pool):
                def front(u):
                    pool.wait_ge(aggr, u.count(1, 1))
                    nc.gpsimd.tensor_tensor(rstd[:, u.par, :], mv[:, u.par, :, 1], g.eps[:, 0:TPG], ALU.add).then_inc(varp, 1)
                    pool.wait_ge(varp, u.count(1, 1))
                    nc.gpsimd.tensor_tensor(rstd[:, u.par, :], rstd[:, u.par, :], g.mhalf[:, 0:TPG],
                                            ALU.pow).then_inc(rstd_done, 1)

                skewed(pool, LN_ORDER, {"front": front})

            @block.scalar
            def _(act):
                def front(u):
                    if from_dram is not None:
                        act.wait_ge(turned, u.count(1, 1))
                        nc.scalar.activation(g.xT[:, u.cols()], TA[u.par][:, :], ACT.Copy).then_inc(x_done, 1)

                def back(u):
                    act.wait_ge(back_done, u.count(1, 1))
                    for q in range(SPG):
                        nc.scalar.activation(dst[:, u.cols(q * SEQ, SEQ)], TB[u.par][:, q * SEQ:(q + 1) * SEQ],
                                             ACT.Identity, bias=bias[:, u.seq(q)],
                                             scale=scale[:, u.seq(q)]).then_inc(out_done, 1)

                skewed(act, LN_ORDER, {"front": front, "back": back})


GATED_LOADS = 4 + 3 * GCH


def layer_weights(nc, ctx):
    sb = lambda n, s, d=F32: ctx.enter_context(nc.sbuf_tensor("lw_" + n, s, d))
    parts = ("high", "low")
    return type("LayerWeights", (), dict(
        wqkv_full=sb("wqkv", [128, 3, INNER]), wqkv=[sb("wqkv_" + n, [128, 3, INNER], F32R) for n in parts],
        scb=sb("scb", [128, 2, HD]),
        w1_full=sb("w1", [128, 2 * GLU]), w1=[sb("w1_" + n, [128, 2 * GLU], F32R) for n in parts],
        w2=sb("w2", [128, GCH, D]), b1=sb("b1", [128, 2, GCH]),
        vec=sb("vec", [128, 3])))


def attention_weights_load(sp, layer, g, w, loaded):
    lw = g.lw
    sp.dma_start(lw.wqkv_full[:, :, :], w.Wqkv[bass.ds(layer, 1)].rearrange(
        "l p (t n) -> (l p) t n", t=3)).then_inc(loaded, 16)
    for n, v in enumerate((w.q_scale, w.k_scale)):
        sp.dma_start(lw.scb[:, n, :], v[bass.ds(layer, 1)].broadcast_to((128, HD))).then_inc(loaded, 16)


def gated_weights_load(sp, layer, g, w):
    lw, loaded = g.lw, g.wa_sems.gated_loaded
    sp.dma_start(lw.w1_full[:, :], w.W1[bass.ds(layer, 1)].rearrange("l p n -> (l p) n")).then_inc(loaded, 16)
    for j in range(GCH):
        r = glu_rows(j)
        sp.dma_start(lw.w2[0:r, j, :], w.W2[bass.ds(layer, 1), j * GW:j * GW + r, :].rearrange(
            "l p n -> (l p) n")).then_inc(loaded, 16)
        for a in range(2):
            c0 = a * GLU + j * GW
            sp.dma_start(lw.b1[0:r, a, j:j + 1], w.b1[bass.ds(layer, 1), c0:c0 + r].rearrange(
                "l p -> p l")).then_inc(loaded, 16)
    for n, v in enumerate((w.ln_g, w.ln_b, w.b2)):
        sp.dma_start(lw.vec[:, n:n + 1], v[bass.ds(layer, 1), :].rearrange("l p -> p l")).then_inc(loaded, 16)


def first_attention_weights(nc, g, w):
    with ExitStack() as ctx:
        sem = phase_semaphores(nc, ctx, "fw_")
        loaded, high = sem("loaded"), sem("high")
        with nc.Block() as block:

            @block.sync
            def _(sp):
                attention_weights_load(sp, 0, g, w, loaded)

            @block.vector
            def _(dve):
                full, (hi, lo) = g.lw.wqkv_full, g.lw.wqkv
                dve.wait_ge(loaded, 48)
                nc.vector.tensor_copy(hi[:, :, :], full[:, :, :]).then_inc(high, 1)
                dve.wait_ge(high, 1)
                nc.vector.tensor_tensor(lo[:, :, :], full[:, :, :], hi[:, :, :].bitcast(F32), ALU.subtract)


GM_SEMS = ("w_next", "w_high", "xn_parts", "fs_ready", "fs_turned", "stats", "aggr", "varp", "rstd", "normed", "xn_turned",
           "xn_out", "gate_done", "a_done", "gelu_done", "act_done", "down_done", "y_out", "pads")


def gated_mlp(nc, layer, g, w):
    yT, ident = g.yT, g.ident
    with ExitStack() as ctx:
        sb = lambda n, s, d=F32: ctx.enter_context(nc.sbuf_tensor("gm_" + n, s, d))
        ps = lambda n: ctx.enter_context(nc.psum_tensor("gm_" + n, [128, GRP], F32))
        s = g.gm_sems
        w1, w2, b1, vec = g.lw.w1, g.lw.w2, g.lw.b1, g.lw.vec
        fs = sb("fs", [128, GRP])
        st = sb("st", [128, TPG, 6])
        mv = sb("mv", [128, TPG, 2])
        rstd = sb("rstd", [128, TPG])
        tick = sb("tick", [128, 1])
        xn = sb("xn", [128, TPG, D])
        xnT = sb("xnT", [128, GRP])
        xp = [sb(f"x{n}", [128, GRP], F32R) for n in ("high", "low")]
        gl = sb("gl", [128, 2, GRP])
        hid = sb("hid", [128, 2, GRP])
        TA, TB, Y = ps("ta"), ps("tb"), ps("y")
        GT = [ps("g0"), ps("g1")]
        AT = [ps("a0"), ps("a1")]

        class L(Group):
            def __init__(self, at, loop=None):
                super().__init__(at, loop)

            def n(self, per, r, lag=0):
                return layer * (per * NGRP) + self.count(per, r, lag)

        def run(eng, prepare, multiply):
            prepare(L(0), 0), prepare(L(0), 1), prepare(L(0), 2)
            multiply(L(0), lambda part: prepare(L(1), part))
            with eng.Fori(0, NGRP - 2) as loop:
                multiply(L(1, loop), lambda part: prepare(L(2, loop), part))
            multiply(L(NGRP - 1), lambda part: None)

        def wait_chunk(eng, sem, u, per, r):
            if r > 0 or u.at > 0:
                eng.wait_ge(sem, u.n(per, r))

        with nc.Block() as block:

            @block.sync
            def _(sp):
                sp.wait_ge(s.pads, layer + 1)

                def shift(u):
                    sp.dma_start(fs[0:64, :], yT[0:64, u.cols()]).then_inc(s.fs_ready, 16)
                    for q in range(SPG):
                        sp.dma_start(fs[64:128, q * SEQ + 1:(q + 1) * SEQ],
                                     yT[64:128, u.cols(q * SEQ, SEQ - 1)]).then_inc(s.fs_ready, 16)

                shift(L(0))
                attention_weights_load(sp, (layer + 1) % DEPTH, g, w, s.w_next)
                with sp.Fori(0, NGRP - 1) as loop:
                    u = L(1, loop)
                    sp.wait_ge(s.fs_turned, u.n(1, 1, 1))
                    shift(u)

            @block.tensor
            def _(pe):
                def prepare(u, part):
                    if part == 0:
                        pe.wait_ge(s.fs_ready, u.n(48, 48))
                        if u.has(1):
                            pe.wait_ge(s.normed, u.n(1, 1, 1))
                        for t in range(TPG):
                            last = nc.tensor.transpose(TA[:, t * D:(t + 1) * D], fs[:, t * D:(t + 1) * D], ident[:, :])
                        last.then_inc(s.fs_turned, 1)
                    elif part == 1:
                        pe.wait_ge(s.normed, u.n(1, 1))
                        if u.has(1):
                            pe.wait_ge(s.xn_out, u.n(2, 2, 1))
                        for t in range(TPG):
                            last = nc.tensor.transpose(TB[:, t * D:(t + 1) * D], xn[:, t, :], ident[:, :])
                        last.then_inc(s.xn_turned, 1)

                def multiply(u, prepare_next):
                    def down(j):
                        r = glu_rows(j)
                        pe.wait_ge(s.act_done, u.n(GCH, j + 1))
                        if j == 0:
                            wait_chunk(pe, s.y_out, u, 1, 0)
                        last = nc.tensor.matmul(Y[:, :], w2[0:r, j, :], hid[0:r, j % 2, :],
                                                start=(j == 0), stop=(j == GCH - 1))
                        if j == GCH - 1:
                            last.then_inc(s.down_done, 1)

                    pe.wait_ge(s.xn_parts, u.n(1, 1))
                    for j in range(GCH):
                        r = glu_rows(j)
                        wait_chunk(pe, s.gelu_done, u, GCH, max(j - 1, 0))
                        three_passes(nc, GT[j % 2][0:r, :], [x[:, GLU + j * GW:GLU + j * GW + r] for x in w1],
                                     [x[:, :] for x in xp]).then_inc(s.gate_done, 1)
                        wait_chunk(pe, s.act_done, u, GCH, max(j - 1, 0))
                        three_passes(nc, AT[j % 2][0:r, :], [x[:, j * GW:j * GW + r] for x in w1],
                                     [x[:, :] for x in xp]).then_inc(s.a_done, 1)
                        if j == GCH - 1:
                            prepare_next(1)
                        if j >= 1:
                            down(j - 1)
                        if j == 0:
                            prepare_next(0)
                    down(GCH - 1)

                run(pe, prepare, multiply)

            @block.scalar
            def _(act):
                def prepare(u, part):
                    if part == 1:
                        act.wait_ge(s.xn_turned, u.n(1, 1))
                        if u.has(1):
                            act.wait_ge(s.xn_parts, u.n(1, 1, 1))
                        for dst in (xnT, xp[0]):
                            if dst is xp[0] and u.has(1):
                                act.wait_ge(s.a_done, u.n(GCH, GCH, 1))
                            nc.scalar.activation(dst[:, :], TB[:, :], ACT.Identity, bias=vec[:, 1:2],
                                                 scale=vec[:, 0:1]).then_inc(s.xn_out, 1)

                def multiply(u, prepare_next):
                    for j in range(GCH):
                        r = glu_rows(j)
                        act.wait_ge(s.gate_done, u.n(GCH, j + 1))
                        wait_chunk(act, s.act_done, u, GCH, max(j - 1, 0))
                        nc.scalar.activation(gl[0:r, j % 2, :], GT[j % 2][0:r, :], ACT.Gelu,
                                             bias=b1[0:r, 1, j:j + 1]).then_inc(s.gelu_done, 1)
                    prepare_next(1)

                run(act, prepare, multiply)

            @block.vector
            def _(dve):
                nc.vector.memset(fs[:, :], 0.0).then_inc(s.pads, 1)
                rows = TA[:, :].rearrange("p (t f) -> p t f", t=TPG)

                def prepare(u, part):
                    if part == 0:
                        dve.wait_ge(s.fs_turned, u.n(1, 1))
                        for t in range(TPG):
                            last = nc.vector.bn_stats(st[:, t, :], rows[:, t, :])
                        last.then_inc(s.stats, 1)
                        dve.wait_ge(s.stats, u.n(1, 1))
                        if u.has(1):
                            dve.wait_ge(s.rstd, u.n(1, 1, 1))
                        nc.vector.memset(tick[:, :], 0.0)
                        for t in range(TPG):
                            last = nc.vector.bn_aggr(mv[:, t, :], st[:, t, :])
                        last.then_inc(s.aggr, 1)
                    elif part == 1:
                        dve.wait_ge(s.rstd, u.n(1, 1))
                        if u.has(1):
                            dve.wait_ge(s.xn_turned, u.n(1, 1, 1))
                        for t in range(TPG):
                            last = nc.vector.tensor_scalar(xn[:, t, :], rows[:, t, :], mv[:, t, 0:1],
                                                           rstd[:, t:t + 1], ALU.subtract, ALU.mult)
                        last.then_inc(s.normed, 1)
                    else:
                        dve.wait_ge(s.xn_out, u.n(2, 2))
                        nc.vector.tensor_tensor(xp[1][:, :], xnT[:, :], xp[0][:, :].bitcast(F32),
                                                ALU.subtract).then_inc(s.xn_parts, 1)

                def multiply(u, prepare_next):
                    for j in range(GCH):
                        r = glu_rows(j)
                        dve.wait_ge(s.gelu_done, u.n(GCH, j + 1))
                        dve.wait_ge(s.a_done, u.n(GCH, j + 1))
                        if j < 2:
                            wait_chunk(dve, s.down_done, u, 1, 0)
                        nc.vector.scalar_tensor_tensor(
                            out=hid[0:r, j % 2, :], in0=AT[j % 2][0:r, :], scalar=b1[0:r, 0, j:j + 1],
                            in1=gl[0:r, j % 2, :], op0=ALU.add, op1=ALU.mult).then_inc(s.act_done, 1)
                        if j < 2:
                            prepare_next(j)
                    prepare_next(2)
                    dve.wait_ge(s.down_done, u.n(1, 1))
                    nc.vector.scalar_tensor_tensor(out=yT[:, u.cols()], in0=Y[:, :], scalar=vec[:, 2:3],
                                                   in1=yT[:, u.cols()], op0=ALU.add, op1=ALU.add).then_inc(s.y_out, 1)

                run(dve, prepare, multiply)

            @block.gpsimd
            def _(pool):
                WCOLS = 3 * INNER // (NGRP - 2)
                full, hi, lo = (x[:, :, :].rearrange("p t n -> p (t n)") for x in (g.lw.wqkv_full, *g.lw.wqkv))

                def split_next(u):
                    here = bass.ds(u.loop * WCOLS, WCOLS)
                    pool.wait_ge(s.w_next, layer * 48 + 48)
                    nc.gpsimd.tensor_tensor(hi[:, here], full[:, here], g.zero.broadcast_to((128, WCOLS)),
                                            ALU.add).then_inc(s.w_high, 1)
                    pool.wait_ge(s.w_high, layer * (NGRP - 2) + u.loop + 1)
                    nc.gpsimd.tensor_tensor(lo[:, here], full[:, here], hi[:, here].bitcast(F32), ALU.subtract)

                def prepare(u, part):
                    if part == 0:
                        pool.wait_ge(s.aggr, u.n(1, 1))
                        if u.has(1):
                            pool.wait_ge(s.normed, u.n(1, 1, 1))
                        nc.gpsimd.tensor_tensor(rstd[:, :], mv[:, :, 1], g.eps[:, 0:TPG], ALU.add).then_inc(s.varp, 1)
                        pool.wait_ge(s.varp, u.n(1, 1))
                        nc.gpsimd.tensor_tensor(rstd[:, :], rstd[:, :], g.mhalf[:, 0:TPG], ALU.pow).then_inc(s.rstd, 1)

                def multiply(u, prepare_next):
                    prepare_next(0)
                    if u.loop is not None:
                        split_next(u)

                run(pool, prepare, multiply)


LA_ORDER = [("project", 0), ("feature", 1), ("to_rows", 0), ("weigh", 1), ("to_cols", 0), ("sum", 1),
            ("divide", 1), ("finish", 1)]


def linear_attention(nc, g, w):
    yT, ident = g.yT, g.ident
    with ExitStack() as ctx:
        sb = lambda n, s, d=F32: ctx.enter_context(nc.sbuf_tensor("la_" + n, s, d))
        ps = lambda n: ctx.enter_context(nc.psum_tensor("la_" + n, [128, GRP], F32))
        sem = phase_semaphores(nc, ctx, "la_")
        aT = g.aT
        wqkv = sb("wqkv", [128, 3, D])
        wf = sb("wf", [128, 2, D])
        vec = sb("vec", [128, 11])
        gvb = sb("gvb", [128, 2, D])
        hmask = sb("hmask", [128, D])
        hsel = sb("hsel", [128, HEADS])
        hprobe = sb("hprobe", [128, HEADS])
        hselT = sb("hselT", [HEADS, 128])
        pk0 = sb("pk0", [128, 1])
        col = sb("col", [128, 3, GRP])
        st = sb("st", [128, 3 * TPG, 6])
        mv = sb("mv", [128, 3 * TPG, 2])
        rstd = sb("rstd", [128, 3 * TPG])
        st2 = sb("st2", [128, TPG, 6])
        mv2 = sb("mv2", [128, TPG, 2])
        rstd2 = sb("rstd2", [128, TPG])
        tick = sb("tick", [128, 1])
        row = sb("row", [128, 3, TPG, D])
        vt = sb("vt", [128, 2, TPG, D + 1])
        qk = sb("qk", [128, 2, 2, GRP])
        qsum = sb("qsum", [128, 2, SPG])
        probe = sb("probe", [128, SPG, HEADS])
        phi = sb("phi", [128, 2, GRP])
        mx = sb("mx", [HEADS, SPG])
        nm = sb("nm", [HEADS, SPG])
        ex = sb("ex", [HEADS, SPG, SEQ])
        tot = sb("tot", [HEADS, SPG])
        z0 = sb("z0", [HEADS, SPG])
        rc = sb("rc", [HEADS, SPG])
        s0 = sb("s0", [HEADS, SPG])
        sct = sb("sct", [128, TPG * HEADS + SPG])
        pkw = sb("pkw", [128, TPG, D])
        ks = sb("ks", [128, SPG])
        kvx = sb("kvx", [128, SPG, D + HEADS])
        dn = sb("dn", [128, TPG, HEADS])
        ao = sb("ao", [128, TPG, D])
        an = sb("an", [128, TPG, D])
        A = [ps(f"a{i}") for i in range(4)]
        B = [ps(f"b{i}") for i in range(4)]
        names = ("loaded pads pk0_t pk0_ready projected col_out rowed stats aggr varp rstd_done normed vt_scaled vt_ready "
                 "coled qk_out probe_done phi_done logits_done tanh_done plus1 mx_done nm_done exp_done tot_done rc_done "
                 "s0_done ex_done pk_turned sct_turned sct_out pkw_done kv_done ks_done kvx_done num_done dn_done rdn_done "
                 "ao_done stats2 aggr2 varp2 rstd2_done an_done an_turned a_out y_out").split()
        s = type("Sems", (), {n: sem(n) for n in names})

        def tiles(bank):
            return bank[:, :].rearrange("p (t f) -> p t f", t=TPG)

        with nc.Block() as block:

            @block.sync
            def _(sp):
                for n, v in enumerate((w.Wq, w.Wk, w.Wv)):
                    sp.dma_start(wqkv[:, n, :], v).then_inc(s.loaded, 16)
                for n, v in enumerate((w.Wfq, w.Wfk)):
                    sp.dma_start(wf[:, n, :], v).then_inc(s.loaded, 16)
                for n, v in enumerate((w.bq, w.bk, w.bv, w.gq, w.betaq, w.gk, w.betak, w.bfq, w.bfk, w.ga, w.ba)):
                    sp.dma_start(vec[:, n:n + 1], v.unsqueeze(1)).then_inc(s.loaded, 16)
                for n, v in enumerate((w.gv, w.betav)):
                    sp.dma_start(gvb[:, n, :], v.unsqueeze(0).broadcast_to((128, D))).then_inc(s.loaded, 16)
                for dst, v in ((hmask, w.c_hmask), (hsel, w.c_hsel), (hprobe, w.c_hprobe), (hselT, w.c_hselT)):
                    sp.dma_start(dst[:, :], v).then_inc(s.loaded, 16)

            ALL_LOADED = 16 * 22

            @block.tensor
            def _(pe):
                pe.wait_ge(s.loaded, ALL_LOADED)

                def project(u):
                    ring_wait(pe, s.qk_out, u, SPG + 1, 1)
                    ring_wait(pe, s.normed, u, 3, 1)
                    for n in range(3):
                        nc.tensor.matmul(A[n][:, :], wqkv[:, n, :], yT[:, u.cols()], start=True,
                                         stop=True).then_inc(s.projected, 1)

                def to_rows(u):
                    for n in range(3):
                        pe.wait_ge(s.col_out, u.count(3, n + 1))
                        out = A[(3 + n) % 4]
                        for t in range(TPG):
                            last = nc.tensor.transpose(out[:, t * D:(t + 1) * D], col[:, n, t * D:(t + 1) * D], ident[:, :])
                        last.then_inc(s.rowed, 1)

                def to_cols(u):
                    for n in range(2):
                        pe.wait_ge(s.normed, u.count(3, n + 1))
                        if n == 0:
                            pe.wait_ge(s.col_out, u.count(3, 3))
                        for t in range(TPG):
                            last = nc.tensor.transpose(A[2 + n][:, t * D:(t + 1) * D], row[:, n, t, :], ident[:, :])
                        last.then_inc(s.coled, 1)

                def feature(u):
                    pe.wait_ge(s.qk_out, u.count(SPG + 1, SPG + 1))
                    ring_wait(pe, s.ao_done, u, 2, 1)
                    ring_wait(pe, s.a_out, u, 1, 1)
                    for n in range(2):
                        nc.tensor.matmul(B[n][:, :], wf[:, n, :], qk[:, u.par, n, :], start=True,
                                         stop=True).then_inc(s.phi_done, 1)
                    pe.wait_ge(s.probe_done, u.count(1, 1))
                    ring_wait(pe, s.kvx_done, u, 1, 1)
                    for q in range(SPG):
                        last = nc.tensor.matmul(B[2][0:HEADS, q * SEQ:(q + 1) * SEQ], probe[:, q, :],
                                                qk[:, u.par, 1, q * SEQ:(q + 1) * SEQ], start=True, stop=True)
                    last.then_inc(s.logits_done, 1)

                def weigh(u):
                    pe.wait_ge(s.tanh_done, u.count(2, 2))
                    for t in range(TPG):
                        last = nc.tensor.transpose(B[1][:, t * D:(t + 1) * D], phi[:, 1, t * D:(t + 1) * D], ident[:, :])
                    last.then_inc(s.pk_turned, 1)
                    pe.wait_ge(s.s0_done, u.count(1, 1))
                    pe.wait_ge(s.ex_done, u.count(1, 1))
                    nc.tensor.matmul(B[3][:, TPG * HEADS:TPG * HEADS + SPG], hselT[:, :], s0[:, :], start=True, stop=True)
                    for t in range(TPG):
                        q, tt = divmod(t, TPG // SPG)
                        last = nc.tensor.transpose(B[3][:, t * HEADS:(t + 1) * HEADS], ex[:, q, tt * D:(tt + 1) * D],
                                                   ident[0:HEADS, 0:HEADS])
                    last.then_inc(s.sct_turned, 1)

                def sum_(u):
                    pe.wait_ge(s.pkw_done, u.count(1, 1))
                    pe.wait_ge(s.vt_ready, u.count(1, 1))
                    for q in range(SPG):
                        for tt in range(TPG // SPG):
                            t = q * (TPG // SPG) + tt
                            last = nc.tensor.matmul(B[2][:, q * (D + 1):(q + 1) * (D + 1)], pkw[:, t, :],
                                                    vt[:, u.par, t, :], start=(tt == 0), stop=(tt == TPG // SPG - 1))
                    last.then_inc(s.kv_done, 1)

                def divide(u):
                    pe.wait_ge(s.kvx_done, u.count(1, 1))
                    pe.wait_ge(s.plus1, u.count(1, 1))
                    for q in range(SPG):
                        for tt in range(TPG // SPG):
                            t = q * (TPG // SPG) + tt
                            last = nc.tensor.matmul(B[3 * q][:, tt * (D + HEADS):(tt + 1) * (D + HEADS)],
                                                    phi[:, 0, t * D:(t + 1) * D], kvx[:, q, :], start=True, stop=True)
                        last.then_inc(s.num_done, 1)

                def finish(u):
                    pe.wait_ge(s.an_done, u.count(1, 1))
                    for t in range(TPG):
                        last = nc.tensor.transpose(B[1][:, t * D:(t + 1) * D], an[:, t, :], ident[:, :])
                    last.then_inc(s.an_turned, 1)

                skewed(pe, LA_ORDER, {"project": project, "to_rows": to_rows, "to_cols": to_cols, "feature": feature,
                                      "weigh": weigh, "sum": sum_, "divide": divide, "finish": finish})

            @block.scalar
            def _(act):
                act.wait_ge(s.loaded, ALL_LOADED)
                nc.scalar.activation(pk0[:, :], vec[:, 8:9], ACT.Tanh).then_inc(s.pk0_t, 1)

                def project(u):
                    ring_wait(act, s.rowed, u, 3, 1)
                    for n in range(3):
                        act.wait_ge(s.projected, u.count(3, n + 1))
                        nc.scalar.activation(col[:, n, :], A[n][:, :], ACT.Identity,
                                             bias=vec[:, n:n + 1]).then_inc(s.col_out, 1)

                def to_cols(u):
                    act.wait_ge(s.coled, u.count(2, 1))
                    ring_wait(act, s.logits_done, u, 1)
                    ring_wait(act, s.probe_done, u, 1)
                    for q in range(SPG):
                        nc.scalar.activation(qk[:, u.par, 0, q * SEQ:(q + 1) * SEQ], A[2][:, q * SEQ:(q + 1) * SEQ],
                                             ACT.Identity, bias=vec[:, 4:5], scale=vec[:, 3:4],
                                             accum_out=qsum[:, u.par, q:q + 1]).then_inc(s.qk_out, 1)
                    act.wait_ge(s.coled, u.count(2, 2))
                    nc.scalar.activation(qk[:, u.par, 1, :], A[3][:, :], ACT.Identity, bias=vec[:, 6:7],
                                         scale=vec[:, 5:6]).then_inc(s.qk_out, 1)

                def feature(u):
                    ring_wait(act, s.num_done, u, 2, 1)
                    for n in range(2):
                        act.wait_ge(s.phi_done, u.count(2, n + 1))
                        nc.scalar.activation(phi[:, n, :], B[n][:, :], ACT.Tanh,
                                             bias=vec[:, 7 + n:8 + n]).then_inc(s.tanh_done, 1)
                    act.wait_ge(s.nm_done, u.count(1, 1))
                    ring_wait(act, s.sct_turned, u, 1, 1)
                    for q in range(SPG):
                        nc.scalar.activation(ex[:, q, :], B[2][0:HEADS, q * SEQ:(q + 1) * SEQ], ACT.Exp,
                                             bias=nm[:, q:q + 1], accum_out=tot[:, q:q + 1])
                    nc.scalar.activation(z0[:, :], nm[:, :], ACT.Exp).then_inc(s.exp_done, 1)

                def finish(u):
                    act.wait_ge(s.an_turned, u.count(1, 1))
                    nc.scalar.activation(aT[:, u.cols()], B[1][:, :], ACT.Identity, bias=vec[:, 10:11],
                                         scale=vec[:, 9:10]).then_inc(s.a_out, 1)

                skewed(act, LA_ORDER, {"project": project, "to_cols": to_cols, "feature": feature, "finish": finish})

            @block.vector
            def _(dve):
                nc.vector.memset(vt[:, :, :, D:D + 1], 1.0).then_inc(s.pads, 1)
                dve.wait_ge(s.pk0_t, 1)
                nc.vector.tensor_scalar(pk0[:, :], pk0[:, :], 1.0, None, ALU.add).then_inc(s.pk0_ready, 1)
                dve.wait_ge(s.loaded, ALL_LOADED)

                def to_rows(u):
                    for n in range(3):
                        dve.wait_ge(s.rowed, u.count(3, n + 1))
                        for t in range(TPG):
                            last = nc.vector.bn_stats(st[:, n * TPG + t, :], tiles(A[(3 + n) % 4])[:, t, :])
                    last.then_inc(s.stats, 1)
                    dve.wait_ge(s.stats, u.count(1, 1))
                    nc.vector.memset(tick[:, :], 0.0)
                    for t in range(3 * TPG):
                        last = nc.vector.bn_aggr(mv[:, t, :], st[:, t, :])
                    last.then_inc(s.aggr, 1)

                def to_cols(u):
                    dve.wait_ge(s.rstd_done, u.count(1, 1))
                    ring_wait(dve, s.vt_ready, u, 1, 1)
                    for n in range(3):
                        for t in range(TPG):
                            k = n * TPG + t
                            last = nc.vector.tensor_scalar(row[:, n, t, :], tiles(A[(3 + n) % 4])[:, t, :], mv[:, k, 0:1],
                                                           rstd[:, k:k + 1], ALU.subtract, ALU.mult)
                        last.then_inc(s.normed, 1)

                def feature(u):
                    dve.wait_ge(s.qk_out, u.count(SPG + 1, SPG))
                    ring_wait(dve, s.logits_done, u, 1, 1)
                    for q in range(SPG):
                        last = nc.vector.tensor_scalar(probe[:, q, :], hprobe[:, :], qsum[:, u.par, q:q + 1], None, ALU.mult)
                    last.then_inc(s.probe_done, 1)
                    dve.wait_ge(s.logits_done, u.count(1, 1))
                    nc.vector.tensor_reduce(mx[:, :], B[2][0:HEADS, :].rearrange("p (q k) -> p q k", q=SPG), AX.X,
                                            ALU.max).then_inc(s.mx_done, 1)
                    dve.wait_ge(s.mx_done, u.count(1, 1))
                    nc.vector.tensor_scalar(nm[:, :], mx[:, :], 0.0, -1.0, ALU.max, ALU.mult).then_inc(s.nm_done, 1)

                def weigh(u):
                    dve.wait_ge(s.tanh_done, u.count(2, 1))
                    nc.vector.tensor_scalar(phi[:, 0, :], phi[:, 0, :], 1.0, None, ALU.add).then_inc(s.plus1, 1)
                    dve.wait_ge(s.exp_done, u.count(1, 1))
                    nc.vector.tensor_tensor(tot[:, :], tot[:, :], z0[:, :], ALU.add).then_inc(s.tot_done, 1)
                    dve.wait_ge(s.tot_done, u.count(1, 1))
                    nc.vector.reciprocal(rc[:, :], tot[:, :]).then_inc(s.rc_done, 1)
                    dve.wait_ge(s.rc_done, u.count(1, 1))
                    nc.vector.tensor_tensor(s0[:, :], z0[:, :], rc[:, :], ALU.mult).then_inc(s.s0_done, 1)
                    nc.vector.tensor_tensor(ex[:, :, :], ex[:, :, :], rc[:, :].unsqueeze(2).broadcast_to(
                        (HEADS, SPG, SEQ)), ALU.mult).then_inc(s.ex_done, 1)
                    dve.wait_ge(s.sct_turned, u.count(1, 1))
                    nc.vector.tensor_copy(sct[:, :], B[3][:, 0:TPG * HEADS + SPG]).then_inc(s.sct_out, 1)
                    dve.wait_ge(s.sct_out, u.count(1, 1))
                    dve.wait_ge(s.pk_turned, u.count(1, 1))
                    for t in range(TPG):
                        last = nc.vector.scalar_tensor_tensor(
                            out=pkw[:, t, :].rearrange("p (h d) -> p h d", h=HEADS),
                            in0=tiles(B[1])[:, t, :].rearrange("p (h d) -> p h d", h=HEADS), scalar=1.0,
                            in1=sct[:, t * HEADS:(t + 1) * HEADS].unsqueeze(2).broadcast_to((128, HEADS, LIN_HD)),
                            op0=ALU.add, op1=ALU.mult)
                    last.then_inc(s.pkw_done, 1)

                def sum_(u):
                    kv = B[2][:, 0:SPG * (D + 1)].rearrange("p (q e) -> p q e", q=SPG)
                    dve.wait_ge(s.kv_done, u.count(1, 1))
                    dve.wait_ge(s.pk0_ready, 1)
                    nc.vector.scalar_tensor_tensor(out=ks[:, :], in0=sct[:, TPG * HEADS:TPG * HEADS + SPG],
                                                   scalar=pk0[:, 0:1], in1=kv[:, :, D], op0=ALU.mult,
                                                   op1=ALU.add).then_inc(s.ks_done, 1)
                    nc.vector.tensor_tensor(kvx[:, :, 0:D], kv[:, :, 0:D], hmask[:, :].unsqueeze(1).broadcast_to(
                        (128, SPG, D)), ALU.mult)
                    dve.wait_ge(s.ks_done, u.count(1, 1))
                    for q in range(SPG):
                        last = nc.vector.tensor_scalar(kvx[:, q, D:D + HEADS], hsel[:, :], ks[:, q:q + 1], None, ALU.mult)
                    last.then_inc(s.kvx_done, 1)

                def divide(u):
                    half = TPG // SPG
                    nd = [B[3 * q][:, 0:half * (D + HEADS)].rearrange("p (t e) -> p t e", t=half) for q in range(SPG)]
                    for q in range(SPG):
                        dve.wait_ge(s.num_done, u.count(SPG, q + 1))
                        last = nc.vector.tensor_scalar(dn[:, q * half:(q + 1) * half, :], nd[q][:, :, D:D + HEADS], 1e-6,
                                                       None, ALU.add)
                    last.then_inc(s.dn_done, 1)
                    dve.wait_ge(s.dn_done, u.count(1, 1))
                    nc.vector.reciprocal(dn[:, :, :], dn[:, :, :]).then_inc(s.rdn_done, 1)
                    dve.wait_ge(s.rdn_done, u.count(1, 1))
                    for q in range(SPG):
                        nc.vector.tensor_tensor(
                            ao[:, q * half:(q + 1) * half, :].rearrange("p t (h d) -> p t h d", h=HEADS),
                            nd[q][:, :, 0:D].rearrange("p t (h d) -> p t h d", h=HEADS),
                            dn[:, q * half:(q + 1) * half, :].unsqueeze(3).broadcast_to((128, half, HEADS, LIN_HD)),
                            ALU.mult).then_inc(s.ao_done, 1)
                    dve.wait_ge(s.ao_done, u.count(SPG, SPG))
                    for t in range(TPG):
                        last = nc.vector.bn_stats(st2[:, t, :], ao[:, t, :])
                    last.then_inc(s.stats2, 1)
                    dve.wait_ge(s.stats2, u.count(1, 1))
                    nc.vector.memset(tick[:, :], 0.0)
                    for t in range(TPG):
                        last = nc.vector.bn_aggr(mv2[:, t, :], st2[:, t, :])
                    last.then_inc(s.aggr2, 1)

                def finish(u):
                    dve.wait_ge(s.rstd2_done, u.count(1, 1))
                    for t in range(TPG):
                        last = nc.vector.tensor_scalar(an[:, t, :], ao[:, t, :], mv2[:, t, 0:1], rstd2[:, t:t + 1],
                                                       ALU.subtract, ALU.mult)
                    last.then_inc(s.an_done, 1)
                    dve.wait_ge(s.a_out, u.count(1, 1))
                    nc.vector.tensor_tensor(yT[:, u.cols()], yT[:, u.cols()], aT[:, u.cols()], ALU.add).then_inc(s.y_out, 1)

                skewed(dve, LA_ORDER, {"to_rows": to_rows, "to_cols": to_cols, "feature": feature, "weigh": weigh,
                                       "sum": sum_, "divide": divide, "finish": finish})

            @block.gpsimd
            def _(pool):
                pool.wait_ge(s.loaded, ALL_LOADED)
                pool.wait_ge(s.pads, 1)

                def to_rows(u):
                    pool.wait_ge(s.aggr, u.count(1, 1))
                    nc.gpsimd.tensor_tensor(rstd[:, :], mv[:, :, 1], g.eps[:, 0:3 * TPG], ALU.add).then_inc(s.varp, 1)
                    pool.wait_ge(s.varp, u.count(1, 1))
                    nc.gpsimd.tensor_tensor(rstd[:, :], rstd[:, :], g.mhalf[:, 0:3 * TPG], ALU.pow).then_inc(s.rstd_done, 1)

                def to_cols(u):
                    pool.wait_ge(s.normed, u.count(3, 3))
                    ring_wait(pool, s.kv_done, u, 1)
                    nc.gpsimd.tensor_tensor(vt[:, u.par, :, 0:D], row[:, 2, :, :], gvb[:, 0, :].unsqueeze(1).broadcast_to(
                        (128, TPG, D)), ALU.mult).then_inc(s.vt_scaled, 1)
                    pool.wait_ge(s.vt_scaled, u.count(1, 1))
                    nc.gpsimd.tensor_tensor(vt[:, u.par, :, 0:D], vt[:, u.par, :, 0:D], gvb[:, 1, :].unsqueeze(
                        1).broadcast_to((128, TPG, D)), ALU.add).then_inc(s.vt_ready, 1)

                def divide(u):
                    pool.wait_ge(s.aggr2, u.count(1, 1))
                    nc.gpsimd.tensor_tensor(rstd2[:, :], mv2[:, :, 1], g.eps[:, 0:TPG], ALU.add).then_inc(s.varp2, 1)
                    pool.wait_ge(s.varp2, u.count(1, 1))
                    nc.gpsimd.tensor_tensor(rstd2[:, :], rstd2[:, :], g.mhalf[:, 0:TPG], ALU.pow).then_inc(s.rstd2_done, 1)

                skewed(pool, LA_ORDER, {"to_rows": to_rows, "to_cols": to_cols, "divide": divide})


MLP_ORDER = [("up", 0), ("down", 0)]


def plain_mlp(nc, tag, g, src, w1_d, b1_d, w2_d, b2_d, gate, skip=None, out_d=None):
    xT, ident = g.xT, g.ident
    with ExitStack() as ctx:
        sb = lambda n, s, d=F32: ctx.enter_context(nc.sbuf_tensor(tag + n, s, d))
        ps = lambda n: ctx.enter_context(nc.psum_tensor(tag + n, [128, GRP], F32))
        sem = phase_semaphores(nc, ctx, tag)
        w1 = sb("w1", [128, MLP])
        w2 = sb("w2", [128, MCH, D])
        b1 = sb("b1", [128, MCH])
        b2 = sb("b2", [128, 1])
        hid = sb("hid", [128, 2, MCH, GRP])
        sm = sb("sm", [128, 2, GRP])
        xo = sb("xo", [128, 2, GRP])
        rows = sb("rows", [128, 2, TPG, D])
        H = [ps(f"h{i}") for i in range(MCH)]
        Y = [ps("y0"), ps("y1")]
        R = [ps("r0"), ps("r1")]
        loaded, up_done, gelu_done, down_done, sum_done, x_out, turned, row_out = map(sem, (
            "loaded", "up_done", "gelu_done", "down_done", "sum_done", "x_out", "turned", "row_out"))
        stored = [sem("stored0"), sem("stored1")]
        order = [("up", 0), ("down", 1)] + ([("turn", 1)] if out_d is None else [("turn", 2)])

        with nc.Block() as block:

            @block.sync
            def _(sp):
                sp.dma_start(w1[:, :], w1_d).then_inc(loaded, 16)
                for j in range(MCH):
                    sp.dma_start(b1[:, j:j + 1], b1_d[j * 128:(j + 1) * 128].unsqueeze(1)).then_inc(loaded, 16)
                sp.dma_start(w2[:, :, :], w2_d.rearrange("(j p) n -> p j n", p=128)).then_inc(loaded, 16)
                sp.dma_start(b2[:, :], b2_d.unsqueeze(1)).then_inc(loaded, 16)
                if out_d is not None:
                    tokens = out_d.rearrange("b (t p) f -> p (b t) f", p=128)

                    def turn(u):
                        sp.wait_ge(row_out, u.count(1, 1))
                        t = slice(u.at * TPG, (u.at + 1) * TPG) if u.loop is None else bass.ds(
                            u.loop * (2 * TPG) + u.at * TPG, TPG)
                        sp.dma_start(tokens[:, t, :], rows[:, u.par]).then_inc(stored[u.par], 16)

                    skewed(sp, order, {"turn": turn})
                    for sem_ in stored:
                        sp.wait_ge(sem_, 16 * (NGRP // 2))

            @block.tensor
            def _(pe):
                pe.wait_ge(loaded, 16 * (3 + MCH))

                def up(u):
                    for j in range(MCH):
                        if u.has(1):
                            pe.wait_ge(gelu_done, u.count(MCH, j + 1, 1))
                        nc.tensor.matmul(H[j][:, :], w1[:, j * 128:(j + 1) * 128], src[:, u.cols()], start=True,
                                         stop=True).then_inc(up_done, 1)

                def down(u):
                    ring_wait(pe, sum_done, u, 1)
                    for j in range(MCH):
                        pe.wait_ge(gelu_done, u.count(MCH, j + 1))
                        last = nc.tensor.matmul(Y[u.par][:, :], w2[:, j, :], hid[:, u.par, j, :], start=(j == 0),
                                                stop=(j == MCH - 1))
                    last.then_inc(down_done, 1)

                def turn(u):
                    pe.wait_ge(x_out, u.count(1, 1))
                    ring_wait(pe, row_out, u, 1)
                    for t in range(TPG):
                        last = nc.tensor.transpose(R[u.par][:, t * D:(t + 1) * D], xo[:, u.par, t * D:(t + 1) * D],
                                                   ident[:, :])
                    last.then_inc(turned, 1)

                steps = {"up": up, "down": down}
                if out_d is not None:
                    steps["turn"] = turn
                skewed(pe, order, steps)

            @block.scalar
            def _(act):
                act.wait_ge(loaded, 16 * (3 + MCH))

                def up(u):
                    ring_wait(act, down_done, u, 1)
                    for j in range(MCH):
                        act.wait_ge(up_done, u.count(MCH, j + 1))
                        nc.scalar.activation(hid[:, u.par, j, :], H[j][:, :], ACT.Gelu,
                                             bias=b1[:, j:j + 1]).then_inc(gelu_done, 1)

                skewed(act, order, {"up": up})

            @block.vector
            def _(dve):
                dve.wait_ge(loaded, 16 * (3 + MCH))

                def down(u):
                    dve.wait_ge(down_done, u.count(1, 1))
                    ring_wait(dve, x_out, u, 1)
                    if skip is None:
                        nc.vector.tensor_scalar(sm[:, u.par, :], Y[u.par][:, :], b2[:, 0:1], None,
                                                ALU.add).then_inc(sum_done, 1)
                    else:
                        nc.vector.scalar_tensor_tensor(out=sm[:, u.par, :], in0=Y[u.par][:, :], scalar=b2[:, 0:1],
                                                       in1=skip[:, u.cols()], op0=ALU.add,
                                                       op1=ALU.add).then_inc(sum_done, 1)
                    dve.wait_ge(sum_done, u.count(1, 1))
                    if out_d is not None:
                        ring_wait(dve, turned, u, 1)
                    for q in range(SPG):
                        here = u.cols(q * SEQ, SEQ)
                        to = xT[:, here] if out_d is None else xo[:, u.par, q * SEQ:(q + 1) * SEQ]
                        last = nc.vector.scalar_tensor_tensor(
                            out=to, in0=sm[:, u.par, q * SEQ:(q + 1) * SEQ], scalar=gate[:, u.seq(q)],
                            in1=xT[:, here], op0=ALU.mult, op1=ALU.add)
                    last.then_inc(x_out, 1)

                def turn(u):
                    dve.wait_ge(turned, u.count(1, 1))
                    if u.at >= 2 or u.loop is not None:
                        dve.wait_ge(stored[u.par], Group(u.at - 2, u.loop, 2).turns(16))
                    nc.vector.tensor_copy(rows[:, u.par].rearrange("p t f -> p (t f)"), R[u.par][:, :]).then_inc(row_out, 1)

                steps = {"down": down}
                if out_d is not None:
                    steps["turn"] = turn
                skewed(dve, order, steps)


class PairSlot:
    UPS = HEADS // 2

    def __init__(self, k, loop=None, tail=False):
        self.k, self.loop = k, loop
        self.tail = tail
        self.lead = NB if tail else 1 if loop is not None else 0

    def has(self, lag):
        u = self.k - lag
        return u >= 0 if self.lead == 0 else u < 0 if self.tail else True

    def was(self, lag):
        return self.lead > 0 or self.k >= lag

    def count(self, per, lag, r):
        here = per * (self.UPS * self.lead + self.k - lag) + r
        return here if self.loop is None else here + self.loop * (self.UPS * per)

    def seqs(self, per, lag, r):
        here = per * (self.lead + (self.k - lag) // self.UPS) + r
        return here if self.loop is None else here + self.loop * per

    def cols(self, lag):
        first = (self.lead + (self.k - lag) // self.UPS) * SEQ
        return slice(first, first + SEQ) if self.loop is None else bass.ds(self.loop * SEQ + first, SEQ)

    def seq(self, lag):
        first = self.lead + (self.k - lag) // self.UPS
        return slice(first, first + 1) if self.loop is None else bass.ds(self.loop + first, 1)

    def pair(self, lag):
        return (self.k - lag) % self.UPS

    def par(self, lag):
        return (self.k - lag) % 2


def multiquery_attention(nc, g, w):
    xT, hT, ident = g.xT, g.yT, g.ident
    SPAN = 384
    with ExitStack() as ctx:
        sb = lambda n, s, d=F32: ctx.enter_context(nc.sbuf_tensor("mq_" + n, s, d))
        ps = lambda n: ctx.enter_context(nc.psum_tensor("mq_" + n, [128, 512], F32))
        sem = phase_semaphores(nc, ctx, "mq_")
        wq = sb("wq", [128, INNER])
        wkk = sb("wkk", [128, 2, HD])
        wv = sb("wv", [128, 2, HD])
        wout = sb("wout", [128, HEADS // 2, D])
        bout = sb("bout", [128, 1])
        emb = sb("emb", [BUCKETS, HEADS])
        hot = sb("hot", [BUCKETS, SPAN])
        ones = sb("ones", [1, HEADS])
        off = sb("off", [1, SPAN])
        swap = sb("swap", [128, 128])
        dist = sb("dist", [HEADS, SPAN])
        hank = sb("hank", [128, HEADS, SEQ])
        bias = sb("bias", [128, HEADS, SPAN])
        qT = sb("qT", [128, 2, SEQ])
        kT = sb("kT", [128, SEQ])
        vT = sb("vT", [128, SEQ])
        vv = sb("vv", [128, 2, HD + 1])
        pb = sb("pb", [128, 2, 2, SPAN])
        nm = sb("nm", [128, 2, 2, 2])
        pT = sb("pT", [128, 2, 2, SPAN])
        rs = sb("rs", [128, 2, 2])
        on = sb("on", [128, 2, 2, 2, HD])
        oT = sb("oT", [128, 2, SEQ])
        yo = sb("yo", [128, SEQ])
        tick = sb("tick", [128, 2])
        SC = [ps("sc0"), ps("sc1")]
        TR = [ps("tr0"), ps("tr1")]
        PV, PQ, PO, PY = ps("pv"), ps("pq"), ps("po"), ps("py")
        names = ("loaded dist_mm dist_out stored spread swapped swap_out pads ones q_done k_out q_out vT_done vT_out v_turned "
                 "v_out score_done max_done exp_done p_turned p_out pv_done rs_done norm_done o_turned o_out "
                 "y_done yo_done x_out").split()
        s = type("Sems", (), {n: sem(n) for n in names})
        NLOAD = 12

        def run(eng, slot):
            for k in range(8):
                slot(PairSlot(k))
            with eng.Fori(0, NB - 1) as loop:
                for k in range(8):
                    slot(PairSlot(k, loop))
            for k in range(5):
                slot(PairSlot(k, tail=True))

        with nc.Block() as block:

            @block.sync
            def _(sp):
                for dst, src in ((emb[:, :], w.rel_emb), (hot[:, :], w.c_hot), (off[:, :], w.c_off), (swap[:, :], w.c_swap),
                                 (wq[:, :], w.Wq), (wkk[:, 0, :], w.Wkv[:, 0:HD]), (wkk[:, 1, :], w.Wkv[:, 0:HD]),
                                 (wv[:, 0, :], w.Wkv[:, HD:2 * HD]), (wv[:, 1, :], w.Wkv[:, HD:2 * HD]),
                                 (wout[:, :, :], w.Wout.rearrange("(j p) n -> p j n", p=128)),
                                 (bout[:, :], w.bout.unsqueeze(1)), (ones[:, :], w.c_ones)):
                    sp.dma_start(dst, src).then_inc(s.loaded, 16)
                sp.wait_ge(s.dist_out, 1)
                sp.dma_start(w.scratch, dist[:, :]).then_inc(s.stored, 16)
                sp.wait_ge(s.stored, 16)
                src = w.scratch[:, 0:SEQ].unsqueeze(0)
                sp.dma_start(hank[:, :, :], bass.AP(tensor=w.scratch.tensor, offset=0,
                                                    ap=[[1, 128], [SPAN, HEADS], [1, SEQ]])).then_inc(s.spread, 16)

            @block.tensor
            def _(pe):
                pe.wait_ge(s.loaded, 16 * NLOAD)
                nc.tensor.matmul(PY[0:HEADS, 0:SPAN], emb[:, :], hot[:, :], start=True, stop=False)
                nc.tensor.matmul(PY[0:HEADS, 0:SPAN], ones[:, :], off[:, :], start=False, stop=True).then_inc(s.dist_mm, 1)
                pe.wait_ge(s.spread, 16)
                for n in range(HEADS // 2):
                    if n >= 2:
                        pe.wait_ge(s.swap_out, n - 1)
                    nc.tensor.matmul(SC[n % 2][:, :], swap[:, :], hank[:, 2 * n:2 * n + 2, :].rearrange(
                        "p a b -> p (a b)"), start=True, stop=True).then_inc(s.swapped, 1)
                pe.wait_ge(s.swap_out, HEADS // 2)
                pe.wait_ge(s.ones, 1)

                def slot(u):
                    if u.has(0):
                        if u.was(1):
                            pe.wait_ge(s.q_out, u.count(1, 1, 1))
                        if u.k == 0:
                            nc.tensor.matmul(PQ[:, SEQ:2 * SEQ], wkk[:, :, :].rearrange("p a b -> p (a b)"),
                                             hT[:, u.cols(0)], start=True, stop=True)
                        elif u.k == 1:
                            pe.wait_ge(s.k_out, u.seqs(1, 1, 1))
                        nc.tensor.matmul(PQ[:, 0:SEQ], wq[:, u.k * 128:(u.k + 1) * 128], hT[:, u.cols(0)],
                                         start=True, stop=True).then_inc(s.q_done, 1)
                    if u.has(1):
                        pe.wait_ge(s.q_out, u.count(1, 1, 1))
                        if u.k == 1:
                            pe.wait_ge(s.k_out, u.seqs(1, 1, 1))
                        for e in range(2):
                            if u.was(2):
                                pe.wait_ge(s.max_done, u.count(2, 2, e + 1))
                            r = slice(64 * e, 64 * e + 64)
                            nc.tensor.matmul(SC[e][:, 0:128], qT[r, u.par(1), 0:128], kT[r, 0:128], start=True, stop=True)
                            nc.tensor.matmul(SC[e][:, 128:384], qT[r, u.par(1), 128:256], kT[r, :], start=True,
                                             stop=True).then_inc(s.score_done, 1)
                    if u.has(2):
                        for e in range(2):
                            pe.wait_ge(s.exp_done, u.count(2, 2, e + 1))
                            if u.was(3):
                                pe.wait_ge(s.p_out, u.count(2, 3, e + 1))
                            for c in range(3):
                                last = nc.tensor.transpose(TR[e][:, c * 128:(c + 1) * 128],
                                                           pb[:, u.par(2), e, c * 128:(c + 1) * 128], ident[:, :])
                            last.then_inc(s.p_turned, 1)
                    if u.has(3):
                        if u.k == 3:
                            pe.wait_ge(s.v_out, u.seqs(1, 3, 1))
                        if u.was(4):
                            pe.wait_ge(s.norm_done, u.count(1, 4, 1))
                        for e in range(2):
                            pe.wait_ge(s.p_out, u.count(2, 3, e + 1))
                            p = pT[:, u.par(3), e, :]
                            o = [(2 * e + t) * (HD + 1) for t in range(2)]
                            nc.tensor.matmul(PV[:, o[0]:o[0] + HD + 1], p[:, 0:128], vv[:, 0, :], start=True, stop=True)
                            nc.tensor.matmul(PV[:, o[1]:o[1] + HD + 1], p[:, 128:256], vv[:, 0, :], start=True, stop=False)
                            last = nc.tensor.matmul(PV[:, o[1]:o[1] + HD + 1], p[:, 256:384], vv[:, 1, :], start=False, stop=True)
                        last.then_inc(s.pv_done, 1)
                    if u.k == 0 and u.has(0):
                        if u.was(5):
                            pe.wait_ge(s.o_out, u.count(1, 5, 1))
                        nc.tensor.matmul(PO[:, SEQ:2 * SEQ], wv[:, :, :].rearrange("p a b -> p (a b)"), hT[:, u.cols(0)], start=True,
                                         stop=True).then_inc(s.vT_done, 1)
                    if u.k == 2 and u.has(2) and not u.tail:
                        pe.wait_ge(s.vT_out, u.seqs(1, 2, 1))
                        if u.was(5):
                            pe.wait_ge(s.o_out, u.count(1, 5, 1))
                        for t in range(2):
                            last = nc.tensor.transpose(PO[:, SEQ + t * 128:SEQ + (t + 1) * 128], vT[:, t * 128:(t + 1) * 128],
                                                       ident[:, :])
                        last.then_inc(s.v_turned, 1)
                    if u.has(4):
                        pe.wait_ge(s.norm_done, u.count(1, 4, 1))
                        if u.was(5):
                            pe.wait_ge(s.o_out, u.count(1, 5, 1))
                        if u.k == 0 and not u.tail:
                            pe.wait_ge(s.vT_out, u.seqs(1, 0, 1))
                        if u.k in (2, 4) and not u.tail:
                            pe.wait_ge(s.v_out, u.seqs(1, u.k, 1))
                        for t in range(2):
                            last = nc.tensor.transpose(PO[:, t * 128:(t + 1) * 128], on[:, u.par(4), t, :, :].rearrange(
                                "p e d -> p (e d)"), ident[:, :])
                        last.then_inc(s.o_turned, 1)
                    if u.has(5):
                        j = u.pair(5)
                        pe.wait_ge(s.o_out, u.count(1, 5, 1))
                        if j == 0 and not (u.lead == 0):
                            pe.wait_ge(s.yo_done, u.seqs(1, 5, 0))
                        last = nc.tensor.matmul(PY[:, 0:SEQ], wout[:, j, :], oT[:, u.par(5), :], start=(j == 0), stop=(j == 7))
                        last.then_inc(s.y_done, 1)

                run(pe, slot)

            @block.scalar
            def _(act):
                act.wait_ge(s.dist_mm, 1)
                nc.scalar.activation(dist[:, :], PY[0:HEADS, 0:SPAN], ACT.Copy).then_inc(s.dist_out, 1)

                def slot(u):
                    if u.has(0):
                        act.wait_ge(s.q_done, u.count(1, 0, 1))
                        if u.was(2):
                            act.wait_ge(s.score_done, u.count(2, 2, 2))
                        nc.scalar.activation(qT[:, u.par(0), :], PQ[:, 0:SEQ], ACT.Copy,
                                             scale=-HD ** -0.5).then_inc(s.q_out, 1)
                        if u.k == 0:
                            if u.was(1):
                                act.wait_ge(s.score_done, u.count(2, 1, 2))
                            nc.scalar.activation(kT[:, :], PQ[:, SEQ:2 * SEQ], ACT.Copy).then_inc(s.k_out, 1)
                    if u.has(1):
                        for e in range(2):
                            for t in range(2):
                                c = slice(0, 128) if t == 0 else slice(128, 384)
                                act.wait_ge(s.max_done, u.count(2, 1, e + 1))
                                last = nc.scalar.activation(pb[:, u.par(1), e, c], pb[:, u.par(1), e, c], ACT.Exp,
                                                            bias=nm[:, u.par(1), e, t:t + 1], scale=-1.0)
                            last.then_inc(s.exp_done, 1)
                    if u.has(2):
                        for e in range(2):
                            act.wait_ge(s.p_turned, u.count(2, 2, e + 1))
                            if u.was(4):
                                act.wait_ge(s.pv_done, u.count(1, 4, 1))
                            nc.scalar.activation(pT[:, u.par(2), e, :], TR[e][:, 0:SPAN], ACT.Copy).then_inc(s.p_out, 1)
                    if u.k == 0 and u.has(0):
                        act.wait_ge(s.vT_done, u.seqs(1, 0, 1))
                        nc.scalar.activation(vT[:, :], PO[:, SEQ:2 * SEQ], ACT.Copy).then_inc(s.vT_out, 1)
                    if u.k == 2 and not u.tail:
                        act.wait_ge(s.v_turned, u.seqs(1, 2, 1))
                        if u.was(3):
                            act.wait_ge(s.pv_done, u.count(1, 3, 1))
                        nc.scalar.activation(vv[:, :, 0:HD], PO[:, SEQ:2 * SEQ].rearrange(
                            "p (t d) -> p t d", t=2)[:, :, 0:HD], ACT.Copy).then_inc(s.v_out, 1)
                    if u.has(4):
                        act.wait_ge(s.o_turned, u.count(1, 4, 1))
                        if u.was(6):
                            act.wait_ge(s.y_done, u.count(1, 6, 1))
                        nc.scalar.activation(oT[:, u.par(4), :], PO[:, 0:SEQ], ACT.Copy).then_inc(s.o_out, 1)

                run(act, slot)

            @block.vector
            def _(dve):
                nc.vector.memset(vv[:, :, HD:HD + 1], 1.0).then_inc(s.ones, 1)
                for n in range(HEADS // 2):
                    dve.wait_ge(s.swapped, n + 1)
                    two = SC[n % 2][:, :].rearrange("p (a b) -> p a b", a=2)
                    nc.vector.tensor_copy(bias[:, 2 * n:2 * n + 2, 0:128], two[:, :, 128:256])
                    nc.vector.tensor_copy(bias[:, 2 * n:2 * n + 2, 128:384], two).then_inc(s.swap_out, 1)
                dve.wait_ge(s.swap_out, HEADS // 2)

                def slot(u):
                    if u.has(1):
                        for e in range(2):
                            h = 2 * u.pair(1) + e
                            dve.wait_ge(s.score_done, u.count(2, 1, e + 1))
                            if u.was(3):
                                dve.wait_ge(s.p_turned, u.count(2, 3, e + 1))
                            nc.vector.memset(tick[:, e:e + 1], 0.0)
                            for t in range(2):
                                c = slice(0, 128) if t == 0 else slice(128, 384)
                                last = nc.vector.tensor_tensor_reduce(
                                    out=pb[:, u.par(1), e, c], in0=SC[e][:, c], in1=bias[:, h, c], scale=1.0,
                                    scalar=3e38, op0=ALU.add, op1=ALU.min, accum_out=nm[:, u.par(1), e, t:t + 1])
                            last.then_inc(s.max_done, 1)
                    if u.has(3):
                        ov = PV[:, 0:4 * (HD + 1)].rearrange("p (e t d) -> p e t d", e=2, t=2)
                        dve.wait_ge(s.pv_done, u.count(1, 3, 1))
                        nc.vector.reciprocal(rs[:, :, :], ov[:, :, :, HD]).then_inc(s.rs_done, 1)
                        dve.wait_ge(s.rs_done, u.count(1, 3, 1))
                        if u.was(5):
                            dve.wait_ge(s.o_turned, u.count(1, 5, 1))
                        nc.vector.tensor_tensor(on[:, u.par(3)].rearrange("p t e d -> p e t d"), ov[:, :, :, 0:HD],
                                                rs[:, :, :].unsqueeze(3).broadcast_to((128, 2, 2, HD)),
                                                ALU.mult).then_inc(s.norm_done, 1)
                    if u.has(5) and u.pair(5) == 7:
                        dve.wait_ge(s.y_done, u.count(1, 5, 1))
                        nc.vector.tensor_scalar(yo[:, :], PY[:, 0:SEQ], bout[:, 0:1], w.gate[:, u.seq(5)], ALU.add,
                                                ALU.mult).then_inc(s.yo_done, 1)
                        dve.wait_ge(s.yo_done, u.seqs(1, 5, 1))
                        nc.vector.tensor_tensor(xT[:, u.cols(5)], xT[:, u.cols(5)], yo[:, :], ALU.add).then_inc(s.x_out, 1)

                run(dve, slot)


def modulation(nc, g, w):
    with ExitStack() as ctx:
        sb = lambda n, s, d=F32: ctx.enter_context(nc.sbuf_tensor("md_" + n, s, d))
        sem = phase_semaphores(nc, ctx, "md_")
        c = sb("c", [NB, 2, D])
        e = sb("e", [NB, 2, D])
        cT = sb("cT", [128, 2, NB])
        wm = sb("wm", [128, 2, 6 * D])
        raw = sb("raw", [128, 2, 6, NB])
        sg = sb("sg", [128, 2, 2, NB])
        pc = ctx.enter_context(nc.psum_tensor("md_pc", [128, 512], F32))
        pm = ctx.enter_context(nc.psum_tensor("md_pm", [128, 512], F32))
        names = "loaded exp_done plus inv silu turned cT_out mod_done raw_out sign mag ready consts bf".split()
        s = type("Sems", (), {n: sem(n) for n in names})
        with nc.Block() as block:

            @block.sync
            def _(sp):
                for l in range(2):
                    sp.dma_start(c[:, l, :], w.c[l]).then_inc(s.loaded, 16)
                    sp.dma_start(wm[:, l, :], w.wmod[l]).then_inc(s.loaded, 16)
                sp.dma_start(g.ident[:, :], w.c_ident).then_inc(s.loaded, 16)
                sp.dma_start(g.band[:, :, :], w.c_band.rearrange("t p k -> p t k")).then_inc(s.loaded, 16)
                sp.dma_start(g.cbase[:, :, :, :], w.c_cbase.rearrange("t p j d -> p t j d")).then_inc(s.loaded, 16)
                sp.dma_start(g.sbase[:, :, :, :], w.c_sbase.rearrange("t p j d -> p t j d")).then_inc(s.loaded, 16)

            @block.scalar
            def _(act):
                act.wait_ge(s.loaded, 128)
                nc.scalar.activation(e[:, :, :], c[:, :, :], ACT.Exp, scale=-1.0).then_inc(s.exp_done, 1)

            @block.vector
            def _(dve):
                nc.vector.memset(g.mhalf[:, :], -0.5)
                nc.vector.memset(g.zero, 0.0)
                nc.vector.memset(g.eps[:, :], EPS).then_inc(s.consts, 1)
                dve.wait_ge(s.loaded, 128)
                nc.vector.tensor_copy(g.identb[:, :], g.ident[:, :])
                nc.vector.tensor_copy(g.maskb[:, :, :, :], g.band[:, :, :].unsqueeze(2).broadcast_to(
                    (128, 2, HEADS // 4, KEYS))).then_inc(s.bf, 1)
                dve.wait_ge(s.exp_done, 1)
                nc.vector.tensor_scalar(e[:, :, :], e[:, :, :], 1.0, None, ALU.add).then_inc(s.plus, 1)
                dve.wait_ge(s.plus, 1)
                nc.vector.reciprocal(e[:, :, :], e[:, :, :]).then_inc(s.inv, 1)
                dve.wait_ge(s.inv, 1)
                nc.vector.tensor_tensor(c[:, :, :], c[:, :, :], e[:, :, :], ALU.mult).then_inc(s.silu, 1)
                dve.wait_ge(s.turned, 1)
                nc.vector.tensor_copy(cT[:, :, :], pc[:, 0:2 * NB].rearrange("p (l b) -> p l b", l=2)).then_inc(s.cT_out, 1)
                dve.wait_ge(s.mod_done, 1)
                nc.vector.tensor_copy(raw[:, :, :, :], pm[:, 0:12 * NB].rearrange(
                    "p (l j b) -> p l j b", l=2, j=6)).then_inc(s.raw_out, 1)
                dve.wait_ge(s.raw_out, 1)
                nc.vector.tensor_copy(g.mod[:, :, 0::3, :], raw[:, :, 0::3, :])
                nc.vector.tensor_scalar(g.mod[:, :, 1::3, :], raw[:, :, 1::3, :], 1.0, None, ALU.add)
                nc.vector.tensor_scalar(sg[:, :, :, :], raw[:, :, 2::3, :], 0.0, 2.0, ALU.is_ge, ALU.mult).then_inc(s.sign, 1)
                nc.vector.tensor_scalar(g.mod[:, :, 2::3, :], raw[:, :, 2::3, :], -1.0, None, ALU.mult).then_inc(s.mag, 1)
                dve.wait_ge(s.mag, 1)
                nc.vector.tensor_tensor(raw[:, :, 2::3, :], raw[:, :, 2::3, :], g.mod[:, :, 2::3, :], ALU.max).then_inc(s.mag, 1)
                dve.wait_ge(s.mag, 2)
                nc.vector.tensor_scalar(raw[:, :, 2::3, :], raw[:, :, 2::3, :], 0.25, None, ALU.max).then_inc(s.mag, 1)
                dve.wait_ge(s.sign, 1)
                nc.vector.tensor_scalar(sg[:, :, :, :], sg[:, :, :, :], -1.0, None, ALU.add).then_inc(s.sign, 1)
                dve.wait_ge(s.sign, 2)
                dve.wait_ge(s.mag, 3)
                nc.vector.tensor_tensor(g.mod[:, :, 2::3, :], raw[:, :, 2::3, :], sg[:, :, :, :], ALU.mult).then_inc(s.ready, 1)

            @block.tensor
            def _(pe):
                pe.wait_ge(s.silu, 1)
                for l in range(2):
                    last = nc.tensor.transpose(pc[:, l * NB:(l + 1) * NB], c[:, l, :], g.ident[0:NB, 0:NB])
                last.then_inc(s.turned, 1)
                pe.wait_ge(s.cT_out, 1)
                for l in range(2):
                    for j in range(6):
                        at = (l * 6 + j) * NB
                        last = nc.tensor.matmul(pm[:, at:at + NB], wm[:, l, j * D:(j + 1) * D], cT[:, l, :], start=True, stop=True)
                last.then_inc(s.mod_done, 1)


def build(nc, a, out):
    with ExitStack() as ctx:
        sb = lambda n, s, d=F32: ctx.enter_context(nc.sbuf_tensor(n, s, d))
        g = type("Shared", (), dict(
            xT=sb("xT", [128, TOK]), yT=sb("yT", [128, TOK]),
            ident=sb("ident", [128, 128]), identb=sb("identb", [128, 128], BF16),
            band=sb("band", [128, 2, KEYS]), maskb=sb("maskb", [128, 2, HEADS // 4, KEYS], BF16),
            cbase=sb("cbase", [128, 2, 2, HD]), sbase=sb("sbase", [128, 2, 2, HD]),
            zero=sb("zero", [128, 1])[:, :], mhalf=sb("mhalf", [128, HEADS]), eps=sb("eps", [128, HEADS]), mod=sb("mod", [128, 2, 6, NB])))
        sems = lambda p, names: type("Sems", (), {n: nc.alloc_semaphore(p + n) for n in names})
        g.wa_sems = sems("wa_", WA_SEMS)
        g.gm_sems = sems("gm_", GM_SEMS)
        pick = lambda prefix, **more: type("Weights", (), {
            **{k[len(prefix):]: v for k, v in a.items() if k.startswith(prefix)},
            **{k: v for k, v in a.items() if k.startswith("c_")}, **more})
        modulation(nc, g, pick("none", c=[a["L0_c"], a["L1_c"]], wmod=[a["L0_wmod"], a["L1_wmod"]]))
        mod = lambda l, j: g.mod[:, l, j, :]
        layernorm_modulate(nc, "n0_", g, g.yT, mod(0, 1), mod(0, 0), from_dram=a["L0_attn_x"])
        w = pick("L0_attn_")
        with nc.sbuf_tensor("aT", [128, TOK], F32) as g.aT:
            linear_attention(nc, g, w)
            plain_mlp(nc, "m0_", g, g.aT, w.W1, w.b1, w.W2, w.b2, mod(0, 2), skip=g.yT)
        layernorm_modulate(nc, "n1_", g, g.yT, mod(0, 4), mod(0, 3))
        w = pick("L0_ffn_")
        with ExitStack() as loop_ctx:
            g.lw = layer_weights(nc, loop_ctx)
            first_attention_weights(nc, g, w)
            with nc.Fori(0, DEPTH) as layer:
                window_attention(nc, layer, g, w)
                gated_mlp(nc, layer, g, w)
        gated_residual(nc, g, mod(0, 5))
        layernorm_modulate(nc, "n2_", g, g.yT, mod(1, 1), mod(1, 0))
        w = pick("L1_attn_", gate=mod(1, 2), scratch=nc.dram_tensor("bias_by_distance", (HEADS, 384), F32, kind="Internal").ap())
        multiquery_attention(nc, g, w)
        layernorm_modulate(nc, "n3_", g, g.yT, mod(1, 4), mod(1, 3))
        w = pick("L1_ffn_")
        plain_mlp(nc, "m1_", g, g.yT, w.w1, w.b1, w.w2, w.b2, mod(1, 5), out_d=out)


def gated_residual(nc, g, gate):
    done = nc.alloc_semaphore("gr_done")
    with nc.Block() as block:

        @block.vector
        def _(dve):
            with dve.Fori(0, NB) as b:
                cols = bass.ds(b * SEQ, SEQ)
                nc.vector.scalar_tensor_tensor(out=g.xT[:, cols], in0=g.yT[:, cols], scalar=gate[:, bass.ds(b, 1)],
                                               in1=g.xT[:, cols], op0=ALU.mult, op1=ALU.add).then_inc(done, 1)
            dve.wait_ge(done, NB)


def shape_constants():
    import numpy as np
    f = np.float32
    c = {"c_ident": np.eye(128, dtype=f)}
    r, k = np.arange(BLK)[:, None], np.arange(KEYS)[None, :]
    band = np.where((k >= r) & (k <= r + WIN), 0.0, NEG)
    first = np.where(k >= WIN, band, NEG)
    c["c_band"] = np.stack([np.concatenate([first, band]), np.concatenate([band, band])]).astype(f)
    half = np.arange(0, HD, 2, dtype=f)
    inv_freq = f(1) / np.power(f(10000), half / f(HD))
    t = np.arange(SEQ, dtype=f)
    freqs = np.tile(t[:, None] * inv_freq[None, :], (1, 2)).astype(f)
    base_scale = (half + f(0.4 * HD)) / f(1.4 * HD)
    power = (t - f(SEQ // 2)) / f(WIN // 2)
    scale = np.tile(base_scale[None, :] ** power[:, None], (1, 2)).astype(f)
    cos, sin = np.cos(freqs), np.sin(freqs) * np.where(np.arange(HD) < HD // 2, f(-1), f(1))
    c["c_cbase"] = np.stack([cos * scale * 8, cos / scale], 1).reshape(2, 128, 2, HD).astype(f)
    c["c_sbase"] = np.stack([sin * scale * 8, sin / scale], 1).reshape(2, 128, 2, HD).astype(f)
    p = np.arange(128)
    sel = (p[:, None] // LIN_HD == np.arange(HEADS)[None, :]).astype(f)
    c["c_hsel"], c["c_hselT"] = sel, np.ascontiguousarray(sel.T)
    c["c_hprobe"] = (sel / (SEQ * np.sqrt(LIN_HD))).astype(f)
    c["c_hmask"] = (p[:, None] // LIN_HD == p[None, :] // LIN_HD).astype(f)
    n = SEQ - 1 - np.arange(384)
    exact = BUCKETS // 2
    safe = np.maximum(n, 1).astype(f)
    large = exact + (np.log(safe / exact) / np.log(128 / exact) * (BUCKETS - exact)).astype(np.int32)
    bucket = np.where(n < exact, np.maximum(n, 0), np.minimum(large, BUCKETS - 1))
    hot = (np.arange(BUCKETS)[:, None] == bucket[None, :]) & (n >= 0)[None, :]
    c["c_hot"] = (hot * HD ** 0.5).astype(f)
    c["c_off"] = np.where(n < 0, NEG, 0.0)[None, :].astype(f)
    c["c_ones"] = np.ones((1, HEADS), f)
    c["c_swap"] = np.ascontiguousarray(-np.eye(128, dtype=f)[::-1])
    return c


def kernel(**inputs):
    import numpy as np
    import concourse.bacc as bacc
    from concourse.bass_utils import run_bass_kernel_spmd

    nc = bacc.Bacc("TRN2", target_bir_lowering=False, num_devices=1)
    arrays = {k: np.ascontiguousarray(v) for k, v in inputs.items()}
    arrays.update(shape_constants())
    a = {k: nc.dram_tensor(k, v.shape, mybir.dt.from_np(v.dtype), kind="ExternalInput").ap() for k, v in arrays.items()}
    out = nc.dram_tensor("out", (NB, SEQ, D), F32, kind="ExternalOutput").ap()
    build(nc, a, out)
    return run_bass_kernel_spmd(nc, [arrays], core_ids=[0]).results[0]["out"]
```

```python
import concourse.bass as bass
from concourse import mybir
from contextlib import ExitStack

F32 = mybir.dt.float32
BF16 = mybir.dt.bfloat16
F32R = mybir.dt.float32r
ALU = mybir.AluOpType
ACT = mybir.ActivationFunctionType
AX = mybir.AxisListType

D = 128
NB = 16
SEQ = 256
TOK = NB * SEQ
GRP = 512
NGRP = TOK // GRP
SPG = GRP // SEQ
TPG = GRP // D
HEADS = 16
HD = 64
INNER = HEADS * HD
DEPTH = 6
LIN_HD = D // HEADS
MLP = 512
MCH = MLP // D
GLU = int(D * 4 * 2 / 3)
GCH = 3
GW = -(-GLU // GCH)
WIN = 32
BLK = 2 * WIN
KEYS = BLK + WIN
EPS = 1e-5
NEG = -1e30
BUCKETS = 32


def glu_rows(j):
    return min(GW, GLU - j * GW)


def three_passes(nc, out, lhs, rhs, start=True, stop=True):
    nc.tensor.matmul(out, lhs[0], rhs[0], start=start, stop=False)
    nc.tensor.matmul(out, lhs[0], rhs[1], start=False, stop=False)
    return nc.tensor.matmul(out, lhs[1], rhs[0], start=False, stop=stop)


def phase_semaphores(nc, ctx, tag):
    made = []

    def sem(name):
        made.append(nc.alloc_semaphore(tag + name))
        return made[-1]

    def finish():
        nc.clear_and_free_semaphores(made)
        nc.all_engine_barrier()

    ctx.callback(finish)
    return sem


def window_attention(nc, layer, g, w):
    yT, ident, identb, maskb = g.yT, g.ident, g.identb, g.maskb
    HG = HEADS // 2
    PR = HG // 2
    UPS = 4
    UPL = UPS * NB
    with ExitStack() as ctx:
        sb = lambda n, s, d=F32: ctx.enter_context(nc.sbuf_tensor("wa_" + n, s, d))
        ps = lambda n: ctx.enter_context(nc.psum_tensor("wa_" + n, [128, 512], F32))
        s = g.wa_sems
        v_ready = [s.v_ready0, s.v_ready1]
        wqkv = g.lw.wqkv
        scb = g.lw.scb
        xs = g.lw.xs
        wo = sb("wo", [128, HEADS // 2, D])
        ctab = sb("ctab", [128, 2, 2, HD])
        stab = sb("stab", [128, 2, 2, HD])
        xp = [sb(f"x{n}", [128, SEQ], F32R) for n in ("high", "low")]
        sq = sb("sq", [128, 2 * HG, HD])
        t1 = sb("t1", [128, 2, 2, HG, HD])
        t2 = sb("t2", [128, 2, 2, HG, HD])
        ss = sb("ss", [128, 2, 2 * HG])
        rn = sb("rn", [128, 2, 2 * HG])
        qT = sb("qT", [128, 2, PR, 128])
        kT = sb("kT", [128, 2, PR, WIN + SEQ])
        vt = sb("vt", [128, 2, HG, HD])
        vv = sb("vv", [128, UPS, 2, HG, HD])
        pb = sb("pb", [128, 2, 2, PR, KEYS])
        pT = sb("pT", [128, 2, 2, PR, 128])
        nm = sb("nm", [128, 2, 2, PR])
        sm = sb("sm", [128, 2, 2, PR])
        rs = sb("rs", [128, 2, PR])
        oT = sb("oT", [128, 2, HEADS // 2, 128])
        PJ = [ps("pj0"), ps("pj1")]
        TR = [ps("tr0"), ps("tr1")]
        SC = [ps("sc0"), ps("sc1")]
        VB, OB = ps("vb"), ps("ob")

        class Slot:

            def __init__(self, k, lead, loop=None):
                self.k, self.lead, self.loop, self.tail = k, lead, loop, lead == NB

            def was(self, lag):
                return UPS * self.lead + self.k >= lag

            def has(self, lag):
                return self.was(lag) and (not self.tail or self.k < lag)

            def count(self, per, lag, r):
                here = layer * (UPL * per) + (per * (UPS * self.lead + self.k - lag) + r)
                return here if self.loop is None else here + self.loop * (UPS * per)

            def tiles(self, lag, r):
                here = layer * (UPL // 2) + (2 * self.lead + (self.k - lag) // 2 + r)
                return here if self.loop is None else here + self.loop * 2

            def splits(self, seq, r):
                here = layer * (2 * NB) + (2 * seq + r)
                return here if self.loop is None else here + self.loop * 2

            def values(self, lag):
                seq, k = divmod(UPS * self.lead + self.k - lag, UPS)
                here = layer * (16 * 5 * NB) + 16 * (5 * seq + (3 if k < 2 else 5))
                return here if self.loop is None else here + self.loop * (16 * 5)

            def par(self, lag):
                return (self.k - lag) % 2

            def tile(self, lag):
                return (self.k - lag) % UPS // 2

            def half(self, lag):
                return (self.k - lag) % 2

        def run(eng, slot):
            for k in range(UPS):
                slot(Slot(k, 0))
            for k in range(UPS):
                slot(Slot(k, 1))
            with eng.Fori(0, NB - 3) as loop:
                for k in range(UPS):
                    slot(Slot(k, 2, loop))
            for k in range(UPS):
                slot(Slot(k, NB - 1))
            for k in range(4):
                slot(Slot(k, NB))

        with nc.Block() as block:

            @block.sync
            def _(sp):
                sp.dma_start(wo[:, :, :], w.Wo[bass.ds(layer, 1)].rearrange(
                    "l (j p) n -> (l p) j n", p=128)).then_inc(s.w_o, 16)
                gated_weights_load(sp, layer, g, w)
                sp.wait_ge(s.pads, layer + 1)

                def slot(u):
                    if not u.has(0):
                        return
                    if u.k == 0 and u.lead < NB - 1:
                        sp.wait_ge(s.split_done, u.splits(u.lead, 2))
                        first = (u.lead + 1) * SEQ
                        shifted_sequence_load(sp, g, first if u.loop is None else u.loop * SEQ + first)
                    sp.wait_ge(s.v_out, u.count(1, 0, 1))
                    tile = vt[:, u.par(0)]
                    sp.dma_start(vv[WIN:KEYS, u.k, 0], tile[0:BLK]).then_inc(v_ready[u.par(0)], 16)
                    sp.dma_start(vv[0:KEYS, u.k, 1], tile[BLK - WIN:2 * BLK]).then_inc(v_ready[u.par(0)], 16)
                    if u.tile(0) == 0:
                        if u.was(2):
                            sp.wait_ge(s.pv_done, u.count(1, 2, 1))
                        sp.dma_start(vv[0:WIN, u.k + 2, 0], tile[2 * BLK - WIN:2 * BLK]).then_inc(
                            v_ready[u.par(0)], 16)

                run(sp, slot)
                sp.wait_ge(s.wo_out, layer * (UPL // 2) + SPG * UPS // 2)
                shifted_group_load(sp, g, Group(0))

            @block.tensor
            def _(pe):
                def transposes(out, src, n, rows=128):
                    for p in range(n):
                        last = nc.tensor.transpose(out[0:rows, p * 128:(p + 1) * 128], src(p), ident[:, :])
                    return last

                def slot(u):
                    T, hg = u.tile(0), u.half(0)
                    if u.has(0):
                        if u.k == 0:
                            pe.wait_ge(s.split_done, u.splits(u.lead, 2))
                        for j in range(2):
                            if u.was(1):
                                pe.wait_ge(s.rot_done, u.count(2, 1, j + 1))
                            three_passes(nc, PJ[j][:, :], [x[:, T * 128:(T + 1) * 128] for x in xp],
                                         [x[:, j, hg * 512:(hg + 1) * 512] for x in wqkv]).then_inc(s.proj_done, 1)
                    if u.has(3):
                        pe.wait_ge(s.norm_done, u.count(1, 3, 1))
                        if u.has(2):
                            pe.wait_ge(s.qk_out, u.count(2, 2, 2))
                        else:
                            pe.wait_ge(s.pT_out, u.count(2, 4, 2))
                        if u.was(5) and u.k % 2 == 0:
                            pe.wait_ge(s.wo_out, u.tiles(5, 1))
                        for e in range(2):
                            transposes(TR[e], lambda p: pb[:, u.par(3), e, p, :], PR, KEYS).then_inc(s.pT_done, 1)
                    if u.has(4):
                        pe.wait_ge(v_ready[u.par(4)], u.values(4))
                        pe.wait_ge(s.pT_out, u.count(2, 4, 2))
                        if u.was(5):
                            pe.wait_ge(s.oT_out, u.count(1, 5, 1))
                        for p in range(PR):
                            for c in range(2):
                                for e in range(2):
                                    q0 = p * 128 + 64 * c
                                    last = nc.tensor.matmul(OB[64 * e:64 * e + 64, q0:q0 + 64],
                                                            vv[0:KEYS, (u.k - 4) % UPS, c, 2 * p + e, :],
                                                            pT[0:KEYS, u.par(4), e, p, 64 * c:64 * c + 64],
                                                            start=True, stop=True)
                        last.then_inc(s.pv_done, 1)

                    def turn_rotated(j):
                        transposes(TR[1 - j], lambda p: t1[:, u.par(1), j, 2 * p:2 * p + 2, :].rearrange(
                            "p a b -> p (a b)"), PR).then_inc(s.qk_done, 1)

                    if u.has(1):
                        pe.wait_ge(s.qk_ready, u.count(1, 1, 1))
                        for j in (1, 0):
                            if u.was(3):
                                pe.wait_ge(s.pT_out, u.count(2, 3, 2 - j))
                            elif u.was(2):
                                pe.wait_ge(s.qk_out, u.count(2, 2, 2 - j))
                            turn_rotated(j)
                    if u.has(0):
                        if u.was(1):
                            pe.wait_ge(s.v_out, u.count(1, 1, 1))
                        three_passes(nc, VB[:, :], [x[:, T * 128:(T + 1) * 128] for x in xp],
                                     [x[:, 2, hg * 512:(hg + 1) * 512] for x in wqkv]).then_inc(s.proj_done, 1)
                    if u.has(4) and u.k % 2 == 1:
                        pe.wait_ge(s.oT_out, u.count(1, 4, 1))
                        if u.has(1):
                            pe.wait_ge(s.qk_out, u.count(2, 1, 2))
                        else:
                            pe.wait_ge(s.pT_out, u.count(2, 3 if u.has(3) else 4, 2))
                        if u.lead == 1:
                            pe.wait_ge(s.w_o, layer * 16 + 16)
                        for j in range(HEADS // 2):
                            last = nc.tensor.matmul(TR[1][:, 0:128], wo[:, j, :], oT[:, u.tile(4), j, :],
                                                    start=(j == 0), stop=(j == HEADS // 2 - 1))
                        last.then_inc(s.wo_done, 1)
                    if u.has(1):
                        pe.wait_ge(s.qk_out, u.count(2, 1, 2))
                        t, h1 = u.tile(1), u.half(1)
                        for e in range(2):
                            if u.was(2):
                                pe.wait_ge(s.exp_done, u.count(2, 2, e + 1))
                            nc.tensor.matmul(SC[e][:, 0:PR * KEYS], identb[:, :], maskb[:, t, :, :],
                                             start=True, stop=False, skip_group_check=True)
                            for p in range(PR):
                                for c in range(2):
                                    k0 = (2 * t + c) * BLK
                                    last = nc.tensor.matmul(
                                        SC[e][64 * c:64 * c + 64, p * KEYS:(p + 1) * KEYS],
                                        qT[64 * e:64 * e + 64, u.par(1), p, 64 * c:64 * c + 64],
                                        kT[64 * e:64 * e + 64, h1, p, k0:k0 + KEYS],
                                        start=False, stop=True, skip_group_check=True)
                            last.then_inc(s.score_done, 1)

                run(pe, slot)

            @block.scalar
            def _(act):
                def slot(u):
                    def weights(lag, e, pairs):
                        if not u.has(lag):
                            return
                        if pairs[0] == 0:
                            act.wait_ge(s.mx_done, u.count(2, lag, e + 1))
                            if u.was(lag + 2):
                                act.wait_ge(s.pT_done, u.count(2, lag + 2, 2))
                        for p in pairs:
                            last = nc.scalar.activation(
                                pb[:, u.par(lag), e, p, :], SC[e][:, p * KEYS:(p + 1) * KEYS], ACT.Exp,
                                bias=nm[:, u.par(lag), e, p:p + 1], accum_out=sm[:, u.par(lag), e, p:p + 1])
                        if pairs[-1] == PR - 1:
                            last.then_inc(s.exp_done, 1)

                    def turned_out(e):
                        act.wait_ge(s.pT_done, u.count(2, 3, e + 1))
                        if u.was(5):
                            act.wait_ge(s.pv_done, u.count(1, 5, 1))
                        nc.scalar.activation(pT[0:KEYS, u.par(3), e, :, :], TR[e][0:KEYS, :].rearrange(
                            "p (a b) -> p a b", a=PR), ACT.Copy).then_inc(s.pT_out, 1)

                    def squares(j):
                        act.wait_ge(s.proj_done, u.count(3, 0, j + 1))
                        if u.was(1):
                            act.wait_ge(s.ss_done, u.count(1, 1, 1))
                        nc.scalar.activation(sq[:, j * HG:(j + 1) * HG, :], PJ[j][:, :].rearrange(
                            "p (h d) -> p h d", h=HG), ACT.Square).then_inc(s.sq_done, 1)

                    if u.has(0):
                        squares(0)
                        squares(1)
                    if u.has(3):
                        turned_out(0)
                        turned_out(1)
                    weights(2, 1, (0,))
                    if u.has(4):
                        act.wait_ge(s.pv_done, u.count(1, 4, 1))
                        nc.scalar.activation(oT[:, u.tile(4), PR * u.half(4):PR * (u.half(4) + 1), :],
                                             OB[:, :].rearrange("p (a b) -> p a b", a=PR),
                                             ACT.Copy).then_inc(s.oT_out, 1)
                    if u.has(1):
                        act.wait_ge(s.qk_done, u.count(2, 1, 1))
                        if u.was(3):
                            act.wait_ge(s.score_done, u.count(2, 3, 2))
                        k0 = WIN + u.tile(1) * 128
                        nc.scalar.activation(kT[:, u.half(1), :, k0:k0 + 128], TR[0][:, :].rearrange(
                            "p (a b) -> p a b", a=PR), ACT.Copy).then_inc(s.qk_out, 1)
                        act.wait_ge(s.qk_done, u.count(2, 1, 2))
                        nc.scalar.activation(qT[:, u.par(1), :, :], TR[1][:, :].rearrange(
                            "p (a b) -> p a b", a=PR), ACT.Copy).then_inc(s.qk_out, 1)
                    weights(2, 1, (1, 2, 3))
                    if u.has(0):
                        act.wait_ge(s.proj_done, u.count(3, 0, 3))
                        if u.was(2):
                            act.wait_ge(v_ready[u.par(2)], u.values(2))
                        nc.scalar.activation(vt[:, u.par(0), :, :], VB[:, :].rearrange(
                            "p (h d) -> p h d", h=HG), ACT.Copy).then_inc(s.v_out, 1)
                    weights(1, 0, range(PR))

                run(act, slot)

            @block.vector
            def _(dve):
                nc.vector.memset(kT[:, :, :, 0:WIN], 0.0)
                nc.vector.memset(vv[0:WIN, 0:2, 0, :, :], 0.0).then_inc(s.pads, 1)

                def split(loaded, first):
                    dve.wait_ge(s.xs_ready, loaded)
                    nc.vector.tensor_copy(xp[0][:, :], xs[:, :]).then_inc(s.split_done, 1)
                    dve.wait_ge(s.split_done, first)
                    nc.vector.tensor_tensor(xp[1][:, :], xs[:, :], xp[0][:, :].bitcast(F32),
                                            ALU.subtract).then_inc(s.split_done, 1)

                split(layer * (32 * NB) + 32, layer * (2 * NB) + 1)
                for t in range(2):
                    nc.vector.tensor_tensor(ctab[:, t, :, :], g.cbase[:, t, :, :], scb[:, :, :], ALU.mult)
                    nc.vector.tensor_tensor(stab[:, t, :, 0:32], g.sbase[:, t, :, 0:32], scb[:, :, 32:64], ALU.mult)
                    last = nc.vector.tensor_tensor(stab[:, t, :, 32:64], g.sbase[:, t, :, 32:64],
                                                   scb[:, :, 0:32], ALU.mult)
                last.then_inc(s.tables, 1)
                dve.wait_ge(s.tables, layer + 1)

                def slot(u):
                    if u.has(0):
                        b, T = u.par(0), u.tile(0)
                        if u.was(2):
                            dve.wait_ge(s.qk_done, u.count(2, 2, 2))
                        one, two = slice(0, 32), slice(32, 64)

                        def rotate(j):
                            x = PJ[j][:, :].rearrange("p (h d) -> p h d", h=HG)
                            table = lambda t, c: t[:, T, j, c].unsqueeze(1).broadcast_to((128, HG, c.stop - c.start))
                            dve.wait_ge(s.sq_done, u.count(2, 0, j + 1))
                            nc.vector.tensor_tensor(t1[:, b, j], x, table(ctab, slice(0, HD)), ALU.mult)
                            nc.vector.tensor_tensor(t2[:, b, j, :, one], x[:, :, two], table(stab, one), ALU.mult)
                            nc.vector.tensor_tensor(t2[:, b, j, :, two], x[:, :, one], table(stab, two),
                                                    ALU.mult).then_inc(s.rot_done, 1)

                        rotate(0)
                        dve.wait_ge(s.sq_done, u.count(2, 0, 2))
                        if u.was(2):
                            dve.wait_ge(s.rn_done, u.count(1, 2, 1))
                        nc.vector.tensor_reduce(ss[:, b, :], sq[:, :, :], AX.X, ALU.add).then_inc(s.sum_done, 1)
                        dve.wait_ge(s.sum_done, u.count(1, 0, 1))
                        nc.vector.tensor_scalar(ss[:, b, :], ss[:, b, :], 1e-24, None,
                                                ALU.max).then_inc(s.ss_done, 1)
                        rotate(1)
                        dve.wait_ge(s.rot_done, u.count(2, 0, 2))
                        nc.vector.tensor_tensor(t1[:, b, 1], t1[:, b, 1], t2[:, b, 1], ALU.add).then_inc(s.kadd_done, 1)
                    if u.k == UPS - 1 and u.lead < NB - 1:
                        dve.wait_ge(s.proj_done, u.count(3, 0, 3))
                        loaded = layer * (32 * NB) + 32 * (u.lead + 2)
                        split(loaded if u.loop is None else loaded + u.loop * 32, u.splits(u.lead + 1, 1))
                    if u.has(4) and u.k % 2 == 1:
                        dve.wait_ge(s.wo_done, u.tiles(4, 1))
                        c0 = (u.lead + (u.k - 4) // UPS) * SEQ + u.tile(4) * 128
                        col = slice(c0, c0 + 128) if u.loop is None else bass.ds(u.loop * SEQ + c0, 128)
                        nc.vector.tensor_tensor(yT[:, col], TR[1][:, 0:128], yT[:, col],
                                                ALU.add).then_inc(s.wo_out, 1)
                    def largest(e):
                        if u.has(1):
                            dve.wait_ge(s.score_done, u.count(2, 1, e + 1))
                            nc.vector.tensor_reduce(nm[:, u.par(1), e, :], SC[e][:, 0:PR * KEYS].rearrange(
                                "p (a b) -> p a b", a=PR), AX.X, ALU.max, negate=True).then_inc(s.mx_done, 1)

                    largest(0)
                    if u.has(2):
                        b = u.par(2)
                        dve.wait_ge(s.exp_done, u.count(2, 2, 2))
                        nc.vector.reciprocal(rs[:, :, :], sm[:, b]).then_inc(s.rs_done, 1)
                        dve.wait_ge(s.rs_done, u.count(1, 2, 1))
                        weights = pb[:, b].rearrange("p e a k -> p (e a) k")
                        nc.vector.tensor_tensor(weights, weights, rs[:, :, :].rearrange("p e a -> p (e a)").unsqueeze(2)
                                                .broadcast_to((128, HG, KEYS)), ALU.mult).then_inc(s.norm_done, 1)
                    largest(1)

                run(dve, slot)

            @block.gpsimd
            def _(pool):
                def slot(u):
                    if not u.has(0):
                        return
                    b = u.par(0)
                    pool.wait_ge(s.rot_done, u.count(2, 0, 1))
                    nc.gpsimd.tensor_tensor(t1[:, b, 0], t1[:, b, 0], t2[:, b, 0], ALU.add).then_inc(s.radd_done, 1)
                    pool.wait_ge(s.ss_done, u.count(1, 0, 1))
                    if u.was(1):
                        pool.wait_ge(s.qk_ready, u.count(1, 1, 1))
                    nc.gpsimd.tensor_tensor(rn[:, b, :], ss[:, b, :], g.mhalf[:, 0:2 * HG], ALU.pow).then_inc(s.rn_done, 1)
                    pool.wait_ge(s.radd_done, u.count(1, 0, 1))
                    pool.wait_ge(s.kadd_done, u.count(1, 0, 1))
                    pool.wait_ge(s.rn_done, u.count(1, 0, 1))
                    q = t1[:, b].rearrange("p j h d -> p (j h) d")
                    nc.gpsimd.tensor_tensor(q, q, rn[:, b, :].unsqueeze(2).broadcast_to((128, 2 * HG, HD)),
                                            ALU.mult).then_inc(s.qk_ready, 1)

                run(pool, slot)
                pool.wait_ge(s.gated_loaded, layer * (16 * GATED_LOADS) + 16 * GATED_LOADS)
                nc.gpsimd.tensor_tensor(g.lw.w1[0][:, :], g.lw.w1_full[:, :], g.zero.broadcast_to((128, 2 * GLU)),
                                        ALU.add).then_inc(s.w1_high, 1)
                pool.wait_ge(s.w1_high, layer + 1)
                nc.gpsimd.tensor_tensor(g.lw.w1[1][:, :], g.lw.w1_full[:, :], g.lw.w1[0][:, :].bitcast(F32),
                                        ALU.subtract)


WA_SEMS = ("kadd_done", "v_out", "v_ready0", "v_ready1", "w_o", "gated_loaded", "w1_high", "split_done",
           "pads", "tables", "xs_ready", "proj_done", "sq_done", "ss_done", "sum_done", "rn_done", "rot_done",
           "radd_done", "qk_ready", "qk_done", "qk_out", "score_done", "mx_done", "exp_done", "pT_done",
           "pT_out", "pv_done", "rs_done", "norm_done", "oT_out", "wo_done", "wo_out")


class Group:

    def __init__(self, at, loop=None, step=1, base=0):
        self.at, self.loop, self.step, self.base = at, loop, step, base
        self.par = at % 2

    def count(self, per, r, lag=0):
        n = self.base + (per * (self.at - lag) + r)
        return n if self.loop is None else n + self.loop * (per * self.step)

    def has(self, lag):
        return self.loop is not None and self.at >= 1 or self.at >= lag

    def turns(self, per):
        n = per * (self.at // 2 + 1)
        return n if self.loop is None else n + self.loop * per

    def cols(self, start=0, size=GRP):
        if self.loop is None:
            return slice(self.at * GRP + start, self.at * GRP + start + size)
        return bass.ds(self.loop * (GRP * self.step) + (self.at * GRP + start), size)

    def seq(self, q):
        if self.loop is None:
            return slice(self.at * SPG + q, self.at * SPG + q + 1)
        return bass.ds(self.loop * (SPG * self.step) + (self.at * SPG + q), 1)


def skewed(eng, order, steps, n=NGRP):
    deepest = max(lag for _, lag in order)
    head = deepest + 2
    pairs = (n - head) // 2

    def turn(t, loop=None):
        for name, lag in order:
            if name in steps and (loop is not None or 0 <= t - lag < n):
                steps[name](Group(t - lag, loop, 2))

    for t in range(head):
        turn(t)
    with eng.Fori(0, pairs) as loop:
        turn(head, loop)
        turn(head + 1, loop)
    for t in range(head + 2 * pairs, n + deepest):
        turn(t)


def ring_wait(eng, sem, grp, per, lag=2):
    if grp.at >= lag or grp.loop is not None:
        eng.wait_ge(sem, grp.count(per, per, lag))


LN_ORDER = [("front", 0), ("norm", 2), ("stats", 1), ("back", 2)]


def layernorm_modulate(nc, tag, g, dst, scale, bias, from_dram=None):
    with ExitStack() as ctx:
        sb = lambda n, s, d=F32: ctx.enter_context(nc.sbuf_tensor(tag + n, s, d))
        ps = lambda n: ctx.enter_context(nc.psum_tensor(tag + n, [128, GRP], F32))
        sem = phase_semaphores(nc, ctx, tag)
        src = sb("src", [128, 2, TPG, D])
        xn = sb("xn", [128, 2, TPG, D])
        st = sb("st", [128, 2, TPG, 6])
        mv = sb("mv", [128, 2, TPG, 2])
        rstd = sb("rstd", [128, 2, TPG])
        tick = sb("tick", [128, 1])
        TA = [ps("ta0"), ps("ta1")]
        TB = [ps("tb0"), ps("tb1")]
        src_ready = [sem("src_ready0"), sem("src_ready1")]
        turned, stats, aggr, varp, rstd_done, normed, back_done, out_done, x_done = map(sem, (
            "turned", "stats", "aggr", "varp", "rstd_done", "normed", "back_done", "out_done", "x_done"))
        per_src = 16 if from_dram is not None else 1
        with nc.Block() as block:
            if from_dram is not None:
                @block.sync
                def _(sp):
                    tokens = from_dram.rearrange("b (t p) f -> p (b t) f", p=128)

                    def front(u):
                        ring_wait(sp, normed, u, 1)
                        ring_wait(sp, turned, u, 1)
                        t = slice(u.at * TPG, (u.at + 1) * TPG) if u.loop is None else bass.ds(
                            u.loop * (2 * TPG) + u.at * TPG, TPG)
                        sp.dma_start(src[:, u.par], tokens[:, t, :]).then_inc(src_ready[u.par], 16)

                    skewed(sp, LN_ORDER, {"front": front})

            @block.tensor
            def _(pe):
                def front(u):
                    pe.wait_ge(src_ready[u.par], u.turns(per_src))
                    if from_dram is None:
                        ring_wait(pe, normed, u, 1)
                    else:
                        ring_wait(pe, x_done, u, 1)
                    for t in range(TPG):
                        last = nc.tensor.transpose(TA[u.par][:, t * D:(t + 1) * D], src[:, u.par, t, :], g.ident[:, :])
                    last.then_inc(turned, 1)

                def back(u):
                    pe.wait_ge(normed, u.count(1, 1))
                    ring_wait(pe, out_done, u, SPG)
                    for t in range(TPG):
                        last = nc.tensor.transpose(TB[u.par][:, t * D:(t + 1) * D], xn[:, u.par, t, :], g.ident[:, :])
                    last.then_inc(back_done, 1)

                skewed(pe, LN_ORDER, {"front": front, "back": back})

            @block.vector
            def _(dve):
                def rows(u):
                    return src[:, u.par] if from_dram is not None else TA[u.par][:, :].rearrange(
                        "p (t f) -> p t f", t=TPG)

                def stats_of(u):
                    if from_dram is None:
                        dve.wait_ge(turned, u.count(1, 1))
                    else:
                        dve.wait_ge(src_ready[u.par], u.turns(16))
                    for t in range(TPG):
                        last = nc.vector.bn_stats(st[:, u.par, t, :], rows(u)[:, t, :])
                    last.then_inc(stats, 1)
                    dve.wait_ge(stats, u.count(1, 1))
                    nc.vector.memset(tick[:, :], 0.0)
                    for t in range(TPG):
                        last = nc.vector.bn_aggr(mv[:, u.par, t, :], st[:, u.par, t, :])
                    last.then_inc(aggr, 1)

                def norm(u):
                    dve.wait_ge(rstd_done, u.count(1, 1))
                    ring_wait(dve, back_done, u, 1)
                    for t in range(TPG):
                        last = nc.vector.tensor_scalar(xn[:, u.par, t, :], rows(u)[:, t, :], mv[:, u.par, t, 0:1],
                                                       rstd[:, u.par, t:t + 1], ALU.subtract, ALU.mult)
                    last.then_inc(normed, 1)

                skewed(dve, LN_ORDER, {"norm": norm, "stats": stats_of})

            @block.gpsimd
            def _(pool):
                def front(u):
                    pool.wait_ge(aggr, u.count(1, 1))
                    nc.gpsimd.tensor_tensor(rstd[:, u.par, :], mv[:, u.par, :, 1], g.eps[:, 0:TPG], ALU.add).then_inc(varp, 1)
                    pool.wait_ge(varp, u.count(1, 1))
                    nc.gpsimd.tensor_tensor(rstd[:, u.par, :], rstd[:, u.par, :], g.mhalf[:, 0:TPG],
                                            ALU.pow).then_inc(rstd_done, 1)

                skewed(pool, LN_ORDER, {"stats": front})

            @block.scalar
            def _(act):
                def front(u):
                    if from_dram is None:
                        ring_wait(act, turned, u, 1)
                        nc.scalar.activation(src[:, u.par].rearrange("p t f -> p (t f)"), g.xT[:, u.cols()],
                                             ACT.Copy).then_inc(src_ready[u.par], 1)
                    else:
                        act.wait_ge(turned, u.count(1, 1))
                        nc.scalar.activation(g.xT[:, u.cols()], TA[u.par][:, :], ACT.Copy).then_inc(x_done, 1)

                def back(u):
                    act.wait_ge(back_done, u.count(1, 1))
                    for q in range(SPG):
                        nc.scalar.activation(dst[:, u.cols(q * SEQ, SEQ)], TB[u.par][:, q * SEQ:(q + 1) * SEQ],
                                             ACT.Identity, bias=bias[:, u.seq(q)],
                                             scale=scale[:, u.seq(q)]).then_inc(out_done, 1)

                skewed(act, LN_ORDER, {"front": front, "back": back})


GATED_LOADS = 4 + 3 * GCH


def layer_weights(nc, ctx):
    sb = lambda n, s, d=F32: ctx.enter_context(nc.sbuf_tensor("lw_" + n, s, d))
    parts = ("high", "low")
    return type("LayerWeights", (), dict(
        wqkv_full=sb("wqkv", [128, 3, INNER]), wqkv=[sb("wqkv_" + n, [128, 3, INNER], F32R) for n in parts],
        scb=sb("scb", [128, 2, HD]),
        xs=sb("xs", [128, SEQ]),
        fs=sb("fs", [128, GRP]),
        w1_full=sb("w1", [128, 2 * GLU]), w1=[sb("w1_" + n, [128, 2 * GLU], F32R) for n in parts],
        w2=sb("w2", [128, GCH, D]), b1=sb("b1", [128, 2, GCH]),
        vec=sb("vec", [128, 3])))


def shifted_sequence_load(sp, g, first):
    xs, loaded = g.lw.xs, g.wa_sems.xs_ready
    sp.dma_start(xs[0:64, :], g.yT[0:64, bass.ds(first, SEQ)]).then_inc(loaded, 16)
    sp.dma_start(xs[64:128, 1:SEQ], g.yT[64:128, bass.ds(first, SEQ - 1)]).then_inc(loaded, 16)


def shifted_group_load(sp, g, u):
    fs, loaded = g.lw.fs, g.gm_sems.fs_ready
    sp.dma_start(fs[0:64, :], g.yT[0:64, u.cols()]).then_inc(loaded, 16)
    for q in range(SPG):
        sp.dma_start(fs[64:128, q * SEQ + 1:(q + 1) * SEQ], g.yT[64:128, u.cols(q * SEQ, SEQ - 1)]).then_inc(loaded, 16)


def attention_weights_load(sp, layer, g, w, loaded):
    lw = g.lw
    sp.dma_start(lw.wqkv_full[:, :, :], w.Wqkv[bass.ds(layer, 1)].rearrange(
        "l p (t n) -> (l p) t n", t=3)).then_inc(loaded, 16)
    for n, v in enumerate((w.q_scale, w.k_scale)):
        sp.dma_start(lw.scb[:, n, :], v[bass.ds(layer, 1)].broadcast_to((128, HD))).then_inc(loaded, 16)


def gated_weights_load(sp, layer, g, w):
    lw, loaded = g.lw, g.wa_sems.gated_loaded
    sp.dma_start(lw.w1_full[:, :], w.W1[bass.ds(layer, 1)].rearrange("l p n -> (l p) n")).then_inc(loaded, 16)
    for j in range(GCH):
        r = glu_rows(j)
        sp.dma_start(lw.w2[0:r, j, :], w.W2[bass.ds(layer, 1), j * GW:j * GW + r, :].rearrange(
            "l p n -> (l p) n")).then_inc(loaded, 16)
        for a in range(2):
            c0 = a * GLU + j * GW
            sp.dma_start(lw.b1[0:r, a, j:j + 1], w.b1[bass.ds(layer, 1), c0:c0 + r].rearrange(
                "l p -> p l")).then_inc(loaded, 16)
    for n, v in enumerate((w.ln_g, w.ln_b, w.b2)):
        sp.dma_start(lw.vec[:, n:n + 1], v[bass.ds(layer, 1), :].rearrange("l p -> p l")).then_inc(loaded, 16)


def first_attention_weights(nc, g, w):
    with ExitStack() as ctx:
        sem = phase_semaphores(nc, ctx, "fw_")
        loaded, high, pads = sem("loaded"), sem("high"), sem("pads")
        with nc.Block() as block:

            @block.sync
            def _(sp):
                attention_weights_load(sp, 0, g, w, loaded)
                sp.wait_ge(pads, 1)
                shifted_sequence_load(sp, g, 0)

            @block.vector
            def _(dve):
                nc.vector.memset(g.lw.xs[:, 0:1], 0.0)
                nc.vector.memset(g.lw.fs[:, :], 0.0).then_inc(pads, 1)
                full, (hi, lo) = g.lw.wqkv_full, g.lw.wqkv
                dve.wait_ge(loaded, 48)
                nc.vector.tensor_copy(hi[:, :, :], full[:, :, :]).then_inc(high, 1)
                dve.wait_ge(high, 1)
                nc.vector.tensor_tensor(lo[:, :, :], full[:, :, :], hi[:, :, :].bitcast(F32), ALU.subtract)


GM_SEMS = ("w_next", "w_high", "xn_parts", "fs_ready", "fs_turned", "stats", "aggr", "varp", "rstd", "normed", "xn_turned",
           "xn_out", "gate_done", "a_done", "gelu_done", "act_done", "down_done", "y_out")


def gated_mlp(nc, layer, g, w):
    yT, ident = g.yT, g.ident
    with ExitStack() as ctx:
        sb = lambda n, s, d=F32: ctx.enter_context(nc.sbuf_tensor("gm_" + n, s, d))
        ps = lambda n: ctx.enter_context(nc.psum_tensor("gm_" + n, [128, GRP], F32))
        s = g.gm_sems
        w1, w2, b1, vec = g.lw.w1, g.lw.w2, g.lw.b1, g.lw.vec
        fs = g.lw.fs
        st = sb("st", [128, TPG, 6])
        mv = sb("mv", [128, TPG, 2])
        rstd = sb("rstd", [128, TPG])
        tick = sb("tick", [128, 1])
        xn = sb("xn", [128, TPG, D])
        xnT = sb("xnT", [128, GRP])
        xp = [sb(f"x{n}", [128, GRP], F32R) for n in ("high", "low")]
        gl = sb("gl", [128, 2, GRP])
        hid = sb("hid", [128, 2, GRP])
        TA, TB, Y = ps("ta"), ps("tb"), ps("y")
        GT = [ps("g0"), ps("g1")]
        AT = [ps("a0"), ps("a1")]

        class L(Group):
            def __init__(self, at, loop=None):
                super().__init__(at, loop)

            def n(self, per, r, lag=0):
                return layer * (per * NGRP) + self.count(per, r, lag)

        def run(eng, multiply, turn=None, norm=None, split=None):
            def step(f, *at):
                return (lambda: f(L(*at))) if f else (lambda: None)

            nothing = lambda: None
            step(turn, 0)(), step(norm, 0)(), step(split, 0)(), step(turn, 1)()
            multiply(L(0), step(turn, 2), step(norm, 1), step(split, 1))
            with eng.Fori(0, NGRP - 3) as loop:
                multiply(L(1, loop), step(turn, 3, loop), step(norm, 2, loop), step(split, 2, loop))
            multiply(L(NGRP - 2), nothing, step(norm, NGRP - 1), step(split, NGRP - 1))
            multiply(L(NGRP - 1), nothing, nothing, nothing)

        def wait_chunk(eng, sem, u, per, r):
            if r > 0 or u.at > 0:
                eng.wait_ge(sem, u.n(per, r))

        with nc.Block() as block:

            @block.sync
            def _(sp):
                attention_weights_load(sp, (layer + 1) % DEPTH, g, w, s.w_next)
                with sp.Fori(0, NGRP - 1) as loop:
                    u = L(1, loop)
                    sp.wait_ge(s.fs_turned, u.n(1, 1, 1))
                    shifted_group_load(sp, g, u)
                sp.wait_ge(s.y_out, L(0).n(1, 1))
                shifted_sequence_load(sp, g, 0)

            @block.tensor
            def _(pe):
                def turn(u):
                    pe.wait_ge(s.fs_ready, u.n(48, 48))
                    if u.has(1):
                        pe.wait_ge(s.normed, u.n(1, 1, 1))
                    for t in range(TPG):
                        last = nc.tensor.transpose(TA[:, t * D:(t + 1) * D], fs[:, t * D:(t + 1) * D], ident[:, :])
                    last.then_inc(s.fs_turned, 1)

                def norm(u):
                    pe.wait_ge(s.normed, u.n(1, 1))
                    if u.has(1):
                        pe.wait_ge(s.xn_out, u.n(2, 1, 1))
                    for t in range(TPG):
                        last = nc.tensor.transpose(TB[:, t * D:(t + 1) * D], xn[:, t, :], ident[:, :])
                    last.then_inc(s.xn_turned, 1)

                def multiply(u, turn_later, norm_next, split_next):
                    def down(j):
                        r = glu_rows(j)
                        pe.wait_ge(s.act_done, u.n(GCH, j + 1))
                        if j == 0:
                            wait_chunk(pe, s.y_out, u, 1, 0)
                        last = nc.tensor.matmul(Y[:, :], w2[0:r, j, :], hid[0:r, j % 2, :],
                                                start=(j == 0), stop=(j == GCH - 1))
                        if j == GCH - 1:
                            last.then_inc(s.down_done, 1)

                    pe.wait_ge(s.xn_parts, u.n(1, 1))
                    for j in range(GCH):
                        r = glu_rows(j)
                        wait_chunk(pe, s.gelu_done, u, GCH, max(j - 1, 0))
                        three_passes(nc, GT[j % 2][0:r, :], [x[:, GLU + j * GW:GLU + j * GW + r] for x in w1],
                                     [x[:, :] for x in xp]).then_inc(s.gate_done, 1)
                        wait_chunk(pe, s.act_done, u, GCH, max(j - 1, 0))
                        three_passes(nc, AT[j % 2][0:r, :], [x[:, j * GW:j * GW + r] for x in w1],
                                     [x[:, :] for x in xp]).then_inc(s.a_done, 1)
                        if j == 1:
                            norm_next()
                        if j >= 1:
                            down(j - 1)
                        if j == 1:
                            turn_later()
                    down(GCH - 1)

                run(pe, multiply, turn, norm)

            @block.scalar
            def _(act):
                def norm(u):
                    act.wait_ge(s.xn_turned, u.n(1, 1))
                    if u.has(1):
                        act.wait_ge(s.xn_parts, u.n(1, 1, 1))
                    nc.scalar.activation(xnT[:, :], TB[:, :], ACT.Identity, bias=vec[:, 1:2],
                                         scale=vec[:, 0:1]).then_inc(s.xn_out, 1)

                def split(u):
                    act.wait_ge(s.xn_out, u.n(2, 1))
                    if u.has(1):
                        act.wait_ge(s.a_done, u.n(GCH, GCH, 1))
                    nc.scalar.activation(xp[0][:, :], xnT[:, :], ACT.Copy).then_inc(s.xn_out, 1)

                def multiply(u, turn_later, norm_next, split_next):
                    for j in range(GCH):
                        r = glu_rows(j)
                        act.wait_ge(s.gate_done, u.n(GCH, j + 1))
                        wait_chunk(act, s.act_done, u, GCH, max(j - 1, 0))
                        nc.scalar.activation(gl[0:r, j % 2, :], GT[j % 2][0:r, :], ACT.Gelu,
                                             bias=b1[0:r, 1, j:j + 1]).then_inc(s.gelu_done, 1)
                        if j == 1:
                            norm_next()
                    split_next()

                run(act, multiply, None, norm, split)

            @block.vector
            def _(dve):
                rows = TA[:, :].rearrange("p (t f) -> p t f", t=TPG)

                def turn(u):
                    dve.wait_ge(s.fs_turned, u.n(1, 1))
                    for t in range(TPG):
                        last = nc.vector.bn_stats(st[:, t, :], rows[:, t, :])
                    last.then_inc(s.stats, 1)
                    dve.wait_ge(s.stats, u.n(1, 1))
                    if u.has(1):
                        dve.wait_ge(s.rstd, u.n(1, 1, 1))
                    nc.vector.memset(tick[:, :], 0.0)
                    for t in range(TPG):
                        last = nc.vector.bn_aggr(mv[:, t, :], st[:, t, :])
                    last.then_inc(s.aggr, 1)

                def norm(u):
                    dve.wait_ge(s.rstd, u.n(1, 1))
                    if u.has(1):
                        dve.wait_ge(s.xn_turned, u.n(1, 1, 1))
                    for t in range(TPG):
                        last = nc.vector.tensor_scalar(xn[:, t, :], rows[:, t, :], mv[:, t, 0:1],
                                                       rstd[:, t:t + 1], ALU.subtract, ALU.mult)
                    last.then_inc(s.normed, 1)

                def split(u):
                    dve.wait_ge(s.xn_out, u.n(2, 2))
                    nc.vector.tensor_tensor(xp[1][:, :], xnT[:, :], xp[0][:, :].bitcast(F32),
                                            ALU.subtract).then_inc(s.xn_parts, 1)

                def multiply(u, turn_later, norm_next, split_next):
                    norm_next()
                    for j in range(GCH):
                        r = glu_rows(j)
                        dve.wait_ge(s.gelu_done, u.n(GCH, j + 1))
                        dve.wait_ge(s.a_done, u.n(GCH, j + 1))
                        if j < 2:
                            wait_chunk(dve, s.down_done, u, 1, 0)
                        nc.vector.scalar_tensor_tensor(
                            out=hid[0:r, j % 2, :], in0=AT[j % 2][0:r, :], scalar=b1[0:r, 0, j:j + 1],
                            in1=gl[0:r, j % 2, :], op0=ALU.add, op1=ALU.mult).then_inc(s.act_done, 1)
                        if j == 1:
                            turn_later()
                    split_next()
                    if u.at == NGRP - 1:
                        dve.wait_ge(g.wa_sems.xs_ready, layer * (32 * NB) + 32 * (NB + 1))
                    dve.wait_ge(s.down_done, u.n(1, 1))
                    nc.vector.scalar_tensor_tensor(out=yT[:, u.cols()], in0=Y[:, :], scalar=vec[:, 2:3],
                                                   in1=yT[:, u.cols()], op0=ALU.add, op1=ALU.add).then_inc(s.y_out, 1)

                run(dve, multiply, turn, norm, split)

            @block.gpsimd
            def _(pool):
                WCOLS = 3 * INNER // (NGRP - 2)
                full, hi, lo = (x[:, :, :].rearrange("p t n -> p (t n)") for x in (g.lw.wqkv_full, *g.lw.wqkv))

                def split_weights(u):
                    here = slice((u.at - 1) * WCOLS, u.at * WCOLS) if u.loop is None else bass.ds(u.loop * WCOLS, WCOLS)
                    pool.wait_ge(s.w_next, layer * 48 + 48)
                    nc.gpsimd.tensor_tensor(hi[:, here], full[:, here], g.zero.broadcast_to((128, WCOLS)),
                                            ALU.add).then_inc(s.w_high, 1)
                    done = layer * (NGRP - 2) + u.at
                    pool.wait_ge(s.w_high, done if u.loop is None else done + u.loop)
                    nc.gpsimd.tensor_tensor(lo[:, here], full[:, here], hi[:, here].bitcast(F32), ALU.subtract)

                def turn(u):
                    pool.wait_ge(s.aggr, u.n(1, 1))
                    if u.has(1):
                        pool.wait_ge(s.normed, u.n(1, 1, 1))
                    nc.gpsimd.tensor_tensor(rstd[:, :], mv[:, :, 1], g.eps[:, 0:TPG], ALU.add).then_inc(s.varp, 1)
                    pool.wait_ge(s.varp, u.n(1, 1))
                    nc.gpsimd.tensor_tensor(rstd[:, :], rstd[:, :], g.mhalf[:, 0:TPG], ALU.pow).then_inc(s.rstd, 1)

                def multiply(u, turn_later, norm_next, split_next):
                    turn_later()
                    if 1 <= u.at <= NGRP - 2:
                        split_weights(u)

                run(pool, multiply, turn)


LA_ORDER = [("project", 0), ("finish", 2), ("to_rows", 0), ("feature", 1), ("weigh", 1), ("to_cols", 0), ("sum", 1),
            ("divide", 1)]


def linear_attention(nc, g, w):
    yT, ident = g.yT, g.ident
    with ExitStack() as ctx:
        sb = lambda n, s, d=F32: ctx.enter_context(nc.sbuf_tensor("la_" + n, s, d))
        ps = lambda n: ctx.enter_context(nc.psum_tensor("la_" + n, [128, GRP], F32))
        sem = phase_semaphores(nc, ctx, "la_")
        aT = g.aT
        wqkv = sb("wqkv", [128, 3, D])
        wf = sb("wf", [128, 2, D])
        vec = sb("vec", [128, 11])
        gvb = sb("gvb", [128, 2, D])
        hmask = sb("hmask", [128, D])
        hsel = sb("hsel", [128, HEADS])
        hprobe = sb("hprobe", [128, HEADS])
        hselT = sb("hselT", [HEADS, 128])
        pk0 = sb("pk0", [128, 1])
        col = sb("col", [128, 3, GRP])
        st = sb("st", [128, 3 * TPG, 6])
        mv = sb("mv", [128, 3 * TPG, 2])
        rstd = sb("rstd", [128, 3 * TPG])
        st2 = sb("st2", [128, TPG, 6])
        mv2 = sb("mv2", [128, TPG, 2])
        rstd2 = sb("rstd2", [128, TPG])
        tick = sb("tick", [128, 1])
        row = sb("row", [128, 3, TPG, D])
        vt = sb("vt", [128, 2, TPG, D + 1])
        qk = sb("qk", [128, 2, 2, GRP])
        qsum = sb("qsum", [128, 2, SPG])
        probe = sb("probe", [128, SPG, HEADS])
        phi = sb("phi", [128, 2, GRP])
        mx = sb("mx", [HEADS, SPG])
        nm = sb("nm", [HEADS, SPG])
        ex = sb("ex", [HEADS, SPG, SEQ])
        tot = sb("tot", [HEADS, SPG])
        z0 = sb("z0", [HEADS, SPG])
        rc = sb("rc", [HEADS, SPG])
        s0 = sb("s0", [HEADS, SPG])
        sct = sb("sct", [128, TPG * HEADS + SPG])
        pkw = sb("pkw", [128, TPG, D])
        ks = sb("ks", [128, SPG])
        kvx = sb("kvx", [128, SPG, D + HEADS])
        dn = sb("dn", [128, TPG, HEADS])
        ao = sb("ao", [128, TPG, D])
        an = sb("an", [128, TPG, D])
        A = [ps(f"a{i}") for i in range(4)]
        B = [ps(f"b{i}") for i in range(4)]
        names = ("loaded pads pk0_t pk0_ready projected col_out rowed stats aggr varp rstd_done normed vt_scaled vt_ready "
                 "coled qk_out probe_done phi_done logits_done tanh_done plus1 mx_done nm_done exp_done tot_done rc_done "
                 "s0_done ex_done pk_turned sct_turned sct_out pkw_done kv_done ks_done kvx_done num_done dn_done rdn_done "
                 "ao_done stats2 aggr2 varp2 rstd2_done an_done an_turned a_out y_out").split()
        s = type("Sems", (), {n: sem(n) for n in names})

        def tiles(bank):
            return bank[:, :].rearrange("p (t f) -> p t f", t=TPG)

        with nc.Block() as block:

            @block.sync
            def _(sp):
                for n, v in enumerate((w.Wq, w.Wk, w.Wv)):
                    sp.dma_start(wqkv[:, n, :], v).then_inc(s.loaded, 16)
                for n, v in enumerate((w.Wfq, w.Wfk)):
                    sp.dma_start(wf[:, n, :], v).then_inc(s.loaded, 16)
                for n, v in enumerate((w.bq, w.bk, w.bv, w.gq, w.betaq, w.gk, w.betak, w.bfq, w.bfk, w.ga, w.ba)):
                    sp.dma_start(vec[:, n:n + 1], v.unsqueeze(1)).then_inc(s.loaded, 16)
                for n, v in enumerate((w.gv, w.betav)):
                    sp.dma_start(gvb[:, n, :], v.unsqueeze(0).broadcast_to((128, D))).then_inc(s.loaded, 16)
                for dst, v in ((hmask, w.c_hmask), (hsel, w.c_hsel), (hprobe, w.c_hprobe), (hselT, w.c_hselT)):
                    sp.dma_start(dst[:, :], v).then_inc(s.loaded, 16)

            ALL_LOADED = 16 * 22

            @block.tensor
            def _(pe):
                pe.wait_ge(s.loaded, ALL_LOADED)

                def project(u):
                    ring_wait(pe, s.qk_out, u, SPG + 1, 1)
                    ring_wait(pe, s.normed, u, 3, 1)
                    for n in range(3):
                        nc.tensor.matmul(A[n][:, :], wqkv[:, n, :], yT[:, u.cols()], start=True,
                                         stop=True).then_inc(s.projected, 1)

                def to_rows(u):
                    for n in range(3):
                        pe.wait_ge(s.col_out, u.count(3, n + 1))
                        out = A[(3 + n) % 4]
                        for t in range(TPG):
                            last = nc.tensor.transpose(out[:, t * D:(t + 1) * D], col[:, n, t * D:(t + 1) * D], ident[:, :])
                        last.then_inc(s.rowed, 1)

                def to_cols(u):
                    for n in range(2):
                        pe.wait_ge(s.normed, u.count(3, n + 1))
                        if n == 0:
                            pe.wait_ge(s.col_out, u.count(3, 3))
                        for t in range(TPG):
                            last = nc.tensor.transpose(A[2 + n][:, t * D:(t + 1) * D], row[:, n, t, :], ident[:, :])
                        last.then_inc(s.coled, 1)

                def feature(u):
                    pe.wait_ge(s.qk_out, u.count(SPG + 1, SPG + 1))
                    ring_wait(pe, s.ao_done, u, 2, 1)
                    ring_wait(pe, s.a_out, u, 1, 1)
                    for n in range(2):
                        nc.tensor.matmul(B[n][:, :], wf[:, n, :], qk[:, u.par, n, :], start=True,
                                         stop=True).then_inc(s.phi_done, 1)
                    pe.wait_ge(s.probe_done, u.count(1, 1))
                    ring_wait(pe, s.kvx_done, u, 1, 1)
                    for q in range(SPG):
                        last = nc.tensor.matmul(B[2][0:HEADS, q * SEQ:(q + 1) * SEQ], probe[:, q, :],
                                                qk[:, u.par, 1, q * SEQ:(q + 1) * SEQ], start=True, stop=True)
                    last.then_inc(s.logits_done, 1)

                def weigh(u):
                    pe.wait_ge(s.tanh_done, u.count(2, 2))
                    for t in range(TPG):
                        last = nc.tensor.transpose(B[1][:, t * D:(t + 1) * D], phi[:, 1, t * D:(t + 1) * D], ident[:, :])
                    last.then_inc(s.pk_turned, 1)
                    pe.wait_ge(s.s0_done, u.count(1, 1))
                    pe.wait_ge(s.ex_done, u.count(1, 1))
                    nc.tensor.matmul(B[3][:, TPG * HEADS:TPG * HEADS + SPG], hselT[:, :], s0[:, :], start=True, stop=True)
                    for t in range(TPG):
                        q, tt = divmod(t, TPG // SPG)
                        last = nc.tensor.transpose(B[3][:, t * HEADS:(t + 1) * HEADS], ex[:, q, tt * D:(tt + 1) * D],
                                                   ident[0:HEADS, 0:HEADS])
                    last.then_inc(s.sct_turned, 1)

                def sum_(u):
                    pe.wait_ge(s.pkw_done, u.count(1, 1))
                    pe.wait_ge(s.vt_ready, u.count(1, 1))
                    for q in range(SPG):
                        for tt in range(TPG // SPG):
                            t = q * (TPG // SPG) + tt
                            last = nc.tensor.matmul(B[2][:, q * (D + 1):(q + 1) * (D + 1)], pkw[:, t, :],
                                                    vt[:, u.par, t, :], start=(tt == 0), stop=(tt == TPG // SPG - 1))
                    last.then_inc(s.kv_done, 1)

                def divide(u):
                    pe.wait_ge(s.kvx_done, u.count(1, 1))
                    pe.wait_ge(s.plus1, u.count(1, 1))
                    for q in range(SPG):
                        for tt in range(TPG // SPG):
                            t = q * (TPG // SPG) + tt
                            last = nc.tensor.matmul(B[3 * q][:, tt * (D + HEADS):(tt + 1) * (D + HEADS)],
                                                    phi[:, 0, t * D:(t + 1) * D], kvx[:, q, :], start=True, stop=True)
                        last.then_inc(s.num_done, 1)

                def finish(u):
                    pe.wait_ge(s.an_done, u.count(1, 1))
                    for t in range(TPG):
                        last = nc.tensor.transpose(B[1][:, t * D:(t + 1) * D], an[:, t, :], ident[:, :])
                    last.then_inc(s.an_turned, 1)

                skewed(pe, LA_ORDER, {"project": project, "to_rows": to_rows, "to_cols": to_cols, "feature": feature,
                                      "weigh": weigh, "sum": sum_, "divide": divide, "finish": finish})

            @block.scalar
            def _(act):
                act.wait_ge(s.loaded, ALL_LOADED)
                nc.scalar.activation(pk0[:, :], vec[:, 8:9], ACT.Tanh).then_inc(s.pk0_t, 1)

                def project(u):
                    ring_wait(act, s.rowed, u, 3, 1)
                    for n in range(3):
                        act.wait_ge(s.projected, u.count(3, n + 1))
                        nc.scalar.activation(col[:, n, :], A[n][:, :], ACT.Identity,
                                             bias=vec[:, n:n + 1]).then_inc(s.col_out, 1)

                def to_cols(u):
                    act.wait_ge(s.coled, u.count(2, 1))
                    ring_wait(act, s.logits_done, u, 1)
                    ring_wait(act, s.probe_done, u, 1)
                    for q in range(SPG):
                        nc.scalar.activation(qk[:, u.par, 0, q * SEQ:(q + 1) * SEQ], A[2][:, q * SEQ:(q + 1) * SEQ],
                                             ACT.Identity, bias=vec[:, 4:5], scale=vec[:, 3:4],
                                             accum_out=qsum[:, u.par, q:q + 1]).then_inc(s.qk_out, 1)
                    act.wait_ge(s.coled, u.count(2, 2))
                    nc.scalar.activation(qk[:, u.par, 1, :], A[3][:, :], ACT.Identity, bias=vec[:, 6:7],
                                         scale=vec[:, 5:6]).then_inc(s.qk_out, 1)

                def feature(u):
                    ring_wait(act, s.num_done, u, 2, 1)
                    for n in range(2):
                        act.wait_ge(s.phi_done, u.count(2, n + 1))
                        nc.scalar.activation(phi[:, n, :], B[n][:, :], ACT.Tanh,
                                             bias=vec[:, 7 + n:8 + n]).then_inc(s.tanh_done, 1)
                    act.wait_ge(s.nm_done, u.count(1, 1))
                    ring_wait(act, s.sct_turned, u, 1, 1)
                    for q in range(SPG):
                        nc.scalar.activation(ex[:, q, :], B[2][0:HEADS, q * SEQ:(q + 1) * SEQ], ACT.Exp,
                                             bias=nm[:, q:q + 1], accum_out=tot[:, q:q + 1])
                    nc.scalar.activation(z0[:, :], nm[:, :], ACT.Exp).then_inc(s.exp_done, 1)

                def finish(u):
                    act.wait_ge(s.an_turned, u.count(1, 1))
                    nc.scalar.activation(aT[:, u.cols()], B[1][:, :], ACT.Identity, bias=vec[:, 10:11],
                                         scale=vec[:, 9:10]).then_inc(s.a_out, 1)

                skewed(act, LA_ORDER, {"project": project, "to_cols": to_cols, "feature": feature, "finish": finish})

            @block.vector
            def _(dve):
                nc.vector.memset(vt[:, :, :, D:D + 1], 1.0).then_inc(s.pads, 1)
                dve.wait_ge(s.pk0_t, 1)
                nc.vector.tensor_scalar(pk0[:, :], pk0[:, :], 1.0, None, ALU.add).then_inc(s.pk0_ready, 1)
                dve.wait_ge(s.loaded, ALL_LOADED)

                def to_rows(u):
                    for n in range(3):
                        dve.wait_ge(s.rowed, u.count(3, n + 1))
                        for t in range(TPG):
                            last = nc.vector.bn_stats(st[:, n * TPG + t, :], tiles(A[(3 + n) % 4])[:, t, :])
                    last.then_inc(s.stats, 1)
                    dve.wait_ge(s.stats, u.count(1, 1))
                    nc.vector.memset(tick[:, :], 0.0)
                    for t in range(3 * TPG):
                        last = nc.vector.bn_aggr(mv[:, t, :], st[:, t, :])
                    last.then_inc(s.aggr, 1)

                def to_cols(u):
                    dve.wait_ge(s.rstd_done, u.count(1, 1))
                    ring_wait(dve, s.vt_ready, u, 1, 1)
                    for n in range(3):
                        for t in range(TPG):
                            k = n * TPG + t
                            last = nc.vector.tensor_scalar(row[:, n, t, :], tiles(A[(3 + n) % 4])[:, t, :], mv[:, k, 0:1],
                                                           rstd[:, k:k + 1], ALU.subtract, ALU.mult)
                        last.then_inc(s.normed, 1)

                def feature(u):
                    dve.wait_ge(s.qk_out, u.count(SPG + 1, SPG))
                    ring_wait(dve, s.logits_done, u, 1, 1)
                    for q in range(SPG):
                        last = nc.vector.tensor_scalar(probe[:, q, :], hprobe[:, :], qsum[:, u.par, q:q + 1], None, ALU.mult)
                    last.then_inc(s.probe_done, 1)
                    dve.wait_ge(s.logits_done, u.count(1, 1))
                    nc.vector.tensor_reduce(mx[:, :], B[2][0:HEADS, :].rearrange("p (q k) -> p q k", q=SPG), AX.X,
                                            ALU.max).then_inc(s.mx_done, 1)
                    dve.wait_ge(s.mx_done, u.count(1, 1))
                    nc.vector.tensor_scalar(nm[:, :], mx[:, :], 0.0, -1.0, ALU.max, ALU.mult).then_inc(s.nm_done, 1)

                def weigh(u):
                    dve.wait_ge(s.tanh_done, u.count(2, 1))
                    nc.vector.tensor_scalar(phi[:, 0, :], phi[:, 0, :], 1.0, None, ALU.add).then_inc(s.plus1, 1)
                    dve.wait_ge(s.exp_done, u.count(1, 1))
                    nc.vector.tensor_tensor(tot[:, :], tot[:, :], z0[:, :], ALU.add).then_inc(s.tot_done, 1)
                    dve.wait_ge(s.tot_done, u.count(1, 1))
                    nc.vector.reciprocal(rc[:, :], tot[:, :]).then_inc(s.rc_done, 1)
                    dve.wait_ge(s.rc_done, u.count(1, 1))
                    nc.vector.tensor_tensor(s0[:, :], z0[:, :], rc[:, :], ALU.mult).then_inc(s.s0_done, 1)
                    nc.vector.tensor_tensor(ex[:, :, :], ex[:, :, :], rc[:, :].unsqueeze(2).broadcast_to(
                        (HEADS, SPG, SEQ)), ALU.mult).then_inc(s.ex_done, 1)
                    dve.wait_ge(s.sct_turned, u.count(1, 1))
                    nc.vector.tensor_copy(sct[:, :], B[3][:, 0:TPG * HEADS + SPG]).then_inc(s.sct_out, 1)
                    dve.wait_ge(s.sct_out, u.count(1, 1))
                    dve.wait_ge(s.pk_turned, u.count(1, 1))
                    for t in range(TPG):
                        last = nc.vector.scalar_tensor_tensor(
                            out=pkw[:, t, :].rearrange("p (h d) -> p h d", h=HEADS),
                            in0=tiles(B[1])[:, t, :].rearrange("p (h d) -> p h d", h=HEADS), scalar=1.0,
                            in1=sct[:, t * HEADS:(t + 1) * HEADS].unsqueeze(2).broadcast_to((128, HEADS, LIN_HD)),
                            op0=ALU.add, op1=ALU.mult)
                    last.then_inc(s.pkw_done, 1)

                def sum_(u):
                    kv = B[2][:, 0:SPG * (D + 1)].rearrange("p (q e) -> p q e", q=SPG)
                    dve.wait_ge(s.kv_done, u.count(1, 1))
                    dve.wait_ge(s.pk0_ready, 1)
                    nc.vector.scalar_tensor_tensor(out=ks[:, :], in0=sct[:, TPG * HEADS:TPG * HEADS + SPG],
                                                   scalar=pk0[:, 0:1], in1=kv[:, :, D], op0=ALU.mult,
                                                   op1=ALU.add).then_inc(s.ks_done, 1)
                    nc.vector.tensor_tensor(kvx[:, :, 0:D], kv[:, :, 0:D], hmask[:, :].unsqueeze(1).broadcast_to(
                        (128, SPG, D)), ALU.mult)
                    dve.wait_ge(s.ks_done, u.count(1, 1))
                    for q in range(SPG):
                        last = nc.vector.tensor_scalar(kvx[:, q, D:D + HEADS], hsel[:, :], ks[:, q:q + 1], None, ALU.mult)
                    last.then_inc(s.kvx_done, 1)

                def divide(u):
                    half = TPG // SPG
                    nd = [B[3 * q][:, 0:half * (D + HEADS)].rearrange("p (t e) -> p t e", t=half) for q in range(SPG)]
                    for q in range(SPG):
                        dve.wait_ge(s.num_done, u.count(SPG, q + 1))
                        last = nc.vector.tensor_scalar(dn[:, q * half:(q + 1) * half, :], nd[q][:, :, D:D + HEADS], 1e-6,
                                                       None, ALU.add)
                    last.then_inc(s.dn_done, 1)
                    dve.wait_ge(s.dn_done, u.count(1, 1))
                    nc.vector.reciprocal(dn[:, :, :], dn[:, :, :]).then_inc(s.rdn_done, 1)
                    dve.wait_ge(s.rdn_done, u.count(1, 1))
                    for q in range(SPG):
                        nc.vector.tensor_tensor(
                            ao[:, q * half:(q + 1) * half, :].rearrange("p t (h d) -> p t h d", h=HEADS),
                            nd[q][:, :, 0:D].rearrange("p t (h d) -> p t h d", h=HEADS),
                            dn[:, q * half:(q + 1) * half, :].unsqueeze(3).broadcast_to((128, half, HEADS, LIN_HD)),
                            ALU.mult).then_inc(s.ao_done, 1)
                    dve.wait_ge(s.ao_done, u.count(SPG, SPG))
                    for t in range(TPG):
                        last = nc.vector.bn_stats(st2[:, t, :], ao[:, t, :])
                    last.then_inc(s.stats2, 1)
                    dve.wait_ge(s.stats2, u.count(1, 1))
                    nc.vector.memset(tick[:, :], 0.0)
                    for t in range(TPG):
                        last = nc.vector.bn_aggr(mv2[:, t, :], st2[:, t, :])
                    last.then_inc(s.aggr2, 1)

                def finish(u):
                    dve.wait_ge(s.rstd2_done, u.count(1, 1))
                    for t in range(TPG):
                        last = nc.vector.tensor_scalar(an[:, t, :], ao[:, t, :], mv2[:, t, 0:1], rstd2[:, t:t + 1],
                                                       ALU.subtract, ALU.mult)
                    last.then_inc(s.an_done, 1)
                    dve.wait_ge(s.a_out, u.count(1, 1))
                    nc.vector.tensor_tensor(yT[:, u.cols()], yT[:, u.cols()], aT[:, u.cols()], ALU.add).then_inc(s.y_out, 1)

                skewed(dve, LA_ORDER, {"to_rows": to_rows, "to_cols": to_cols, "feature": feature, "weigh": weigh,
                                       "sum": sum_, "divide": divide, "finish": finish})

            @block.gpsimd
            def _(pool):
                pool.wait_ge(s.loaded, ALL_LOADED)
                pool.wait_ge(s.pads, 1)

                def to_rows(u):
                    pool.wait_ge(s.aggr, u.count(1, 1))
                    nc.gpsimd.tensor_tensor(rstd[:, :], mv[:, :, 1], g.eps[:, 0:3 * TPG], ALU.add).then_inc(s.varp, 1)
                    pool.wait_ge(s.varp, u.count(1, 1))
                    nc.gpsimd.tensor_tensor(rstd[:, :], rstd[:, :], g.mhalf[:, 0:3 * TPG], ALU.pow).then_inc(s.rstd_done, 1)

                def to_cols(u):
                    pool.wait_ge(s.normed, u.count(3, 3))
                    ring_wait(pool, s.kv_done, u, 1)
                    nc.gpsimd.tensor_tensor(vt[:, u.par, :, 0:D], row[:, 2, :, :], gvb[:, 0, :].unsqueeze(1).broadcast_to(
                        (128, TPG, D)), ALU.mult).then_inc(s.vt_scaled, 1)
                    pool.wait_ge(s.vt_scaled, u.count(1, 1))
                    nc.gpsimd.tensor_tensor(vt[:, u.par, :, 0:D], vt[:, u.par, :, 0:D], gvb[:, 1, :].unsqueeze(
                        1).broadcast_to((128, TPG, D)), ALU.add).then_inc(s.vt_ready, 1)

                def divide(u):
                    pool.wait_ge(s.aggr2, u.count(1, 1))
                    nc.gpsimd.tensor_tensor(rstd2[:, :], mv2[:, :, 1], g.eps[:, 0:TPG], ALU.add).then_inc(s.varp2, 1)
                    pool.wait_ge(s.varp2, u.count(1, 1))
                    nc.gpsimd.tensor_tensor(rstd2[:, :], rstd2[:, :], g.mhalf[:, 0:TPG], ALU.pow).then_inc(s.rstd2_done, 1)

                skewed(pool, LA_ORDER, {"to_rows": to_rows, "to_cols": to_cols, "divide": divide})


MLP_ORDER = [("up", 0), ("down", 0)]


def plain_mlp(nc, tag, g, src, w1_d, b1_d, w2_d, b2_d, gate, skip=None, out_d=None):
    xT, ident = g.xT, g.ident
    with ExitStack() as ctx:
        sb = lambda n, s, d=F32: ctx.enter_context(nc.sbuf_tensor(tag + n, s, d))
        ps = lambda n: ctx.enter_context(nc.psum_tensor(tag + n, [128, GRP], F32))
        sem = phase_semaphores(nc, ctx, tag)
        w1 = sb("w1", [128, MLP])
        w2 = sb("w2", [128, MCH, D])
        b1 = sb("b1", [128, MCH])
        b2 = sb("b2", [128, 1])
        hid = sb("hid", [128, 2, MCH, GRP])
        sm = sb("sm", [128, 2, GRP])
        xo = sb("xo", [128, 2, GRP])
        rows = sb("rows", [128, 2, TPG, D])
        H = [ps(f"h{i}") for i in range(MCH)]
        Y = [ps("y0"), ps("y1")]
        R = [ps("r0"), ps("r1")]
        loaded, up_done, gelu_done, down_done, sum_done, x_out, turned, row_out = map(sem, (
            "loaded", "up_done", "gelu_done", "down_done", "sum_done", "x_out", "turned", "row_out"))
        stored = [sem("stored0"), sem("stored1")]
        order = [("up", 0), ("down", 1)] + ([("turn", 1)] if out_d is None else [("turn", 2)])

        with nc.Block() as block:

            @block.sync
            def _(sp):
                sp.dma_start(w1[:, :], w1_d).then_inc(loaded, 16)
                for j in range(MCH):
                    sp.dma_start(b1[:, j:j + 1], b1_d[j * 128:(j + 1) * 128].unsqueeze(1)).then_inc(loaded, 16)
                sp.dma_start(w2[:, :, :], w2_d.rearrange("(j p) n -> p j n", p=128)).then_inc(loaded, 16)
                sp.dma_start(b2[:, :], b2_d.unsqueeze(1)).then_inc(loaded, 16)
                if out_d is not None:
                    tokens = out_d.rearrange("b (t p) f -> p (b t) f", p=128)

                    def turn(u):
                        sp.wait_ge(row_out, u.count(1, 1))
                        t = slice(u.at * TPG, (u.at + 1) * TPG) if u.loop is None else bass.ds(
                            u.loop * (2 * TPG) + u.at * TPG, TPG)
                        sp.dma_start(tokens[:, t, :], rows[:, u.par]).then_inc(stored[u.par], 16)

                    skewed(sp, order, {"turn": turn})
                    for sem_ in stored:
                        sp.wait_ge(sem_, 16 * (NGRP // 2))

            @block.tensor
            def _(pe):
                pe.wait_ge(loaded, 16 * (3 + MCH))

                def up(u):
                    for j in range(MCH):
                        if u.has(1):
                            pe.wait_ge(gelu_done, u.count(MCH, j + 1, 1))
                        nc.tensor.matmul(H[j][:, :], w1[:, j * 128:(j + 1) * 128], src[:, u.cols()], start=True,
                                         stop=True).then_inc(up_done, 1)

                def down(u):
                    ring_wait(pe, sum_done, u, 1)
                    for j in range(MCH):
                        pe.wait_ge(gelu_done, u.count(MCH, j + 1))
                        last = nc.tensor.matmul(Y[u.par][:, :], w2[:, j, :], hid[:, u.par, j, :], start=(j == 0),
                                                stop=(j == MCH - 1))
                    last.then_inc(down_done, 1)

                def turn(u):
                    pe.wait_ge(x_out, u.count(1, 1))
                    ring_wait(pe, row_out, u, 1)
                    for t in range(TPG):
                        last = nc.tensor.transpose(R[u.par][:, t * D:(t + 1) * D], xo[:, u.par, t * D:(t + 1) * D],
                                                   ident[:, :])
                    last.then_inc(turned, 1)

                steps = {"up": up, "down": down}
                if out_d is not None:
                    steps["turn"] = turn
                skewed(pe, order, steps)

            @block.scalar
            def _(act):
                act.wait_ge(loaded, 16 * (3 + MCH))

                def up(u):
                    ring_wait(act, down_done, u, 1)
                    for j in range(MCH):
                        act.wait_ge(up_done, u.count(MCH, j + 1))
                        nc.scalar.activation(hid[:, u.par, j, :], H[j][:, :], ACT.Gelu,
                                             bias=b1[:, j:j + 1]).then_inc(gelu_done, 1)

                skewed(act, order, {"up": up})

            @block.vector
            def _(dve):
                dve.wait_ge(loaded, 16 * (3 + MCH))

                def down(u):
                    dve.wait_ge(down_done, u.count(1, 1))
                    ring_wait(dve, x_out, u, 1)
                    if skip is None:
                        nc.vector.tensor_scalar(sm[:, u.par, :], Y[u.par][:, :], b2[:, 0:1], None,
                                                ALU.add).then_inc(sum_done, 1)
                    else:
                        nc.vector.scalar_tensor_tensor(out=sm[:, u.par, :], in0=Y[u.par][:, :], scalar=b2[:, 0:1],
                                                       in1=skip[:, u.cols()], op0=ALU.add,
                                                       op1=ALU.add).then_inc(sum_done, 1)
                    dve.wait_ge(sum_done, u.count(1, 1))
                    if out_d is not None:
                        ring_wait(dve, turned, u, 1)
                    for q in range(SPG):
                        here = u.cols(q * SEQ, SEQ)
                        to = xT[:, here] if out_d is None else xo[:, u.par, q * SEQ:(q + 1) * SEQ]
                        last = nc.vector.scalar_tensor_tensor(
                            out=to, in0=sm[:, u.par, q * SEQ:(q + 1) * SEQ], scalar=gate[:, u.seq(q)],
                            in1=xT[:, here], op0=ALU.mult, op1=ALU.add)
                    last.then_inc(x_out, 1)

                def turn(u):
                    dve.wait_ge(turned, u.count(1, 1))
                    if u.at >= 2 or u.loop is not None:
                        dve.wait_ge(stored[u.par], Group(u.at - 2, u.loop, 2).turns(16))
                    nc.vector.tensor_copy(rows[:, u.par].rearrange("p t f -> p (t f)"), R[u.par][:, :]).then_inc(row_out, 1)

                steps = {"down": down}
                if out_d is not None:
                    steps["turn"] = turn
                skewed(dve, order, steps)


class PairSlot:
    UPS = HEADS // 2

    def __init__(self, k, loop=None, tail=False):
        self.k, self.loop = k, loop
        self.tail = tail
        self.lead = NB if tail else 1 if loop is not None else 0

    def has(self, lag):
        u = self.k - lag
        return u >= 0 if self.lead == 0 else u < 0 if self.tail else True

    def was(self, lag):
        return self.lead > 0 or self.k >= lag

    def count(self, per, lag, r):
        here = per * (self.UPS * self.lead + self.k - lag) + r
        return here if self.loop is None else here + self.loop * (self.UPS * per)

    def seqs(self, per, lag, r):
        here = per * (self.lead + (self.k - lag) // self.UPS) + r
        return here if self.loop is None else here + self.loop * per

    def cols(self, lag):
        first = (self.lead + (self.k - lag) // self.UPS) * SEQ
        return slice(first, first + SEQ) if self.loop is None else bass.ds(self.loop * SEQ + first, SEQ)

    def seq(self, lag):
        first = self.lead + (self.k - lag) // self.UPS
        return slice(first, first + 1) if self.loop is None else bass.ds(self.loop + first, 1)

    def pair(self, lag):
        return (self.k - lag) % self.UPS

    def par(self, lag):
        return (self.k - lag) % 2


def multiquery_attention(nc, g, w):
    xT, hT, ident = g.xT, g.yT, g.ident
    SPAN = 384
    with ExitStack() as ctx:
        sb = lambda n, s, d=F32: ctx.enter_context(nc.sbuf_tensor("mq_" + n, s, d))
        ps = lambda n: ctx.enter_context(nc.psum_tensor("mq_" + n, [128, 512], F32))
        sem = phase_semaphores(nc, ctx, "mq_")
        wq = sb("wq", [128, INNER])
        wkk = sb("wkk", [128, 2, HD])
        wv = sb("wv", [128, 2, HD])
        wout = sb("wout", [128, HEADS // 2, D])
        bout = sb("bout", [128, 1])
        emb = sb("emb", [BUCKETS, HEADS])
        hot = sb("hot", [BUCKETS, SPAN])
        ones = sb("ones", [1, HEADS])
        off = sb("off", [1, SPAN])
        swap = sb("swap", [128, 128])
        dist = sb("dist", [HEADS, SPAN])
        hank = sb("hank", [128, HEADS, SEQ])
        bias = sb("bias", [128, HEADS, SPAN])
        qT = sb("qT", [128, 2, SEQ])
        kT = sb("kT", [128, SEQ])
        vT = sb("vT", [128, SEQ])
        vv = sb("vv", [128, 2, HD + 1])
        pb = sb("pb", [128, 2, 2, SPAN])
        nm = sb("nm", [128, 2, 2, 2])
        pT = sb("pT", [128, 2, 2, SPAN])
        rs = sb("rs", [128, 2, 2])
        on = sb("on", [128, 2, 2, 2, HD])
        oT = sb("oT", [128, 2, SEQ])
        yo = sb("yo", [128, SEQ])
        tick = sb("tick", [128, 2])
        SC = [ps("sc0"), ps("sc1")]
        TR = [ps("tr0"), ps("tr1")]
        PV, PQ, PO, PY = ps("pv"), ps("pq"), ps("po"), ps("py")
        names = ("loaded dist_mm dist_out stored spread swapped swap_out pads ones q_done k_out q_out vT_done vT_out v_turned "
                 "v_out score_done max_done exp_done p_turned p_out pv_done rs_done norm_done o_turned o_out "
                 "y_done yo_done x_out").split()
        s = type("Sems", (), {n: sem(n) for n in names})
        NLOAD = 12

        def run(eng, slot):
            for k in range(8):
                slot(PairSlot(k))
            with eng.Fori(0, NB - 1) as loop:
                for k in range(8):
                    slot(PairSlot(k, loop))
            for k in range(5):
                slot(PairSlot(k, tail=True))

        with nc.Block() as block:

            @block.sync
            def _(sp):
                for dst, src in ((emb[:, :], w.rel_emb), (hot[:, :], w.c_hot), (off[:, :], w.c_off), (swap[:, :], w.c_swap),
                                 (wq[:, :], w.Wq), (wkk[:, 0, :], w.Wkv[:, 0:HD]), (wkk[:, 1, :], w.Wkv[:, 0:HD]),
                                 (wv[:, 0, :], w.Wkv[:, HD:2 * HD]), (wv[:, 1, :], w.Wkv[:, HD:2 * HD]),
                                 (wout[:, :, :], w.Wout.rearrange("(j p) n -> p j n", p=128)),
                                 (bout[:, :], w.bout.unsqueeze(1)), (ones[:, :], w.c_ones)):
                    sp.dma_start(dst, src).then_inc(s.loaded, 16)
                sp.wait_ge(s.dist_out, 1)
                sp.dma_start(w.scratch, dist[:, :]).then_inc(s.stored, 16)
                sp.wait_ge(s.stored, 16)
                src = w.scratch[:, 0:SEQ].unsqueeze(0)
                sp.dma_start(hank[:, :, :], bass.AP(tensor=w.scratch.tensor, offset=0,
                                                    ap=[[1, 128], [SPAN, HEADS], [1, SEQ]])).then_inc(s.spread, 16)

            @block.tensor
            def _(pe):
                pe.wait_ge(s.loaded, 16 * NLOAD)
                nc.tensor.matmul(PY[0:HEADS, 0:SPAN], emb[:, :], hot[:, :], start=True, stop=False)
                nc.tensor.matmul(PY[0:HEADS, 0:SPAN], ones[:, :], off[:, :], start=False, stop=True).then_inc(s.dist_mm, 1)
                pe.wait_ge(s.spread, 16)
                for n in range(HEADS // 2):
                    if n >= 2:
                        pe.wait_ge(s.swap_out, n - 1)
                    nc.tensor.matmul(SC[n % 2][:, :], swap[:, :], hank[:, 2 * n:2 * n + 2, :].rearrange(
                        "p a b -> p (a b)"), start=True, stop=True).then_inc(s.swapped, 1)
                pe.wait_ge(s.swap_out, HEADS // 2)
                pe.wait_ge(s.ones, 1)

                def slot(u):
                    if u.has(0):
                        if u.was(1):
                            pe.wait_ge(s.q_out, u.count(1, 1, 1))
                        if u.k == 0:
                            nc.tensor.matmul(PQ[:, SEQ:2 * SEQ], wkk[:, :, :].rearrange("p a b -> p (a b)"),
                                             hT[:, u.cols(0)], start=True, stop=True)
                        elif u.k == 1:
                            pe.wait_ge(s.k_out, u.seqs(1, 1, 1))
                        nc.tensor.matmul(PQ[:, 0:SEQ], wq[:, u.k * 128:(u.k + 1) * 128], hT[:, u.cols(0)],
                                         start=True, stop=True).then_inc(s.q_done, 1)
                    if u.has(1):
                        pe.wait_ge(s.q_out, u.count(1, 1, 1))
                        if u.k == 1:
                            pe.wait_ge(s.k_out, u.seqs(1, 1, 1))
                        for e in range(2):
                            if u.was(2):
                                pe.wait_ge(s.max_done, u.count(2, 2, e + 1))
                            r = slice(64 * e, 64 * e + 64)
                            nc.tensor.matmul(SC[e][:, 0:128], qT[r, u.par(1), 0:128], kT[r, 0:128], start=True, stop=True)
                            nc.tensor.matmul(SC[e][:, 128:384], qT[r, u.par(1), 128:256], kT[r, :], start=True,
                                             stop=True).then_inc(s.score_done, 1)
                    if u.has(2):
                        for e in range(2):
                            pe.wait_ge(s.exp_done, u.count(2, 2, e + 1))
                            if u.was(3):
                                pe.wait_ge(s.p_out, u.count(2, 3, e + 1))
                            for c in range(3):
                                last = nc.tensor.transpose(TR[e][:, c * 128:(c + 1) * 128],
                                                           pb[:, u.par(2), e, c * 128:(c + 1) * 128], ident[:, :])
                            last.then_inc(s.p_turned, 1)
                    if u.has(3):
                        if u.k == 3:
                            pe.wait_ge(s.v_out, u.seqs(1, 3, 1))
                        if u.was(4):
                            pe.wait_ge(s.norm_done, u.count(1, 4, 1))
                        for e in range(2):
                            pe.wait_ge(s.p_out, u.count(2, 3, e + 1))
                            p = pT[:, u.par(3), e, :]
                            o = [(2 * e + t) * (HD + 1) for t in range(2)]
                            nc.tensor.matmul(PV[:, o[0]:o[0] + HD + 1], p[:, 0:128], vv[:, 0, :], start=True, stop=True)
                            nc.tensor.matmul(PV[:, o[1]:o[1] + HD + 1], p[:, 128:256], vv[:, 0, :], start=True, stop=False)
                            last = nc.tensor.matmul(PV[:, o[1]:o[1] + HD + 1], p[:, 256:384], vv[:, 1, :], start=False, stop=True)
                        last.then_inc(s.pv_done, 1)
                    if u.k == 0 and u.has(0):
                        if u.was(5):
                            pe.wait_ge(s.o_out, u.count(1, 5, 1))
                        nc.tensor.matmul(PO[:, SEQ:2 * SEQ], wv[:, :, :].rearrange("p a b -> p (a b)"), hT[:, u.cols(0)], start=True,
                                         stop=True).then_inc(s.vT_done, 1)
                    if u.k == 2 and u.has(2) and not u.tail:
                        pe.wait_ge(s.vT_out, u.seqs(1, 2, 1))
                        if u.was(5):
                            pe.wait_ge(s.o_out, u.count(1, 5, 1))
                        for t in range(2):
                            last = nc.tensor.transpose(PO[:, SEQ + t * 128:SEQ + (t + 1) * 128], vT[:, t * 128:(t + 1) * 128],
                                                       ident[:, :])
                        last.then_inc(s.v_turned, 1)
                    if u.has(4):
                        pe.wait_ge(s.norm_done, u.count(1, 4, 1))
                        if u.was(5):
                            pe.wait_ge(s.o_out, u.count(1, 5, 1))
                        if u.k == 0 and not u.tail:
                            pe.wait_ge(s.vT_out, u.seqs(1, 0, 1))
                        if u.k in (2, 4) and not u.tail:
                            pe.wait_ge(s.v_out, u.seqs(1, u.k, 1))
                        for t in range(2):
                            last = nc.tensor.transpose(PO[:, t * 128:(t + 1) * 128], on[:, u.par(4), t, :, :].rearrange(
                                "p e d -> p (e d)"), ident[:, :])
                        last.then_inc(s.o_turned, 1)
                    if u.has(5):
                        j = u.pair(5)
                        pe.wait_ge(s.o_out, u.count(1, 5, 1))
                        if j == 0 and not (u.lead == 0):
                            pe.wait_ge(s.yo_done, u.seqs(1, 5, 0))
                        last = nc.tensor.matmul(PY[:, 0:SEQ], wout[:, j, :], oT[:, u.par(5), :], start=(j == 0), stop=(j == 7))
                        last.then_inc(s.y_done, 1)

                run(pe, slot)

            @block.scalar
            def _(act):
                act.wait_ge(s.dist_mm, 1)
                nc.scalar.activation(dist[:, :], PY[0:HEADS, 0:SPAN], ACT.Copy).then_inc(s.dist_out, 1)

                def slot(u):
                    if u.has(0):
                        act.wait_ge(s.q_done, u.count(1, 0, 1))
                        if u.was(2):
                            act.wait_ge(s.score_done, u.count(2, 2, 2))
                        nc.scalar.activation(qT[:, u.par(0), :], PQ[:, 0:SEQ], ACT.Copy,
                                             scale=-HD ** -0.5).then_inc(s.q_out, 1)
                        if u.k == 0:
                            if u.was(1):
                                act.wait_ge(s.score_done, u.count(2, 1, 2))
                            nc.scalar.activation(kT[:, :], PQ[:, SEQ:2 * SEQ], ACT.Copy).then_inc(s.k_out, 1)
                    if u.has(1):
                        for e in range(2):
                            for t in range(2):
                                c = slice(0, 128) if t == 0 else slice(128, 384)
                                act.wait_ge(s.max_done, u.count(2, 1, e + 1))
                                last = nc.scalar.activation(pb[:, u.par(1), e, c], pb[:, u.par(1), e, c], ACT.Exp,
                                                            bias=nm[:, u.par(1), e, t:t + 1], scale=-1.0)
                            last.then_inc(s.exp_done, 1)
                    if u.has(2):
                        for e in range(2):
                            act.wait_ge(s.p_turned, u.count(2, 2, e + 1))
                            if u.was(4):
                                act.wait_ge(s.pv_done, u.count(1, 4, 1))
                            nc.scalar.activation(pT[:, u.par(2), e, :], TR[e][:, 0:SPAN], ACT.Copy).then_inc(s.p_out, 1)
                    if u.k == 0 and u.has(0):
                        act.wait_ge(s.vT_done, u.seqs(1, 0, 1))
                        nc.scalar.activation(vT[:, :], PO[:, SEQ:2 * SEQ], ACT.Copy).then_inc(s.vT_out, 1)
                    if u.k == 2 and not u.tail:
                        act.wait_ge(s.v_turned, u.seqs(1, 2, 1))
                        if u.was(3):
                            act.wait_ge(s.pv_done, u.count(1, 3, 1))
                        nc.scalar.activation(vv[:, :, 0:HD], PO[:, SEQ:2 * SEQ].rearrange(
                            "p (t d) -> p t d", t=2)[:, :, 0:HD], ACT.Copy).then_inc(s.v_out, 1)
                    if u.has(4):
                        act.wait_ge(s.o_turned, u.count(1, 4, 1))
                        if u.was(6):
                            act.wait_ge(s.y_done, u.count(1, 6, 1))
                        nc.scalar.activation(oT[:, u.par(4), :], PO[:, 0:SEQ], ACT.Copy).then_inc(s.o_out, 1)

                run(act, slot)

            @block.vector
            def _(dve):
                nc.vector.memset(vv[:, :, HD:HD + 1], 1.0).then_inc(s.ones, 1)
                for n in range(HEADS // 2):
                    dve.wait_ge(s.swapped, n + 1)
                    two = SC[n % 2][:, :].rearrange("p (a b) -> p a b", a=2)
                    nc.vector.tensor_copy(bias[:, 2 * n:2 * n + 2, 0:128], two[:, :, 128:256])
                    nc.vector.tensor_copy(bias[:, 2 * n:2 * n + 2, 128:384], two).then_inc(s.swap_out, 1)
                dve.wait_ge(s.swap_out, HEADS // 2)

                def slot(u):
                    if u.has(1):
                        for e in range(2):
                            h = 2 * u.pair(1) + e
                            dve.wait_ge(s.score_done, u.count(2, 1, e + 1))
                            if u.was(3):
                                dve.wait_ge(s.p_turned, u.count(2, 3, e + 1))
                            nc.vector.memset(tick[:, e:e + 1], 0.0)
                            for t in range(2):
                                c = slice(0, 128) if t == 0 else slice(128, 384)
                                last = nc.vector.tensor_tensor_reduce(
                                    out=pb[:, u.par(1), e, c], in0=SC[e][:, c], in1=bias[:, h, c], scale=1.0,
                                    scalar=3e38, op0=ALU.add, op1=ALU.min, accum_out=nm[:, u.par(1), e, t:t + 1])
                            last.then_inc(s.max_done, 1)
                    if u.has(3):
                        ov = PV[:, 0:4 * (HD + 1)].rearrange("p (e t d) -> p e t d", e=2, t=2)
                        dve.wait_ge(s.pv_done, u.count(1, 3, 1))
                        nc.vector.reciprocal(rs[:, :, :], ov[:, :, :, HD]).then_inc(s.rs_done, 1)
                        dve.wait_ge(s.rs_done, u.count(1, 3, 1))
                        if u.was(5):
                            dve.wait_ge(s.o_turned, u.count(1, 5, 1))
                        nc.vector.tensor_tensor(on[:, u.par(3)].rearrange("p t e d -> p e t d"), ov[:, :, :, 0:HD],
                                                rs[:, :, :].unsqueeze(3).broadcast_to((128, 2, 2, HD)),
                                                ALU.mult).then_inc(s.norm_done, 1)
                    if u.has(5) and u.pair(5) == 7:
                        dve.wait_ge(s.y_done, u.count(1, 5, 1))
                        nc.vector.tensor_scalar(yo[:, :], PY[:, 0:SEQ], bout[:, 0:1], w.gate[:, u.seq(5)], ALU.add,
                                                ALU.mult).then_inc(s.yo_done, 1)
                        dve.wait_ge(s.yo_done, u.seqs(1, 5, 1))
                        nc.vector.tensor_tensor(xT[:, u.cols(5)], xT[:, u.cols(5)], yo[:, :], ALU.add).then_inc(s.x_out, 1)

                run(dve, slot)


def modulation(nc, g, w):
    with ExitStack() as ctx:
        sb = lambda n, s, d=F32: ctx.enter_context(nc.sbuf_tensor("md_" + n, s, d))
        sem = phase_semaphores(nc, ctx, "md_")
        c = sb("c", [NB, 2, D])
        e = sb("e", [NB, 2, D])
        cT = sb("cT", [128, 2, NB])
        wm = sb("wm", [128, 2, 6 * D])
        raw = sb("raw", [128, 2, 6, NB])
        sg = sb("sg", [128, 2, 2, NB])
        pc = ctx.enter_context(nc.psum_tensor("md_pc", [128, 512], F32))
        pm = ctx.enter_context(nc.psum_tensor("md_pm", [128, 512], F32))
        names = "loaded exp_done plus inv silu turned cT_out mod_done raw_out sign mag ready consts bf".split()
        s = type("Sems", (), {n: sem(n) for n in names})
        with nc.Block() as block:

            @block.sync
            def _(sp):
                for l in range(2):
                    sp.dma_start(c[:, l, :], w.c[l]).then_inc(s.loaded, 16)
                    sp.dma_start(wm[:, l, :], w.wmod[l]).then_inc(s.loaded, 16)
                sp.dma_start(g.ident[:, :], w.c_ident).then_inc(s.loaded, 16)
                sp.dma_start(g.band[:, :, :], w.c_band.rearrange("t p k -> p t k")).then_inc(s.loaded, 16)
                sp.dma_start(g.cbase[:, :, :, :], w.c_cbase.rearrange("t p j d -> p t j d")).then_inc(s.loaded, 16)
                sp.dma_start(g.sbase[:, :, :, :], w.c_sbase.rearrange("t p j d -> p t j d")).then_inc(s.loaded, 16)

            @block.scalar
            def _(act):
                act.wait_ge(s.loaded, 128)
                nc.scalar.activation(e[:, :, :], c[:, :, :], ACT.Exp, scale=-1.0).then_inc(s.exp_done, 1)

            @block.vector
            def _(dve):
                nc.vector.memset(g.mhalf[:, :], -0.5)
                nc.vector.memset(g.zero, 0.0)
                nc.vector.memset(g.eps[:, :], EPS).then_inc(s.consts, 1)
                dve.wait_ge(s.loaded, 128)
                nc.vector.tensor_copy(g.identb[:, :], g.ident[:, :])
                nc.vector.tensor_copy(g.maskb[:, :, :, :], g.band[:, :, :].unsqueeze(2).broadcast_to(
                    (128, 2, HEADS // 4, KEYS))).then_inc(s.bf, 1)
                dve.wait_ge(s.exp_done, 1)
                nc.vector.tensor_scalar(e[:, :, :], e[:, :, :], 1.0, None, ALU.add).then_inc(s.plus, 1)
                dve.wait_ge(s.plus, 1)
                nc.vector.reciprocal(e[:, :, :], e[:, :, :]).then_inc(s.inv, 1)
                dve.wait_ge(s.inv, 1)
                nc.vector.tensor_tensor(c[:, :, :], c[:, :, :], e[:, :, :], ALU.mult).then_inc(s.silu, 1)
                dve.wait_ge(s.turned, 1)
                nc.vector.tensor_copy(cT[:, :, :], pc[:, 0:2 * NB].rearrange("p (l b) -> p l b", l=2)).then_inc(s.cT_out, 1)
                dve.wait_ge(s.mod_done, 1)
                nc.vector.tensor_copy(raw[:, :, :, :], pm[:, 0:12 * NB].rearrange(
                    "p (l j b) -> p l j b", l=2, j=6)).then_inc(s.raw_out, 1)
                dve.wait_ge(s.raw_out, 1)
                nc.vector.tensor_copy(g.mod[:, :, 0::3, :], raw[:, :, 0::3, :])
                nc.vector.tensor_scalar(g.mod[:, :, 1::3, :], raw[:, :, 1::3, :], 1.0, None, ALU.add)
                nc.vector.tensor_scalar(sg[:, :, :, :], raw[:, :, 2::3, :], 0.0, 2.0, ALU.is_ge, ALU.mult).then_inc(s.sign, 1)
                nc.vector.tensor_scalar(g.mod[:, :, 2::3, :], raw[:, :, 2::3, :], -1.0, None, ALU.mult).then_inc(s.mag, 1)
                dve.wait_ge(s.mag, 1)
                nc.vector.tensor_tensor(raw[:, :, 2::3, :], raw[:, :, 2::3, :], g.mod[:, :, 2::3, :], ALU.max).then_inc(s.mag, 1)
                dve.wait_ge(s.mag, 2)
                nc.vector.tensor_scalar(raw[:, :, 2::3, :], raw[:, :, 2::3, :], 0.25, None, ALU.max).then_inc(s.mag, 1)
                dve.wait_ge(s.sign, 1)
                nc.vector.tensor_scalar(sg[:, :, :, :], sg[:, :, :, :], -1.0, None, ALU.add).then_inc(s.sign, 1)
                dve.wait_ge(s.sign, 2)
                dve.wait_ge(s.mag, 3)
                nc.vector.tensor_tensor(g.mod[:, :, 2::3, :], raw[:, :, 2::3, :], sg[:, :, :, :], ALU.mult).then_inc(s.ready, 1)

            @block.tensor
            def _(pe):
                pe.wait_ge(s.silu, 1)
                for l in range(2):
                    last = nc.tensor.transpose(pc[:, l * NB:(l + 1) * NB], c[:, l, :], g.ident[0:NB, 0:NB])
                last.then_inc(s.turned, 1)
                pe.wait_ge(s.cT_out, 1)
                for l in range(2):
                    for j in range(6):
                        at = (l * 6 + j) * NB
                        last = nc.tensor.matmul(pm[:, at:at + NB], wm[:, l, j * D:(j + 1) * D], cT[:, l, :], start=True, stop=True)
                last.then_inc(s.mod_done, 1)


def build(nc, a, out):
    with ExitStack() as ctx:
        sb = lambda n, s, d=F32: ctx.enter_context(nc.sbuf_tensor(n, s, d))
        g = type("Shared", (), dict(
            xT=sb("xT", [128, TOK]), yT=sb("yT", [128, TOK]),
            ident=sb("ident", [128, 128]), identb=sb("identb", [128, 128], BF16),
            band=sb("band", [128, 2, KEYS]), maskb=sb("maskb", [128, 2, HEADS // 4, KEYS], BF16),
            cbase=sb("cbase", [128, 2, 2, HD]), sbase=sb("sbase", [128, 2, 2, HD]),
            zero=sb("zero", [128, 1])[:, :], mhalf=sb("mhalf", [128, HEADS]), eps=sb("eps", [128, HEADS]), mod=sb("mod", [128, 2, 6, NB])))
        sems = lambda p, names: type("Sems", (), {n: nc.alloc_semaphore(p + n) for n in names})
        g.wa_sems = sems("wa_", WA_SEMS)
        g.gm_sems = sems("gm_", GM_SEMS)
        pick = lambda prefix, **more: type("Weights", (), {
            **{k[len(prefix):]: v for k, v in a.items() if k.startswith(prefix)},
            **{k: v for k, v in a.items() if k.startswith("c_")}, **more})
        modulation(nc, g, pick("none", c=[a["L0_c"], a["L1_c"]], wmod=[a["L0_wmod"], a["L1_wmod"]]))
        mod = lambda l, j: g.mod[:, l, j, :]
        layernorm_modulate(nc, "n0_", g, g.yT, mod(0, 1), mod(0, 0), from_dram=a["L0_attn_x"])
        w = pick("L0_attn_")
        with nc.sbuf_tensor("aT", [128, TOK], F32) as g.aT:
            linear_attention(nc, g, w)
            plain_mlp(nc, "m0_", g, g.aT, w.W1, w.b1, w.W2, w.b2, mod(0, 2), skip=g.yT)
        layernorm_modulate(nc, "n1_", g, g.yT, mod(0, 4), mod(0, 3))
        w = pick("L0_ffn_")
        with ExitStack() as loop_ctx:
            g.lw = layer_weights(nc, loop_ctx)
            first_attention_weights(nc, g, w)
            with nc.Fori(0, DEPTH) as layer:
                window_attention(nc, layer, g, w)
                gated_mlp(nc, layer, g, w)
        gated_residual(nc, g, mod(0, 5))
        layernorm_modulate(nc, "n2_", g, g.yT, mod(1, 1), mod(1, 0))
        w = pick("L1_attn_", gate=mod(1, 2), scratch=nc.dram_tensor("bias_by_distance", (HEADS, 384), F32, kind="Internal").ap())
        multiquery_attention(nc, g, w)
        layernorm_modulate(nc, "n3_", g, g.yT, mod(1, 4), mod(1, 3))
        w = pick("L1_ffn_")
        plain_mlp(nc, "m1_", g, g.yT, w.w1, w.b1, w.w2, w.b2, mod(1, 5), out_d=out)


def gated_residual(nc, g, gate):
    done = nc.alloc_semaphore("gr_done")
    with nc.Block() as block:

        @block.vector
        def _(dve):
            with dve.Fori(0, NB) as b:
                cols = bass.ds(b * SEQ, SEQ)
                nc.vector.scalar_tensor_tensor(out=g.xT[:, cols], in0=g.yT[:, cols], scalar=gate[:, bass.ds(b, 1)],
                                               in1=g.xT[:, cols], op0=ALU.mult, op1=ALU.add).then_inc(done, 1)
            dve.wait_ge(done, NB)


def shape_constants():
    import numpy as np
    f = np.float32
    c = {"c_ident": np.eye(128, dtype=f)}
    r, k = np.arange(BLK)[:, None], np.arange(KEYS)[None, :]
    band = np.where((k >= r) & (k <= r + WIN), 0.0, NEG)
    first = np.where(k >= WIN, band, NEG)
    c["c_band"] = np.stack([np.concatenate([first, band]), np.concatenate([band, band])]).astype(f)
    half = np.arange(0, HD, 2, dtype=f)
    inv_freq = f(1) / np.power(f(10000), half / f(HD))
    t = np.arange(SEQ, dtype=f)
    freqs = np.tile(t[:, None] * inv_freq[None, :], (1, 2)).astype(f)
    base_scale = (half + f(0.4 * HD)) / f(1.4 * HD)
    power = (t - f(SEQ // 2)) / f(WIN // 2)
    scale = np.tile(base_scale[None, :] ** power[:, None], (1, 2)).astype(f)
    cos, sin = np.cos(freqs), np.sin(freqs) * np.where(np.arange(HD) < HD // 2, f(-1), f(1))
    c["c_cbase"] = np.stack([cos * scale * 8, cos / scale], 1).reshape(2, 128, 2, HD).astype(f)
    c["c_sbase"] = np.stack([sin * scale * 8, sin / scale], 1).reshape(2, 128, 2, HD).astype(f)
    p = np.arange(128)
    sel = (p[:, None] // LIN_HD == np.arange(HEADS)[None, :]).astype(f)
    c["c_hsel"], c["c_hselT"] = sel, np.ascontiguousarray(sel.T)
    c["c_hprobe"] = (sel / (SEQ * np.sqrt(LIN_HD))).astype(f)
    c["c_hmask"] = (p[:, None] // LIN_HD == p[None, :] // LIN_HD).astype(f)
    n = SEQ - 1 - np.arange(384)
    exact = BUCKETS // 2
    safe = np.maximum(n, 1).astype(f)
    large = exact + (np.log(safe / exact) / np.log(128 / exact) * (BUCKETS - exact)).astype(np.int32)
    bucket = np.where(n < exact, np.maximum(n, 0), np.minimum(large, BUCKETS - 1))
    hot = (np.arange(BUCKETS)[:, None] == bucket[None, :]) & (n >= 0)[None, :]
    c["c_hot"] = (hot * HD ** 0.5).astype(f)
    c["c_off"] = np.where(n < 0, NEG, 0.0)[None, :].astype(f)
    c["c_ones"] = np.ones((1, HEADS), f)
    c["c_swap"] = np.ascontiguousarray(-np.eye(128, dtype=f)[::-1])
    return c


def kernel(**inputs):
    import numpy as np
    import concourse.bacc as bacc
    from concourse.bass_utils import run_bass_kernel_spmd

    nc = bacc.Bacc("TRN2", target_bir_lowering=False, num_devices=1)
    arrays = {k: np.ascontiguousarray(v) for k, v in inputs.items()}
    arrays.update(shape_constants())
    a = {k: nc.dram_tensor(k, v.shape, mybir.dt.from_np(v.dtype), kind="ExternalInput").ap() for k, v in arrays.items()}
    out = nc.dram_tensor("out", (NB, SEQ, D), F32, kind="ExternalOutput").ap()
    build(nc, a, out)
    return run_bass_kernel_spmd(nc, [arrays], core_ids=[0]).results[0]["out"]
```
